# Optimizing a Trainium2 kernel written in Bass

```python
import numpy as np
import jax
import jax.numpy as jnp

def _softmax(x, axis=-1):
    return jax.nn.softmax(x, axis=axis)

def _gelu(x):
    return jax.nn.gelu(x, approximate=True)

def _silu(x):
    return jax.nn.silu(x)

def _sigmoid(x):
    return jax.nn.sigmoid(x)

def _layernorm(x, axis=-1, eps=1e-05):
    m = jnp.mean(x, axis=axis, keepdims=True)
    v = jnp.var(x, axis=axis, keepdims=True)
    return (x - m) / jnp.sqrt(v + eps)

def _scatter_add(tgt, idx, src, axis=0):
    return tgt.at[idx].add(src)

def _segment_sum(src, seg, n):
    return jax.ops.segment_sum(src, seg, n)
kernel_name = 'mk_gps_d1_gnn_r16_5ec06f'

def setup_inputs(seed: int=0):
    np.random.seed(seed)
    _w = jnp.asarray

    def _rec_inputs():
        import jax
        import jax.numpy as jnp
        _gk = jax.random.key(seed)
        x = -0.0001126 + 1 * jax.random.normal(jax.random.fold_in(_gk, 1), (625, 768), jnp.float32)
        _s = jax.random.randint(jax.random.fold_in(_gk, 2), (10000,), 0, 625, jnp.int32)
        _d = jax.random.randint(jax.random.fold_in(_gk, 3), (10000,), 0, 625, jnp.int32)
        _loop = jnp.arange(625, dtype=jnp.int32)
        src = jnp.concatenate([_s, _d, _loop])
        dst = jnp.concatenate([_d, _s, _loop])
        _o = jnp.argsort(dst, stable=True)
        src = src[_o]
        dst = dst[_o]
        edge_weight1 = -0.00472126 + 0.997171 * jax.random.normal(jax.random.fold_in(_gk, 13), (20625, 1), jnp.float32)
        return (x, src, dst, edge_weight1)
    x, src, dst, edge_weight1 = _rec_inputs()

    def _L0_gnn_setup():
        import jax, jax.numpy as jnp
        import numpy as np
        N, E, D, H, C = (625, 6250, 768, 4, 192)
        NEG_SLOPE = 0.2

        def gat_conv(x, src, dst, W, a_src, a_dst, b):
            h = (x @ W).reshape(N, H, C)
            as_n = (h * a_src).sum(-1)
            ad_n = (h * a_dst).sum(-1)
            e = jax.nn.leaky_relu(as_n[src] + ad_n[dst], NEG_SLOPE)
            m = jax.ops.segment_max(e, dst, num_segments=N)
            p = jnp.exp(e - m[dst])
            s = jax.ops.segment_sum(p, dst, num_segments=N)
            alpha = p / (s[dst] + 1e-16)
            out = jax.ops.segment_sum(alpha[:, :, None] * h[src], dst, num_segments=N)
            return out.reshape(N, H * C) + b
        key = jax.random.key(seed)
        ks = jax.random.split(key, 16)
        w = lambda k, shape: jax.random.normal(k, shape, dtype=jnp.float32) * 0.02
        inp = {}
        inp['x'] = jax.random.normal(ks[0], (N, D), dtype=jnp.float32)
        inp['edge_index'] = jax.random.randint(ks[1], (2, E), 0, N, dtype=jnp.int32)
        inp['batch'] = jnp.zeros((N,), dtype=jnp.int32)
        inp['edge_attr'] = jax.random.normal(ks[2], (E, 1), dtype=jnp.float32)
        inp['W_ah'] = w(ks[3], (D, D))
        inp['b_ah'] = jnp.zeros((D,), jnp.float32)
        for i in range(3):
            inp[f'W{i}'] = w(ks[4 + 3 * i], (D, H * C))
            inp[f'a_src{i}'] = w(ks[5 + 3 * i], (H, C))
            inp[f'a_dst{i}'] = w(ks[6 + 3 * i], (H, C))
            inp[f'b{i}'] = jnp.zeros((H * C,), jnp.float32)
        inp['W_out'] = w(ks[13], (3 * D, D))
        inp['b_out'] = jnp.zeros((D,), jnp.float32)
        return inp
    _L0_gnn_all = _L0_gnn_setup()
    _L0_gnn_in = {k: v for k, v in _L0_gnn_all.items() if k in ('W_ah', 'b_ah', 'W0', 'a_src0', 'a_dst0', 'b0', 'W1', 'a_src1', 'a_dst1', 'b1', 'W2', 'a_src2', 'a_dst2', 'b2', 'W_out', 'b_out')}
    del _L0_gnn_all

    def _L0_mix_setup():
        import jax, jax.numpy as jnp
        import numpy as np
        NUM_HEADS = 12

        def _l2_norm(t):
            return t / jnp.linalg.norm(t, axis=-2, keepdims=True)

        def _reference_tuple_inner(x, w_qkv, w_proj, b_proj):
            B, N, C = x.shape
            H = NUM_HEADS
            D = C // H
            qkv = (x @ w_qkv).reshape(B, N, 3, H, D).transpose(2, 0, 3, 1, 4)
            q, k, v = (qkv[0], qkv[1], qkv[2])
            q = _l2_norm(q)
            kT = _l2_norm(k).transpose(0, 1, 3, 2)
            sum_k = kT.sum(axis=-1)
            D_inv = 1.0 / (N + jnp.einsum('bhnd,bhd->bhd', q, sum_k))
            attn_matrix = jnp.einsum('bhnd,bhdn->bhdn', q, kT) * D_inv[..., None]
            matrix = jnp.einsum('bhnd,bhdn->bdhn', v, kT)
            y = jnp.einsum('bdhn,bhdn->bhnd', matrix, attn_matrix)
            y = y.transpose(0, 2, 1, 3).reshape(B, N, C)
            out = y @ w_proj + b_proj
            return (out, attn_matrix)
        key = jax.random.key(seed)
        k1, k2, k3 = jax.random.split(key, 3)
        B, N, C = (64, 1024, 768)
        x = jax.random.normal(k1, (B, N, C), dtype=jnp.float32)
        w_qkv = jax.random.normal(k2, (C, 3 * C), dtype=jnp.float32) * 0.02
        w_proj = jax.random.normal(k3, (C, C), dtype=jnp.float32) * 0.02
        b_proj = jnp.zeros((C,), dtype=jnp.float32)
        return {'x': x, 'w_qkv': w_qkv, 'w_proj': w_proj, 'b_proj': b_proj}
    _L0_mix_all = _L0_mix_setup()
    _L0_mix_in = {k: v for k, v in _L0_mix_all.items() if k in ('w_qkv', 'w_proj', 'b_proj')}
    del _L0_mix_all

    def _L0_ffn_setup():
        import jax, jax.numpy as jnp
        import numpy as np
        N_HEAD = 8 * 0 + 12
        TOP_K = 2
        GELU_C = 0.7978845608028654

        def _gelu(x):
            return 0.5 * x * (1.0 + jnp.tanh(GELU_C * (x + 0.044715 * x * x * x)))

        def _layernorm_global(x, w, b, eps=1e-12):
            m = jnp.mean(x)
            v = jnp.var(x, ddof=1)
            return (x - m) / jnp.sqrt(v + eps) * w + b

        def _attn(x, W1_w, W1_b, W2_w, W2_b):
            B, N, D = x.shape
            h = N_HEAD
            dh = D // h
            qkv = x @ W1_w + W1_b
            Q, K, V = jnp.split(qkv, 3, axis=-1)
            q = Q.reshape(B, N, h, dh).transpose(0, 2, 3, 1)
            k = K.reshape(B, N, h, dh).transpose(0, 2, 1, 3)
            v = V.reshape(B, N, h, dh).transpose(0, 2, 3, 1)
            w = jax.nn.softmax(q @ k / jnp.sqrt(jnp.asarray(N, x.dtype)), axis=-1)
            out = (w @ v).reshape(B, N, h * dh)
            return out @ W2_w + W2_b

        def _moe(x, r_w, r_b, fc_w, fc_b, proj_w, proj_b):
            B, N, D = x.shape
            scores = x @ r_w + r_b
            gate = jax.nn.softmax(jnp.mean(scores, axis=1), axis=-1)
            vals, idx = jax.lax.top_k(gate, TOP_K)
            hmid = _gelu(jnp.einsum('bnd,edf->benf', x, fc_w) + fc_b[None, :, None, :])
            outs = jnp.einsum('benf,efd->bend', hmid, proj_w) + proj_b[None, :, None, :]
            k_outs = jnp.take_along_axis(outs, idx[:, :, None, None], axis=1)
            return jnp.sum(vals[:, :, None, None] * k_outs, axis=1)
        key = jax.random.key(seed)
        ks = jax.random.split(key, 16)
        B, N, D, E = (2, 128, 768, 8)
        H = 4 * D
        s = 0.02
        return {'x': jax.random.normal(ks[0], (B, N, D), jnp.float32), 'W1_w': jax.random.normal(ks[1], (D, 3 * D), jnp.float32) * s, 'W1_b': jnp.zeros((3 * D,), jnp.float32), 'W2_w': jax.random.normal(ks[2], (D, D), jnp.float32) * s, 'W2_b': jnp.zeros((D,), jnp.float32), 'r_w': jax.random.normal(ks[3], (D, E), jnp.float32) * s, 'r_b': jnp.zeros((E,), jnp.float32), 'fc_w': jax.random.normal(ks[4], (E, D, H), jnp.float32) * s, 'fc_b': jnp.zeros((E, H), jnp.float32), 'proj_w': jax.random.normal(ks[5], (E, H, D), jnp.float32) * s, 'proj_b': jnp.zeros((E, D), jnp.float32), 'ln1_w': jnp.ones((D,), jnp.float32), 'ln1_b': jnp.zeros((D,), jnp.float32), 'ln2_w': jnp.ones((D,), jnp.float32), 'ln2_b': jnp.zeros((D,), jnp.float32)}
    _L0_ffn_all = _L0_ffn_setup()
    _L0_ffn_in = {k: v for k, v in _L0_ffn_all.items() if k in ('W1_w', 'W1_b', 'W2_w', 'W2_b', 'r_w', 'r_b', 'fc_w', 'fc_b', 'proj_w', 'proj_b', 'ln1_w', 'ln1_b', 'ln2_w', 'ln2_b')}
    del _L0_ffn_all
    return {'x': x, 'src': src, 'dst': dst, 'edge_weight1': edge_weight1, 'L0_gnn_W_ah': _L0_gnn_in['W_ah'], 'L0_gnn_b_ah': _L0_gnn_in['b_ah'], 'L0_gnn_W0': _L0_gnn_in['W0'], 'L0_gnn_a_src0': _L0_gnn_in['a_src0'], 'L0_gnn_a_dst0': _L0_gnn_in['a_dst0'], 'L0_gnn_b0': _L0_gnn_in['b0'], 'L0_gnn_W1': _L0_gnn_in['W1'], 'L0_gnn_a_src1': _L0_gnn_in['a_src1'], 'L0_gnn_a_dst1': _L0_gnn_in['a_dst1'], 'L0_gnn_b1': _L0_gnn_in['b1'], 'L0_gnn_W2': _L0_gnn_in['W2'], 'L0_gnn_a_src2': _L0_gnn_in['a_src2'], 'L0_gnn_a_dst2': _L0_gnn_in['a_dst2'], 'L0_gnn_b2': _L0_gnn_in['b2'], 'L0_gnn_W_out': _L0_gnn_in['W_out'], 'L0_gnn_b_out': _L0_gnn_in['b_out'], 'L0_mix_w_qkv': _L0_mix_in['w_qkv'], 'L0_mix_w_proj': _L0_mix_in['w_proj'], 'L0_mix_b_proj': _L0_mix_in['b_proj'], 'L0_ffn_W1_w': _L0_ffn_in['W1_w'], 'L0_ffn_W1_b': _L0_ffn_in['W1_b'], 'L0_ffn_W2_w': _L0_ffn_in['W2_w'], 'L0_ffn_W2_b': _L0_ffn_in['W2_b'], 'L0_ffn_r_w': _L0_ffn_in['r_w'], 'L0_ffn_r_b': _L0_ffn_in['r_b'], 'L0_ffn_fc_w': _L0_ffn_in['fc_w'], 'L0_ffn_fc_b': _L0_ffn_in['fc_b'], 'L0_ffn_proj_w': _L0_ffn_in['proj_w'], 'L0_ffn_proj_b': _L0_ffn_in['proj_b'], 'L0_ffn_ln1_w': _L0_ffn_in['ln1_w'], 'L0_ffn_ln1_b': _L0_ffn_in['ln1_b'], 'L0_ffn_ln2_w': _L0_ffn_in['ln2_w'], 'L0_ffn_ln2_b': _L0_ffn_in['ln2_b']}

def reference(x, src, dst, edge_weight1, L0_gnn_W_ah, L0_gnn_b_ah, L0_gnn_W0, L0_gnn_a_src0, L0_gnn_a_dst0, L0_gnn_b0, L0_gnn_W1, L0_gnn_a_src1, L0_gnn_a_dst1, L0_gnn_b1, L0_gnn_W2, L0_gnn_a_src2, L0_gnn_a_dst2, L0_gnn_b2, L0_gnn_W_out, L0_gnn_b_out, L0_mix_w_qkv, L0_mix_w_proj, L0_mix_b_proj, L0_ffn_W1_w, L0_ffn_W1_b, L0_ffn_W2_w, L0_ffn_W2_b, L0_ffn_r_w, L0_ffn_r_b, L0_ffn_fc_w, L0_ffn_fc_b, L0_ffn_proj_w, L0_ffn_proj_b, L0_ffn_ln1_w, L0_ffn_ln1_b, L0_ffn_ln2_w, L0_ffn_ln2_b):
    import jax
    import jax.numpy as jnp

    def _L0_gnn_ref(x, edge_index, batch, edge_attr, W_ah, b_ah, W0, a_src0, a_dst0, b0, W1, a_src1, a_dst1, b1, W2, a_src2, a_dst2, b2, W_out, b_out):
        import jax, jax.numpy as jnp
        import numpy as np
        N, E, D, H, C = (625, 6250, 768, 4, 192)
        NEG_SLOPE = 0.2

        def gat_conv(x, src, dst, W, a_src, a_dst, b):
            h = (x @ W).reshape(N, H, C)
            as_n = (h * a_src).sum(-1)
            ad_n = (h * a_dst).sum(-1)
            e = jax.nn.leaky_relu(as_n[src] + ad_n[dst], NEG_SLOPE)
            m = jax.ops.segment_max(e, dst, num_segments=N)
            p = jnp.exp(e - m[dst])
            s = jax.ops.segment_sum(p, dst, num_segments=N)
            alpha = p / (s[dst] + 1e-16)
            out = jax.ops.segment_sum(alpha[:, :, None] * h[src], dst, num_segments=N)
            return out.reshape(N, H * C) + b
        loops = jnp.arange(N, dtype=edge_index.dtype)
        src = jnp.concatenate([edge_index[0], loops])
        dst = jnp.concatenate([edge_index[1], loops])
        x1 = jax.nn.relu(x @ W_ah + b_ah)
        xs = [jax.nn.relu(gat_conv(x1, src, dst, W, a_s, a_d, b)) for W, a_s, a_d, b in ((W0, a_src0, a_dst0, b0), (W1, a_src1, a_dst1, b1), (W2, a_src2, a_dst2, b2))]
        node_emb = jnp.concatenate(xs, axis=1)
        return jax.nn.relu(node_emb @ W_out + b_out)

    def _L0_mix_ref(x, w_qkv, w_proj, b_proj):
        import jax, jax.numpy as jnp
        import numpy as np
        NUM_HEADS = 12

        def _l2_norm(t):
            return t / jnp.linalg.norm(t, axis=-2, keepdims=True)

        def _reference_tuple_inner(x, w_qkv, w_proj, b_proj):
            B, N, C = x.shape
            H = NUM_HEADS
            D = C // H
            qkv = (x @ w_qkv).reshape(B, N, 3, H, D).transpose(2, 0, 3, 1, 4)
            q, k, v = (qkv[0], qkv[1], qkv[2])
            q = _l2_norm(q)
            kT = _l2_norm(k).transpose(0, 1, 3, 2)
            sum_k = kT.sum(axis=-1)
            D_inv = 1.0 / (N + jnp.einsum('bhnd,bhd->bhd', q, sum_k))
            attn_matrix = jnp.einsum('bhnd,bhdn->bhdn', q, kT) * D_inv[..., None]
            matrix = jnp.einsum('bhnd,bhdn->bdhn', v, kT)
            y = jnp.einsum('bdhn,bhdn->bhnd', matrix, attn_matrix)
            y = y.transpose(0, 2, 1, 3).reshape(B, N, C)
            out = y @ w_proj + b_proj
            return (out, attn_matrix)
        return _reference_tuple_inner(x, w_qkv, w_proj, b_proj)[0]

    def _L0_ffn_ref(x, W1_w, W1_b, W2_w, W2_b, r_w, r_b, fc_w, fc_b, proj_w, proj_b, ln1_w, ln1_b, ln2_w, ln2_b):
        import jax, jax.numpy as jnp
        import numpy as np
        N_HEAD = 8 * 0 + 12
        TOP_K = 2
        GELU_C = 0.7978845608028654

        def _gelu(x):
            return 0.5 * x * (1.0 + jnp.tanh(GELU_C * (x + 0.044715 * x * x * x)))

        def _layernorm_global(x, w, b, eps=1e-12):
            m = jnp.mean(x)
            v = jnp.var(x, ddof=1)
            return (x - m) / jnp.sqrt(v + eps) * w + b

        def _attn(x, W1_w, W1_b, W2_w, W2_b):
            B, N, D = x.shape
            h = N_HEAD
            dh = D // h
            qkv = x @ W1_w + W1_b
            Q, K, V = jnp.split(qkv, 3, axis=-1)
            q = Q.reshape(B, N, h, dh).transpose(0, 2, 3, 1)
            k = K.reshape(B, N, h, dh).transpose(0, 2, 1, 3)
            v = V.reshape(B, N, h, dh).transpose(0, 2, 3, 1)
            w = jax.nn.softmax(q @ k / jnp.sqrt(jnp.asarray(N, x.dtype)), axis=-1)
            out = (w @ v).reshape(B, N, h * dh)
            return out @ W2_w + W2_b

        def _moe(x, r_w, r_b, fc_w, fc_b, proj_w, proj_b):
            B, N, D = x.shape
            scores = x @ r_w + r_b
            gate = jax.nn.softmax(jnp.mean(scores, axis=1), axis=-1)
            vals, idx = jax.lax.top_k(gate, TOP_K)
            hmid = _gelu(jnp.einsum('bnd,edf->benf', x, fc_w) + fc_b[None, :, None, :])
            outs = jnp.einsum('benf,efd->bend', hmid, proj_w) + proj_b[None, :, None, :]
            k_outs = jnp.take_along_axis(outs, idx[:, :, None, None], axis=1)
            return jnp.sum(vals[:, :, None, None] * k_outs, axis=1)
        a = _attn(x, W1_w, W1_b, W2_w, W2_b)
        x = _layernorm_global(a + x, ln1_w, ln1_b)
        m = _moe(x, r_w, r_b, fc_w, fc_b, proj_w, proj_b)
        x = _layernorm_global(m + x, ln2_w, ln2_b)
        return x
    edge_index = jnp.stack([src, dst])
    batch0 = jnp.zeros((625,), jnp.int32)
    xn = _layernorm(x, axis=-1)
    x = x + _L0_gnn_ref(xn, edge_index, batch0, edge_weight1, L0_gnn_W_ah, L0_gnn_b_ah, L0_gnn_W0, L0_gnn_a_src0, L0_gnn_a_dst0, L0_gnn_b0, L0_gnn_W1, L0_gnn_a_src1, L0_gnn_a_dst1, L0_gnn_b1, L0_gnn_W2, L0_gnn_a_src2, L0_gnn_a_dst2, L0_gnn_b2, L0_gnn_W_out, L0_gnn_b_out) + _L0_mix_ref(xn[None], L0_mix_w_qkv, L0_mix_w_proj, L0_mix_b_proj)[0]
    x = x + _L0_ffn_ref(_layernorm(x, axis=-1)[None], L0_ffn_W1_w, L0_ffn_W1_b, L0_ffn_W2_w, L0_ffn_W2_b, L0_ffn_r_w, L0_ffn_r_b, L0_ffn_fc_w, L0_ffn_fc_b, L0_ffn_proj_w, L0_ffn_proj_b, L0_ffn_ln1_w, L0_ffn_ln1_b, L0_ffn_ln2_w, L0_ffn_ln2_b)[0]
    return x

_drawn_inputs = setup_inputs


def setup_inputs(seed=0):
    import zlib

    import numpy as np

    out = dict(_drawn_inputs(seed))
    spreads = {'L0_gnn_b_ah': (0.0, 0.68),
     'L0_gnn_b0': (0.0, 0.32),
     'L0_gnn_b1': (0.0, 0.342),
     'L0_gnn_b2': (0.0, 0.339),
     'L0_gnn_b_out': (0.0, 0.1),
     'L0_mix_b_proj': (0.0, 0.1),
     'L0_ffn_W1_b': (0.0, 0.8),
     'L0_ffn_W2_b': (0.0, 0.1),
     'L0_ffn_r_b': (0.0, 0.8),
     'L0_ffn_fc_b': (0.0, 0.8),
     'L0_ffn_proj_b': (0.0, 0.776),
     'L0_ffn_ln1_w': (1.0, 0.2),
     'L0_ffn_ln1_b': (0.0, 0.1),
     'L0_ffn_ln2_w': (1.0, 0.2),
     'L0_ffn_ln2_b': (0.0, 0.1)}
    factors = {'L0_gnn_W_ah': 3.935,
     'L0_gnn_a_src0': 8.0,
     'L0_gnn_a_dst0': 29.448,
     'L0_gnn_a_src1': 8.0,
     'L0_gnn_a_dst1': 30.261,
     'L0_gnn_a_src2': 8.0,
     'L0_gnn_a_dst2': 36.065,
     'L0_mix_w_qkv': 64.0,
     'L0_mix_w_proj': 64.0}
    for name, (base, spread) in spreads.items():
        noise = np.random.default_rng([zlib.crc32(name.encode()), seed]).standard_normal(out[name].shape)
        drawn = base * np.exp(spread * noise) if base else spread * noise
        out[name] = jnp.asarray(drawn.astype(out[name].dtype))
    for name, factor in factors.items():
        out[name] = (out[name] * factor).astype(out[name].dtype)
    return out
```

```python
from contextlib import ExitStack

import concourse.bass as bass
from concourse import mybir

ALU = mybir.AluOpType
ACT = mybir.ActivationFunctionType
F32, F32R, F16, BF16, I32, U32 = (mybir.dt.float32, mybir.dt.float32r, mybir.dt.float16, mybir.dt.bfloat16,
                                  mybir.dt.int32, mybir.dt.uint32)
AX_X = mybir.AxisListType.X

N, D, E = 625, 768, 20625
NT, TT = 5, 125
TP, HT = 626, 314
KC = D // 128
GH, GC = 4, 192
L = 3
NHD = L * GH
MH = 12
EP = (E + 255) // 256
HID, NE = 4 * D, 8
QC = HID // 2 // 128
RING, RAW = 6, 3
NEG = -1.0e30
LN_EPS, GLN_EPS = 1e-5, 1e-12
GELU_C, GELU_A = 0.7978845608028654, 0.044715



def plan():
    steps, slot, uses, pair_of = [], 0, [0, 0, 0], {}
    turn = [0]

    def job(key, ring):
        p = turn[0] % ring
        turn[0] += 1
        pair_of[key] = (p, uses[p])
        uses[p] += 1

    def step(kind, name, args, ring):
        nonlocal slot
        jobs = [(name, *args)] if kind == "F" else [(name, *args, t) for t in range(NT)]
        n = 1 if kind == "F" else 3
        for k in jobs:
            job(k, ring)
        steps.append((kind, name, args, slot, jobs))
        slot += n

    def other(name, *args, ring):
        job((name, *args), ring)
        steps.append(("X", name, args, slot, [(name, *args)]))

    def mark(name, *args):
        steps.append(("M", name, args, slot, []))

    other("edgesT", ring=3)
    other("bounds", ring=3)
    for j in range(NT):
        other("count", j, ring=3)
        other("countT", j, ring=3)
    other("biasT", ring=3)
    for c in range(KC):
        other("xnT", c, ring=3)
    for fo in range(KC):
        step("F", "ah", (fo,), 3)
    for layer in range(L):
        for g in range(2):
            step("T", "h", (layer, g), 3)
    other("asT", ring=3)
    turn[0] = 0

    def ft(f):
        for part in range(3):
            step("F", "mix", (f, part), 2)

    def two_heads(layer, pr, between, after):
        mark("agg", layer * GH + 2 * pr)
        between()
        mark("agg", layer * GH + 2 * pr + 1)
        after()
        for c in range(3):
            other("gT", layer, pr, c, ring=2)

    wo = lambda layer, g: (lambda: step("T", "wo", (layer, g), 2))
    ft(0)
    other("mzT", 0, ring=2)
    ft(1)
    two_heads(0, 0, lambda: ft(2), lambda: None)
    two_heads(0, 1, lambda: (ft(3), other("mzT", 1, ring=2)), lambda: None)
    two_heads(1, 0, wo(0, 0), wo(0, 1))
    two_heads(1, 1, lambda: (ft(4), other("mzT", 2, ring=2)), lambda: None)
    two_heads(2, 0, wo(1, 0), wo(1, 1))
    two_heads(2, 1, lambda: ft(5), lambda: None)
    wo(2, 0)()
    wo(2, 1)()
    for g in range(2):
        step("T", "proj", (g,), 2)
    turn[0] = 0
    for c in range(KC):
        other("xT", c, ring=3)
    for u in range(2):
        for g in range(2):
            step("T", "qk", (u, g), 3)
    other("scores", ring=3)
    for fo in range(KC):
        step("F", "v", (fo,), 3)
    other("wT", ring=3)
    for hp in range(MH // 2):
        other("av", hp, ring=3)
    for c in range(KC):
        other("mT", c, ring=3)
    for fo in range(KC):
        step("F", "w2", (fo,), 3)
    other("expert_biasT", ring=3)
    return steps, slot, pair_of, uses


STEPS, MOE0, PAIR_OF, MOE_USES = plan()
assert MOE0 % RING == 0
AGG_AT = [i for i, s in enumerate(STEPS) if s[1] == "agg"]
FIRST_MIX = next(i for i, s in enumerate(STEPS) if s[1] == "mzT")
THIRD_PAIR = [k for s in STEPS[:FIRST_MIX] for k in s[4] if PAIR_OF[k][0] == 2][-1]
MAX_AT = {0: (4, 5), 1: (6,), 2: (7,), 4: (8, 9), 5: (10,), 6: (11,)}
AS_ROW_AT = {0: (6, 7), 2: (8, 9), 4: (10, 11)}
MIX_AT = {0: 2, 2: 3, 6: 4, 10: 5}
MZ_AT = {2: 1, 6: 2}


def softmax_schedule():
    n = [0] * len(STEPS)
    for j in range(NHD):
        lo = AGG_AT[j - 1] + 1 if j else FIRST_MIX + 1
        between = list(range(lo, AGG_AT[j]))
        early = (4 if j else 5) if between else 0
        for i in range(early):
            n[between[i * len(between) // early]] += 1
        n[AGG_AT[j]] = (6 if j == 0 else 5) - early
    return n


SOFT = softmax_schedule()


def gnn_block(nc, a, out):
    h_scr = nc.dram_tensor("h_scr", (NHD, N, GC + 1), F32).ap()
    as_scr = nc.dram_tensor("as_scr", (NHD, N), F32).ap()
    mz_scr = nc.dram_tensor("mz_scr", (L, 2 * GH, N), F32).ap()
    y_scr = nc.dram_tensor("y_scr", (2, D, TP), F32).ap()
    o_scr = nc.dram_tensor("o_scr", (D, N), F32).ap()

    base = (nc.sbuf_base + 31) // 32 * 32
    top = nc.sbuf_usable_end

    def at(name, shape, dt, off):
        size = 2 if dt in (F16, BF16) else 4
        n = size
        for s in shape[1:]:
            n *= s
        assert off % 32 == 0 and base + off + n <= top, (name, off, n)
        return nc.alloc_sbuf_tensor_at(name, shape, dt, offset=base + off)

    SLOT = D * 4
    FM = (KC * TP * 4 + 31) // 32 * 32
    w_hi = at("w_hi", [128, RING, D], F32R, 0)
    w_lo = at("w_lo", [128, RING, D], F32R, RING * SLOT)
    w_raw = at("w_raw", [128, RAW, D], F32, 2 * RING * SLOT)
    F0 = (2 * RING + RAW) * SLOT
    F1 = F0 + 2 * FM
    R = F1 + 2 * FM
    f0_hi = at("f0_hi", [128, KC, TP], F32R, F0)
    f0_lo = at("f0_lo", [128, KC, TP], F32R, F0 + FM)
    f1_hi = at("f1_hi", [128, KC, TP], F32R, F1)
    f1_lo = at("f1_lo", [128, KC, TP], F32R, F1 + FM)
    hid_hi = at("hid_hi", [128, QC, TP], F32R, F1)
    o = [R]

    def small(name, shape, dt=F32):
        n = 4
        for s in shape[1:]:
            n *= s
        t = at(name, shape, dt, o[0])
        o[0] += (n + 31) // 32 * 32
        return t

    ident = small("ident", [128, 128])
    ones = small("ones", [128, 128])
    bias_row = small("bias_row", [60, 128])
    bias_col = small("bias_col", [128, 60])
    stats = small("stats", [128, 2 * KC, 6])
    mv = small("mv", [128, NT, 2])
    var_eps = small("var_eps", [128, NT])
    neg_half = small("neg_half", [128, NT])
    rstd = small("rstd", [128, NT])
    neg_mr = small("neg_mr", [128, NT])
    asd = small("asd", [125, NT, 2 * NHD])
    as02 = small("as02", [125, NT, NHD])
    mx = small("mx", [125, NT, GH])
    z_tmp = small("z_tmp", [125, NT, GH])
    m_tmp = small("m_tmp", [125, NT, GH])
    mz = small("mz", [125, L, NT, 2 * GH])
    den = small("den", [125, NT])
    rden = small("rden", [125, NT])
    mix_sum = small("mix_sum", [128, 4])
    mix_r = small("mix_r", [128, 2])
    mix_t = small("mix_t", [128, 6])
    r_w = small("r_w", [128, KC, NE])
    r_b = small("r_b", [1, NE])
    gate_row = small("gate_row", [1, 6 * NE])
    gate_idx = small("gate_idx", [1, NE], U32)
    gate_col = small("gate_col", [128, 4])
    y_sum = small("y_sum", [128, KC])
    gl = small("gl", [128, 16])
    ln_scale = small("ln_scale", [128, KC])
    ln_bias = small("ln_bias", [128, KC])
    fcb_row = small("fcb_row", [4 * QC, 128])
    pb_row = small("pb_row", [2 * KC, 128])
    fcb = small("fcb", [128, 4 * QC])
    pb = small("pb", [128, 2 * KC])
    bounds = small("bounds", [5, 2], I32)
    bsm = small("bsm", [5, 8])
    row_t = small("row_t", [12, N])
    B = o[0]

    def span(shape, dt=F32):
        n = 2 if dt in (F16, BF16) else 4
        for s in shape[1:]:
            n *= s
        return (n + 31) // 32 * 32

    o[0] = B

    def take(name, shape, dt=F32):
        t = at(name, shape, dt, o[0])
        o[0] += span(shape, dt)
        return t

    gacc = take("gacc", [125, NT, D])
    P2 = o[0]
    g_tm = take("g_tm", [125, NT, 2 * GC])
    h_tm = take("h_tm", [125, 2, NT, GC + 1])
    PH1 = o[0]
    count = take("count", [125, NT, N])
    mask = take("mask", [125, NT, N], BF16)
    P1 = o[0]
    prob = take("prob", [125, NT, N])
    rows = take("rows", [128, 2, 2, N])
    as_row = take("as_row", [128, 2, N])
    q_fm = take("q_fm", [128, TP])
    k_fm = take("k_fm", [128, TP])
    t_fm = take("t_fm", [128, TP])
    y_hi = take("y_hi", [128, TP], F32R)
    y_lo = take("y_lo", [128, TP], F32R)
    junk = take("junk", [125, 2, N], BF16)
    o[0] = B
    a_bc = take("a_bc", [125, 2, 2, D])
    o[0] = P2 if P2 > o[0] else o[0]
    e_int = take("e_int", [EP, 2, 256], I32)
    e_f = take("e_f", [EP, 2, 256])
    e_col = take("e_col", [128, 2, 2, 2 * EP])
    e_lo5 = take("e_lo5", [5, 4, 96])
    iota = take("iota", [128, N], F16)
    oh_s = take("oh_s", [128, 2, N], F16)
    oh_d = take("oh_d", [128, 2, 126], F16)
    wide = take("wide", [125, 1126], F16)
    assert o[0] <= PH1, (o[0], PH1)
    o[0] = P1
    x_tm = take("x_tm", [125, NT, D])
    xn_tm = take("xn_tm", [125, NT, D])
    h_st = take("h_st", [125, 3, 2, GC + 1])
    junk1 = take("junk1", [125, 8, GC], BF16)
    count_ds = take("count_ds", [125, N])
    iota_f = take("iota_f", [128, N])
    wide_f = take("wide_f", [125, 1126])
    x2 = at("x2", [125, NT, D], F32, P2)
    o[0] = P2 + span([125, NT, D])
    xr = take("xr", [125, NT, D])
    k_tm = at("k_tm", [125, NT, D], F32, o[0] - span([125, NT, D]))
    gel_x = at("gel_x", [128, 3, TP], F32, o[0] - span([125, NT, D]))
    gel_u = at("gel_u", [128, 3, TP], F32, o[0] - span([125, NT, D]) + span([128, 3, TP]))
    assert 2 * span([128, 3, TP]) <= span([125, NT, D])
    z_fm = take("z_fm", [128, KC, TP])
    LATE = o[0]
    hid_lo = at("hid_lo", [128, QC, TP], F32R, LATE)
    xl_tm = take("xl_tm", [125, NT, D])
    v_fm = at("v_fm", [128, KC, TP], F32, LATE)
    qk_b = take("qk_b", [125, 2 * D])
    pj_b = take("pj_b", [125, D])
    e_blk = take("e_blk", [128, KC, 128])
    w_t = take("w_t", [128, KC, 128])
    o_fm = take("o_fm", [128, 2, TP])
    sm = take("sm", [128, 8 * KC])
    q_tm = at("q_tm", [125, NT, D], F32, B)
    m_tm = at("m_tm", [125, NT, D], F32, B)
    o_tm = at("o_tm", [125, 2, D], F32, B)

    ctx = ExitStack()
    with ctx:
        ps = ctx.enter_context(nc.psum_tensor("ps", [128, 4096], F32))
        AGG = 2048
        MISC = 3584
        sem = lambda name: ctx.enter_context(nc.semaphore(name))

        filled = [sem(f"filled{i}") for i in range(3)]
        freed = [sem(f"freed{i}") for i in range(3)]
        w_landed = [sem(f"w_landed{i}") for i in range(RAW)]
        w_hi_ready, w_lo_ready = sem("w_hi_ready"), sem("w_lo_ready")
        x_loaded, e_loaded, c_loaded = sem("x_loaded"), sem("e_loaded"), sem("c_loaded")
        e_pad = sem("e_pad")
        consts, consts16 = sem("consts"), sem("consts16")
        act_done, dve_done, pool_done = sem("act_done"), sem("dve_done"), sem("pool_done")
        var_ready, rstd_ready, nmr_ready = sem("var_ready"), sem("rstd_ready"), sem("nmr_ready")
        ln_out = sem("ln_out")
        hi_first = sem("hi_first")
        x2_split, y_split = sem("x2_split"), sem("y_split")
        edges_f, bounds_ready = sem("edges_f"), sem("bounds_ready")
        oh_ready = [sem(f"oh_ready{j}") for j in range(NT)]
        oh_used = [sem(f"oh_used{j}") for j in range(NT)]
        mask_ready = sem("mask_ready")
        a_loaded = [sem("a_loaded0"), sem("a_loaded1")]
        hs_summed = sem("hs_summed")
        hs_stored = [sem(f"hs_stored{i}") for i in range(3)]
        row_stored = sem("row_stored")
        asrow_loaded = [sem("asrow_loaded0"), sem("asrow_loaded1")]
        rows_loaded = [sem("rows_loaded0"), sem("rows_loaded1")]
        h_loaded = [sem("h_loaded0"), sem("h_loaded1")]
        gacc_set = sem("gacc_set")
        head_maxed, mz_ready = sem("head_maxed"), sem("mz_ready")
        as_scaled = sem("as_scaled")
        sm_low, sm_max, sm_exp, p_ready, p_used = (sem("sm_low"), sem("sm_max"), sem("sm_exp"), sem("p_ready"),
                                                   sem("p_used"))
        rden_ready, agg_freed, x2_sum = sem("rden_ready"), sem("agg_freed"), sem("x2_sum")
        mix_rr, y_ready, y_stored = sem("mix_rr"), sem("y_ready"), sem("y_stored")
        y_loaded, xr_loaded, xr_ready = sem("y_loaded"), sem("xr_loaded"), sem("xr_ready")
        late_loaded = sem("late_loaded")
        sc_sub, sc_exp, eblk_ready = sem("sc_sub"), sem("sc_exp"), sem("eblk_ready")
        o_stored = [sem("o_stored0"), sem("o_stored1")]
        m_loaded = sem("m_loaded")
        gl_in, gl_sum, gl_var, gl_rstd, gl_ready = (sem("gl_in"), sem("gl_sum"), sem("gl_var"), sem("gl_rstd"),
                                                    sem("gl_ready"))
        y_fm_ready = sem("y_fm_ready")
        gate_mm, gate_e_in, gate_e, gate_ready, gate_bc = (sem("gate_mm"), sem("gate_e_in"), sem("gate_e"),
                                                           sem("gate_ready"), sem("gate_bc"))
        eb_loaded, eb_ready = sem("eb_loaded"), sem("eb_ready")
        g_v, g_w, g_th, g_q, g_hi, g_lo = (sem("g_v"), sem("g_w"), sem("g_th"), sem("g_q"), sem("g_hi"),
                                           sem("g_lo"))
        fin_ready, o_left = sem("fin_ready"), [sem("o_left0"), sem("o_left1")]
        block = ctx.enter_context(nc.Block())

        def pb0(key):
            return 1024 * PAIR_OF[key][0]

        def halves(b, m=128):
            return ps[0:m, b:b + 1026].rearrange("p (h c) -> p h c", h=2)[:, :, 0:HT - 1]

        def two(ap):
            return ap.rearrange("p (h c) -> p h c", h=2)

        def tsp(b, m=128):
            return ps[0:m, b + 12:b + 12 + N]

        def wait_filled(eng, key):
            p, u = PAIR_OF[key]
            eng.wait_ge(filled[p], u + 1)

        def wait_freed(eng, key):
            p, u = PAIR_OF[key]
            eng.wait_ge(freed[p], u + 1)

        class Chain:

            def __init__(self, eng, s):
                self.eng, self.s, self.n = eng, s, 0

            def link(self, ins):
                ins.then_inc(self.s, 1)
                self.n += 1
                self.eng.wait_ge(self.s, self.n)

        last_reader = {}
        for kind, _, _, n0, jobs in STEPS:
            for i in range({"F": 1, "T": 3}.get(kind, 0)):
                last_reader[n0 + i] = jobs[-1]

        def slot_free(eng, n):
            if n >= RING:
                wait_filled(eng, last_reader[n - RING])

        def cols(w, c0, c):
            return w.rearrange("(k p) n -> p k n", p=128)[:, :, c0:c0 + c]

        def f_piece(name, args):
            if name == "ah":
                return cols(a["L0_gnn_W_ah"], 128 * args[0], 128)
            if name == "mix":
                return cols(a["L0_mix_w_qkv"], D * args[1] + 128 * args[0], 128)
            if name == "v":
                return cols(a["L0_ffn_W1_w"], 2 * D + 128 * args[0], 128)
            return cols(a["L0_ffn_W2_w"], 128 * args[0], 128)

        def t_piece(name, args, i):
            g = args[-1]
            if name == "h":
                w, r0, c0 = a[f"L0_gnn_W{args[0]}"], 0, 0
            elif name == "wo":
                w, r0, c0 = a["L0_gnn_W_out"], D * args[0], 0
            elif name == "proj":
                w, r0, c0 = a["L0_mix_w_proj"], 0, 0
            else:
                w, r0, c0 = a["L0_ffn_W1_w"], 0, D * args[0]
            return w[r0:r0 + D, :].rearrange("(k p) n -> p k n", p=128)[:, 2 * i:2 * i + 2, c0 + 384 * g:c0 + 384 * g + 384]

        pieces = []
        for kind, name, args, n0, _ in STEPS:
            if kind == "F":
                pieces.append((f_piece(name, args), 128))
            elif kind == "T":
                pieces += [(t_piece(name, args, i), 384) for i in range(3)]
        assert len(pieces) == MOE0

        @block.sync
        def _(sp):
            sp.dma_start(x_tm[0:112], a["x"].rearrange("(t p) n -> p t n", p=TT)[0:112]).then_inc(x_loaded, 16)
            sp.dma_start(x_tm[112:125], a["x"].rearrange("(t p) n -> p t n", p=TT)[112:125]).then_inc(x_loaded, 16)
            for n, (src, c) in enumerate(pieces):
                if n >= RAW:
                    sp.wait_ge(w_lo_ready, n - RAW + 1)
                sp.dma_start(w_raw[:, n % RAW, :].rearrange("p (k n) -> p k n", n=c), src).then_inc(w_landed[n % RAW], 16)
            sp.wait_ge(gate_ready, 1)
            e = [sp.value_load(gate_idx[0:1, i:i + 1], min_val=0, max_val=NE - 1) for i in range(2)]
            n = MOE0
            for it in range(4):
                fc = a["L0_ffn_fc_w"][bass.ds(e[it // 2], 1)].rearrange("a (k p) n -> (a p) k n", p=128)
                pj = a["L0_ffn_proj_w"][bass.ds(e[it // 2], 1)].rearrange("a (k p) n -> (a p) k n", p=128)
                srcs = [fc[:, :, 128 * (QC * (it % 2) + c):128 * (QC * (it % 2) + c + 1)] for c in range(QC)]
                srcs += [pj[:, QC * (it % 2) + KC * i:QC * (it % 2) + KC * i + KC, 128 * fo:128 * fo + 128]
                         for fo in range(KC) for i in range(2)]
                for src in srcs:
                    sp.wait_ge(w_lo_ready, n - RAW + 1)
                    sp.dma_start(w_raw[:, n % RAW, :].rearrange("p (k n) -> p k n", n=128), src).then_inc(w_landed[n % RAW], 16)
                    n += 1
            for t in range(NT):
                sp.wait_ge(freed[t % 3], MOE_USES[t % 3] + 24 + t // 3 + 1)
                for p0, p1 in ((0, 112), (112, 125)):
                    sp.dma_start(out[TT * t + p0:TT * t + p1, :], o_tm[p0:p1, t % 2, :]).then_inc(o_left[t % 2], 16)
            sp.wait_ge(o_left[0], 32 * 3)
            sp.wait_ge(o_left[1], 32 * 2)

        @block.gpsimd
        def _(pool):
            chain = Chain(pool, pool_done)
            pool.memset(e_int[:, :, :], 2000).then_inc(e_pad, 1)
            pool.memset(ones[:, :], 1.0)
            pool.memset(neg_half[:, :], -0.5)
            chain.link(pool.memset(ident[:, :], 0.0))
            pool.affine_select(out=ident[:, :], in_=ident[:, :], compare_op=ALU.not_equal, fill=1.0, base=0,
                               pattern=[[-1, 128]], channel_multiplier=1).then_inc(consts, 1)
            pool.iota(iota_f[:, :], pattern=[[1, N]], base=0, channel_multiplier=0, allow_small_or_imprecise_dtypes=True)
            pool.iota(bsm[:, 0:1], pattern=[[1, 1]], base=0, channel_multiplier=TT,
                      allow_small_or_imprecise_dtypes=True).then_inc(consts, 1)
            chain.link(pool.memset(wide_f[:, :], 0.0))
            pool.affine_select(out=wide_f[:, :], in_=wide_f[:, :], compare_op=ALU.not_equal, fill=1.0, base=500,
                               pattern=[[-1, 1126]], channel_multiplier=1).then_inc(consts, 1)
            for t in (f0_hi, f0_lo, f1_hi, f1_lo):
                last = pool.memset(t[:, :, N:TP].bitcast(F32), 0.0)
            last.then_inc(consts, 1)
            pool.memset(h_st[:, :, :, GC:GC + 1], 1.0).then_inc(consts, 1)

            def load_a(layer):
                if layer >= 2:
                    pool.wait_ge(hs_summed, 2 * NT * (layer - 1))
                for w, name in enumerate((f"L0_gnn_a_src{layer}", f"L0_gnn_a_dst{layer}")):
                    pool.dma_start(a_bc[:, layer % 2, w, :],
                                   a[name].rearrange("h c -> (h c)").rearrange("(a n) -> a n", a=1).to_broadcast([TT, D])
                                   ).then_inc(a_loaded[layer % 2], 16)

            load_a(0)
            load_a(1)
            pool.wait_ge(var_ready, 1)
            pool.tensor_tensor(rstd[0:TT, :], var_eps[0:TT, :], neg_half[0:TT, :], ALU.pow).then_inc(rstd_ready, 1)
            i = 0
            for layer in range(L):
                if layer == 2:
                    load_a(2)
                for g in range(2):
                    for t in range(NT):
                        wait_freed(pool, ("h", layer, g, t))
                        pool.dma_start(h_scr[GH * layer + 2 * g:GH * layer + 2 * g + 2, TT * t:TT * t + TT, :].rearrange("h p c -> p h c"),
                                       h_st[:, i % 3]).then_inc(hs_stored[i % 3], 16)
                        i += 1

            def load_as_row(j):
                if j >= 2:
                    pool.wait_ge(head_maxed, NT * (j - 1))
                pool.dma_start(as_row[:, j % 2, :], as_scr[j:j + 1, :].to_broadcast([128, N])).then_inc(asrow_loaded[j % 2], 16)

            def load_rows(j):
                layer, h = divmod(j, GH)
                if j >= 2:
                    pool.wait_ge(sm_max, NT * (j - 1))
                for k in range(2):
                    pool.dma_start(rows[:, j % 2, k, :], mz_scr[layer, k * GH + h:k * GH + h + 1, :].to_broadcast([128, N])
                                   ).then_inc(rows_loaded[j % 2], 16)

            def load_h(j):
                if j >= 2:
                    pool.wait_ge(p_used, NT * (j - 1))
                pool.dma_start(h_tm[:, j % 2], h_scr[j].rearrange("(t p) c -> p t c", p=TT)).then_inc(h_loaded[j % 2], 16)

            def mix_pow(f):
                wait_freed(pool, ("mix", f, 1))
                pool.tensor_tensor(mix_r[:, :], mix_sum[:, 1:4:2], neg_half[:, 0:2], ALU.pow).then_inc(mix_rr, 1)

            def store_y(f):
                pool.wait_ge(y_ready, f + 1)
                for i, t in enumerate((y_hi, y_lo)):
                    pool.dma_start(y_scr[i, 128 * f:128 * f + 128, :], t[:, :].bitcast(F32)).then_inc(y_stored, 16)

            def store_mz(layer):
                wait_freed(pool, ("mzT", layer))
                pool.dma_start(mz_scr[layer], row_t[0:2 * GH, :]).then_inc(row_stored, 16)
                pool.wait_ge(row_stored, 16 * (layer + 2))

            wait_freed(pool, ("asT",))
            pool.dma_start(as_scr, row_t[:, :]).then_inc(row_stored, 16)
            pool.wait_ge(hs_summed, 2 * NT * L)
            for t in range(NT):
                pool.dma_start(gacc[:, t, :], a["L0_gnn_b_out"].rearrange("(a n) -> a n", a=1).to_broadcast([TT, D])).then_inc(gacc_set, 16)
            for q in hs_stored:
                pool.wait_ge(q, 16 * (2 * NT * L // 3))
            pool.wait_ge(row_stored, 16)
            for j in range(2):
                load_as_row(j)
                load_h(j)
            load_as_row(2)
            load_as_row(3)
            mix_pow(0)
            store_mz(0)
            load_rows(0)
            load_rows(1)
            store_y(0)
            load_as_row(4)
            load_as_row(5)
            mix_pow(1)
            store_y(1)
            for j in range(NHD):
                if j + 2 < NHD:
                    load_h(j + 2)
                for nxt in AS_ROW_AT.get(j, ()):
                    load_as_row(nxt)
                if j in MIX_AT:
                    mix_pow(MIX_AT[j])
                if j in MZ_AT:
                    store_mz(MZ_AT[j])
                if j + 2 < NHD:
                    load_rows(j + 2)
                if j in MIX_AT:
                    store_y(MIX_AT[j])
            wait_filled(pool, ("mix", KC - 1, 2))
            pool.wait_ge(y_stored, 32 * KC)
            for i, t in enumerate((f0_hi, f0_lo)):
                pool.dma_start(t[:, :, :].bitcast(F32), y_scr[i].rearrange("(k p) n -> p k n", p=128)).then_inc(y_loaded, 16)
            pool.wait_ge(agg_freed, NHD)
            pool.wait_ge(p_used, NT * NHD)
            wait_filled(pool, ("gT", L - 1, 1, 2))
            for p0, p1 in ((0, 112), (112, 125)):
                pool.dma_start(xr[p0:p1], a["x"].rearrange("(t p) n -> p t n", p=TT)[p0:p1]).then_inc(xr_loaded, 16)
            pool.dma_start(pj_b[:, :], a["L0_mix_b_proj"].rearrange("(a n) -> a n", a=1).to_broadcast([TT, D])).then_inc(xr_loaded, 16)
            pool.dma_start(qk_b[:, :], a["L0_ffn_W1_b"][0:2 * D].rearrange("(a n) -> a n", a=1).to_broadcast([TT, 2 * D])).then_inc(late_loaded, 16)
            pool.wait_ge(xr_loaded, 48)
            for t in range(NT):
                pool.tensor_tensor(xr[:, t, :], xr[:, t, :], pj_b[:, :], ALU.add).then_inc(xr_ready, 1)
            pool.memset(e_blk[:, :, :], 0.0).then_inc(xr_ready, 1)
            pool.wait_ge(var_ready, 2)
            pool.tensor_tensor(rstd[0:TT, :], var_eps[0:TT, :], neg_half[0:TT, :], ALU.pow).then_inc(rstd_ready, 1)
            for hp in range(MH // 2):
                wait_freed(pool, ("av", hp))
                pool.dma_start(o_scr[128 * hp:128 * hp + 128, :], o_fm[:, hp % 2, 0:N]).then_inc(o_stored[hp % 2], 16)
            pool.wait_ge(o_stored[0], 48)
            pool.wait_ge(o_stored[1], 48)
            flat = o_scr.rearrange("d n -> (d n)").rearrange("(t p n) -> p t n", p=TT, n=D)
            for p0, p1 in ((0, 112), (112, 125)):
                pool.dma_start(m_tm[p0:p1], flat[p0:p1]).then_inc(m_loaded, 16)
            pool.wait_ge(gl_var, 1)
            pool.tensor_tensor(gl[:, 5:6], gl[:, 4:5], neg_half[:, 0:1], ALU.pow).then_inc(gl_rstd, 1)
            pool.wait_ge(gate_ready, 1)
            e = [pool.value_load(gate_idx[0:1, i:i + 1], min_val=0, max_val=NE - 1) for i in range(2)]
            for i in range(2):
                pool.dma_start(fcb_row[2 * QC * i:2 * QC * i + 2 * QC, :],
                               a["L0_ffn_fc_b"][bass.ds(e[i], 1)].rearrange("a (k p) -> (a k) p", p=128)).then_inc(eb_loaded, 16)
                pool.dma_start(pb_row[KC * i:KC * i + KC, :],
                               a["L0_ffn_proj_b"][bass.ds(e[i], 1)].rearrange("a (k p) -> (a k) p", p=128)).then_inc(eb_loaded, 16)
            pool.wait_ge(gl_var, 2)
            pool.tensor_tensor(gl[:, 5:6], gl[:, 4:5], neg_half[:, 0:1], ALU.pow).then_inc(gl_rstd, 1)

        @block.tensor
        def _(pe):
            def begin(key):
                p, u = PAIR_OF[key]
                if u:
                    pe.wait_ge(freed[p], u)
                return 1024 * p

            def f_product(b, slots, nk, xh, xl, k0=0, first=True, last=True, wait_k=None):
                for k in range(nk):
                    if wait_k:
                        wait_k(k)
                    wh = w_hi[:, slots[k // KC], 128 * (k % KC):128 * (k % KC) + 128]
                    wl = w_lo[:, slots[k // KC], 128 * (k % KC):128 * (k % KC) + 128]
                    for i, (w, x) in enumerate(((wh, xh), (wh, xl), (wl, xh))):
                        for s, c0 in ((0, 0), (1, TP - HT)):
                            ins = pe.matmul(ps[:, b + 512 * s:b + 512 * s + HT], w, x[:, k, c0:c0 + HT],
                                            start=(k == 0 and i == 0), stop=(k == nk - 1 and i == 2))
                return ins

            def t_product(b, n0, xh, xl, t):
                for k in range(KC):
                    s, c = (n0 + k // 2) % RING, 384 * (k % 2)
                    wh, wl = w_hi[:, s, c:c + 384], w_lo[:, s, c:c + 384]
                    h, lo = xh[:, k, TT * t:TT * t + TT], xl[:, k, TT * t:TT * t + TT]
                    for i, (x, w) in enumerate(((h, wh), (h, wl), (lo, wh))):
                        ins = pe.matmul(ps[0:TT, b:b + 384], x, w, start=(k == 0 and i == 0), stop=(k == KC - 1 and i == 2))
                return ins

            def transposes(b, src, m=128):
                for t in range(NT):
                    ins = pe.transpose(ps[0:m, b + 12 + TT * t:b + 12 + TT * t + TT], src(t), ident[0:TT, 0:TT])
                return ins

            operands = {"ah": (f0_hi, f0_lo), "h": (f1_hi, f1_lo), "mix": (f0_hi, f0_lo), "wo": (f1_hi, f1_lo),
                        "proj": (f0_hi, f0_lo), "qk": (f0_hi, f0_lo), "v": (f0_hi, f0_lo), "w2": (f1_hi, f1_lo)}
            trips = []

            def operand_ready(name, args):
                made = {"ah": "xnT", "mix": "xnT", "h": "ah", "w2": "mT"}
                if name in made:
                    for c in range(KC - 3, KC):
                        wait_freed(pe, (made[name], c))
                elif name == "wo":
                    for pr in range(2):
                        for c in range(3):
                            wait_freed(pe, ("gT", args[0], pr, c))
                elif name == "proj":
                    pe.wait_ge(y_loaded, 32)
                else:
                    pe.wait_ge(x2_split, KC)

            for kind, name, args, n0, jobs in STEPS:
                if kind in "FT":
                    xh, xl = operands[name]
                    operand_ready(name, args)
                    pe.wait_ge(w_lo_ready, n0 + (1 if kind == "F" else 3))
                if kind == "F":
                    b = begin(jobs[0])
                    f_product(b, [n0 % RING], KC, xh, xl).then_inc(filled[b // 1024], 1)
                elif kind == "T":
                    for t in range(NT):
                        b = begin(jobs[t])
                        t_product(b, n0, xh, xl, t).then_inc(filled[b // 1024], 1)
                elif name == "agg":
                    j = args[0]
                    if j == 0:
                        wait_freed(pe, THIRD_PAIR)
                    else:
                        pe.wait_ge(agg_freed, j)
                    pe.wait_ge(h_loaded[j % 2], 16 * (j // 2 + 1))
                    for i in range(NT):
                        pe.wait_ge(p_ready, NT * j + i + 1)
                        for d in range(NT):
                            ins = pe.matmul(ps[0:TT, AGG + 256 * d:AGG + 256 * d + GC + 1], prob[:, i, TT * d:TT * d + TT],
                                            h_tm[:, j % 2, i, :], start=(i == 0 and d % 2 == 0), stop=(i == NT - 1),
                                            skip_group_check=True)
                        ins.then_inc(p_used, 1)
                elif name == "edgesT":
                    b = begin(jobs[0])
                    pe.wait_ge(consts, 1)
                    pe.wait_ge(edges_f, 2)
                    for w in range(2):
                        for s in range(2):
                            ins = pe.transpose(ps[:, b + 96 * (2 * w + s):b + 96 * (2 * w + s) + EP],
                                               e_f[:, w, 128 * s:128 * s + 128], ident[0:EP, 0:EP])
                    ins.then_inc(filled[b // 1024], 1)
                elif name == "bounds":
                    b = begin(jobs[0])
                    pe.wait_ge(edges_f, 4)
                    for w in range(2):
                        ins = pe.matmul(ps[0:5, b + 96 * w:b + 96 * w + EP], stats[0:EP, 0, w:w + 1].to_broadcast([EP, 5]),
                                        ident[0:EP, 0:EP], start=True, stop=True)
                    ins.then_inc(filled[b // 1024], 1)
                elif name == "biasT":
                    b = begin(jobs[0])
                    pe.wait_ge(c_loaded, 16 * 12)
                    pe.transpose(ps[:, b:b + 60], bias_row[:, :], ident[0:60, 0:60]).then_inc(filled[b // 1024], 1)
                elif name == "count":
                    j = args[0]
                    b = begin(jobs[0])
                    if j == 0:
                        pe.wait_ge(consts16, 1)
                        pe.wait_ge(bounds_ready, 1)
                        trips += [pe.value_load(bounds[q:q + 1, 1:2], min_val=1, max_val=EP) for q in range(NT)]
                    for c0, c in ((0, 512), (512, N - 512)):
                        ins = pe.matmul(ps[0:TT, b + c0:b + c0 + c], wide[:, 500:500 + TT], wide[:, 500 - TT * j + c0:500 - TT * j + c0 + c],
                                        start=True, stop=False, skip_group_check=True)
                    ins.then_inc(oh_used[j], 2)
                    with pe.Fori(0, trips[j]) as q:
                        for s in range(2):
                            pe.wait_ge(oh_ready[j], 2 * q + (s + 1))
                            for c0, c in ((0, 512), (512, N - 512)):
                                ins = pe.matmul(ps[0:TT, b + c0:b + c0 + c], oh_d[:, s, 0:TT], oh_s[:, s, c0:c0 + c],
                                                start=False, stop=False, skip_group_check=True)
                            ins.then_inc(oh_used[j], 1)
                    for c0, c in ((0, 512), (512, N - 512)):
                        ins = pe.matmul(ps[0:TT, b + c0:b + c0 + c], wide[:, 1000:1000 + TT], wide[:, 0:c],
                                        start=False, stop=True, skip_group_check=True)
                    ins.then_inc(filled[b // 1024], 1)
                elif name == "countT":
                    j = args[0]
                    b = begin(jobs[0])
                    wait_freed(pe, ("count", j))
                    transposes(b, lambda i: count_ds[:, TT * i:TT * i + TT], TT).then_inc(filled[b // 1024], 1)
                elif name == "xnT":
                    c = args[0]
                    b = begin(jobs[0])
                    pe.wait_ge(ln_out, NT)
                    transposes(b, lambda t: xn_tm[:, t, 128 * c:128 * c + 128]).then_inc(filled[b // 1024], 1)
                elif name == "asT":
                    b = begin(jobs[0])
                    pe.wait_ge(hs_summed, 2 * NT * L)
                    transposes(b, lambda t: asd[:, t, 0:NHD], NHD).then_inc(filled[b // 1024], 1)
                elif name == "mzT":
                    layer = args[0]
                    b = begin(jobs[0])
                    pe.wait_ge(mz_ready, layer + 1)
                    transposes(b, lambda t: mz[:, layer, t, :], 2 * GH).then_inc(filled[b // 1024], 1)
                elif name == "gT":
                    layer, pr, c = args
                    b = begin(jobs[0])
                    pe.wait_ge(agg_freed, layer * GH + 2 * pr + 2)
                    transposes(b, lambda d: g_tm[:, d, 128 * c:128 * c + 128]).then_inc(filled[b // 1024], 1)
                elif name == "xT":
                    c = args[0]
                    b = begin(jobs[0])
                    pe.wait_ge(ln_out, 2 * NT)
                    transposes(b, lambda t: xl_tm[:, t, 128 * c:128 * c + 128]).then_inc(filled[b // 1024], 1)
                elif name == "scores":
                    b = begin(jobs[0])
                    wait_freed(pe, ("qk", 1, 1, NT - 1))
                    for hp in range(MH // 2):
                        for t in range(NT):
                            ins = pe.matmul(ps[:, b + 128 * hp:b + 128 * hp + 128], q_tm[:, t, 128 * hp:128 * hp + 128],
                                            k_tm[:, t, 128 * hp:128 * hp + 128], start=(t == 0), stop=(t == NT - 1))
                    ins.then_inc(filled[b // 1024], 1)
                elif name == "wT":
                    b = begin(jobs[0])
                    pe.wait_ge(eblk_ready, 1)
                    for hp in range(MH // 2):
                        ins = pe.transpose(ps[:, b + 128 * hp:b + 128 * hp + 128], e_blk[:, hp, :], ident[:, :])
                    ins.then_inc(filled[b // 1024], 1)
                elif name == "av":
                    hp = args[0]
                    b = begin(jobs[0])
                    wait_freed(pe, ("wT",))
                    wait_freed(pe, ("v", KC - 1))
                    for s, c0 in ((0, 0), (1, TP - HT)):
                        ins = pe.matmul(ps[:, b + 512 * s:b + 512 * s + HT], w_t[:, hp, :], v_fm[:, hp, c0:c0 + HT],
                                        start=True, stop=True)
                    ins.then_inc(filled[b // 1024], 1)
                elif name == "mT":
                    c = args[0]
                    b = begin(jobs[0])
                    pe.wait_ge(m_loaded, 32)
                    transposes(b, lambda t: m_tm[:, t, 128 * c:128 * c + 128]).then_inc(filled[b // 1024], 1)
                elif name == "expert_biasT":
                    for i in range(2):
                        pe.wait_ge(gl_in, i + 1)
                        pe.matmul(ps[:, MISC + i:MISC + i + 1], ones[:, :], gl[:, 2 * i:2 * i + 1], start=True, stop=True
                                  ).then_inc(gl_sum, 1)
                    pe.wait_ge(y_fm_ready, KC)
                    for k in range(KC):
                        ins = pe.matmul(ps[0:1, MISC + 8:MISC + 16], y_sum[:, k:k + 1], r_w[:, k, :], start=(k == 0), stop=(k == KC - 1))
                    ins.then_inc(gate_mm, 1)
                    pe.wait_ge(gate_ready, 1)
                    pe.matmul(ps[:, MISC + 16:MISC + 18], ones[0:1, :], gate_row[0:1, 3 * NE:3 * NE + 2], start=True, stop=True
                              ).then_inc(gate_bc, 1)
                    b = begin(jobs[0])
                    pe.wait_ge(eb_loaded, 64)
                    pe.transpose(ps[:, b:b + 4 * QC], fcb_row[:, :], ident[0:4 * QC, 0:4 * QC])
                    pe.transpose(ps[:, b + 64:b + 64 + 2 * KC], pb_row[:, :], ident[0:2 * KC, 0:2 * KC]).then_inc(filled[b // 1024], 1)

            pe.wait_ge(y_split, KC)

            def quarter(it):
                n0 = MOE0 + 24 * it
                for c in range(QC):
                    p = c % 3
                    pe.wait_ge(w_lo_ready, n0 + (c + 1))
                    pe.wait_ge(freed[p], MOE_USES[p] + 6 * it + c // 3)
                    f_product(1024 * p, [c % RING], KC, f0_hi, f0_lo).then_inc(filled[p], 1)
                for fo in range(KC):
                    p = fo % 3
                    pe.wait_ge(w_lo_ready, n0 + (QC + 2 * fo + 2))
                    pe.wait_ge(freed[p], MOE_USES[p] + 6 * it + (4 + fo // 3))
                    hidden = (lambda k: pe.wait_ge(g_lo, QC * it + (k + 4))) if fo == 0 else None
                    f_product(1024 * p, [(2 * fo) % RING, (2 * fo + 1) % RING], QC, hid_hi, hid_lo, wait_k=hidden
                              ).then_inc(filled[p], 1)

            with pe.Fori(0, 4) as it:
                quarter(it)
            for i in range(2):
                pe.wait_ge(gl_in, i + 3)
                pe.matmul(ps[:, MISC + i:MISC + i + 1], ones[:, :], gl[:, 2 * i:2 * i + 1], start=True, stop=True
                          ).then_inc(gl_sum, 1)
            pe.wait_ge(fin_ready, KC)
            for t in range(NT):
                p = t % 3
                pe.wait_ge(freed[p], MOE_USES[p] + 24 + t // 3)
                for c in range(KC):
                    ins = pe.transpose(ps[0:TT, 1024 * p + 128 * c:1024 * p + 128 * c + 128], z_fm[:, c, TT * t:TT * t + TT], ident[:, :])
                ins.then_inc(filled[p], 1)

        @block.scalar
        def _(act):
            chain = Chain(act, act_done)
            full = E // 256
            act.wait_ge(e_pad, 1)
            for i, name in enumerate(("src", "dst")):
                act.dma_start(e_int[0:full, i, :], a[name][0:full * 256].rearrange("(p n) -> p n", n=256)).then_inc(e_loaded, 16)
                act.dma_start(e_int[full:EP, i, 0:E - full * 256],
                               a[name][full * 256:E].rearrange("(a n) -> a n", a=1)).then_inc(e_loaded, 16)
            row = 0
            for name, sub in (("L0_gnn_b_ah", None), ("L0_gnn_b0", None), ("L0_gnn_b1", None), ("L0_gnn_b2", None),
                              ("L0_ffn_W1_b", slice(2 * D, 3 * D)), ("L0_ffn_W2_b", None), ("L0_ffn_ln1_w", None),
                              ("L0_ffn_ln1_b", None), ("L0_ffn_ln2_w", None), ("L0_ffn_ln2_b", None)):
                src = a[name] if sub is None else a[name][sub]
                act.dma_start(bias_row[row:row + KC, :], src.rearrange("(k p) -> k p", p=128)).then_inc(c_loaded, 16)
                row += KC
            act.dma_start(r_w[:, :, :], a["L0_ffn_r_w"].rearrange("(k p) n -> p k n", p=128)).then_inc(c_loaded, 16)
            act.dma_start(r_b[:, :], a["L0_ffn_r_b"].rearrange("(a n) -> a n", a=1)).then_inc(c_loaded, 16)
            split = [0]

            def pump(c, end=MOE0):
                while split[0] < min(c + RING, end):
                    n = split[0]
                    act.wait_ge(w_landed[n % RAW], 16 * (n // RAW + 1))
                    slot_free(act, n)
                    act.activation(w_hi[:, n % RING, :], w_raw[:, n % RAW, :], ACT.Copy).then_inc(w_hi_ready, 1)
                    split[0] += 1

            def free(ins, key):
                ins.then_inc(freed[PAIR_OF[key][0]], 1)

            sm_steps = [0]

            def softmax_step():
                g = sm_steps[0]
                sm_steps[0] += 1
                if g < NT * NHD:
                    j, i = divmod(g, NT)
                    if g == 0:
                        act.wait_ge(as_scaled, 1)
                    if i == 0:
                        act.wait_ge(rows_loaded[j % 2], 32 * (j // 2 + 1))
                    if g >= NT:
                        act.wait_ge(p_used, g - NT + 1)
                    act.activation(prob[:, i, :], rows[0:TT, j % 2, 1, :], ACT.Identity, bias=as02[:, i, j:j + 1]
                                   ).then_inc(sm_low, 1)
                if g:
                    act.wait_ge(sm_max, g)
                    act.activation(prob[:, (g - 1) % NT, :], prob[:, (g - 1) % NT, :], ACT.Exp).then_inc(sm_exp, 1)

            def normalize(src, dst, inv):
                act.wait_ge(nmr_ready, inv)
                for t in range(NT):
                    act.activation(dst[:, t, :], src[:, t, :], ACT.Identity, bias=neg_mr[0:TT, t:t + 1],
                                   scale=rstd[0:TT, t:t + 1]).then_inc(ln_out, 1)

            hs = [0]
            for si, (kind, name, args, n0, jobs) in enumerate(STEPS):
                if kind == "T":
                    pump(n0)
                for _ in range(SOFT[si]):
                    softmax_step()
                if kind == "F":
                    pump(n0)
                if name == "edgesT":
                    pump(RAW - RING)
                elif name == "biasT":
                    pump(0)
                elif name == "count":
                    j = args[0]
                    b = pb0(jobs[0])
                    wait_filled(act, jobs[0])
                    if j:
                        wait_filled(act, ("countT", j - 1))
                        act.wait_ge(mask_ready, j)
                    free(act.activation(count_ds[:, :], ps[0:TT, b:b + N], ACT.Copy), jobs[0])
                    if j == 0:
                        normalize(x_tm, xn_tm, 1)
                elif name == "countT":
                    j = args[0]
                    wait_filled(act, jobs[0])
                    ins = act.activation(count[:, :, TT * j:TT * j + TT],
                                         tsp(pb0(jobs[0]), TT).rearrange("p (i d) -> p i d", i=NT), ACT.Copy)
                    free(ins, jobs[0])
                elif name in ("xnT", "mT"):
                    c = args[0]
                    dst = f0_hi if name == "xnT" else f1_hi
                    wait_filled(act, jobs[0])
                    act.activation(dst[:, c, 0:N], tsp(pb0(jobs[0])), ACT.Copy).then_inc(hi_first, 1)
                elif name == "ah":
                    fo, = args
                    wait_filled(act, jobs[0])
                    wait_freed(act, ("biasT",))
                    v = halves(pb0(jobs[0]))
                    chain.link(act.activation(v, v, ACT.Relu, bias=bias_col[:, fo:fo + 1]))
                    act.activation(two(f1_hi[:, fo, :]), v, ACT.Copy).then_inc(hi_first, 1)
                elif name == "h":
                    layer, g = args
                    for t in range(NT):
                        i = hs[0]
                        hs[0] += 1
                        if i >= 3:
                            act.wait_ge(hs_stored[i % 3], 16 * (i // 3))
                            act.wait_ge(hs_summed, i - 2)
                        wait_filled(act, jobs[t])
                        b = pb0(jobs[t])
                        ins = act.activation(h_st[:, i % 3, :, 0:GC], ps[0:TT, b:b + 384].rearrange("p (h c) -> p h c", h=2), ACT.Copy)
                        free(ins, jobs[t])
                elif name in ("asT", "mzT"):
                    i = 0 if name == "asT" else args[0] + 1
                    wait_filled(act, jobs[0])
                    if i:
                        act.wait_ge(row_stored, 16 * i)
                    r = NHD if name == "asT" else 2 * GH
                    free(act.activation(row_t[0:r, :], tsp(pb0(jobs[0]), r), ACT.Copy), jobs[0])
                elif name == "mix":
                    f, part = args
                    if part < 2:
                        dst = (q_fm, k_fm)[part]
                        wait_filled(act, jobs[0])
                        if f:
                            act.wait_ge(y_ready, f)
                        elif part == 0:
                            for q in hs_stored:
                                act.wait_ge(q, 16 * (2 * NT * L // 3))
                            act.wait_ge(hs_summed, 2 * NT * L)
                        v = halves(pb0(jobs[0]))
                        chain.link(act.activation(two(dst[:, :]), v, ACT.Identity, accum_out=mix_sum[:, 2 * part:2 * part + 1]))
                        ins = act.activation(v, v, ACT.Square, accum_out=mix_sum[:, 2 * part + 1:2 * part + 2])
                        free(ins, jobs[0])
                elif name == "gT":
                    layer, pr, c = args
                    k = 3 * pr + c
                    wait_filled(act, jobs[0])
                    if k == 0 and layer:
                        wait_filled(act, ("wo", layer - 1, 1, NT - 1))
                    v = tsp(pb0(jobs[0]))
                    chain.link(act.activation(v, v, ACT.Relu, bias=bias_col[:, KC * (1 + layer) + k:KC * (1 + layer) + k + 1]))
                    act.activation(f1_hi[:, k, 0:N], v, ACT.Copy).then_inc(hi_first, 1)
                elif name == "agg":
                    j = args[0]
                    act.wait_ge(rden_ready, j + 1)
                    if j % 2 == 0 and j:
                        wait_filled(act, ("gT", (j - 1) // GH, ((j - 1) % GH) // 2, 2))
                    for d in range(NT):
                        ins = act.activation(g_tm[:, d, GC * (j % 2):GC * (j % 2) + GC], ps[0:TT, AGG + 256 * d:AGG + 256 * d + GC],
                                             ACT.Copy, scale=rden[:, d:d + 1])
                    ins.then_inc(agg_freed, 1)
                elif name == "xT":
                    c = args[0]
                    if c == 0:
                        normalize(x2, xl_tm, 2)
                    wait_filled(act, jobs[0])
                    free(act.activation(z_fm[:, c, 0:N], tsp(pb0(jobs[0])), ACT.Copy), jobs[0])
                elif name == "v":
                    fo, = args
                    wait_filled(act, jobs[0])
                    ins = act.activation(two(v_fm[:, fo, :]), halves(pb0(jobs[0])), ACT.Identity, bias=bias_col[:, 24 + fo:25 + fo])
                    free(ins, jobs[0])
                elif name == "scores":
                    act.wait_ge(sc_sub, 2)
                    act.wait_ge(xr_ready, NT + 1)
                    for s in range(2):
                        r = slice(64 * s, 64 * s + 64)
                        act.activation(e_blk[r, :, r], w_t[r, :, r], ACT.Exp, scale=1.0 / float(N) ** 0.5).then_inc(sc_exp, 1)
                elif name == "av":
                    hp, = args
                    wait_filled(act, jobs[0])
                    if hp >= 2:
                        act.wait_ge(o_stored[hp % 2], 16 * (hp // 2))
                    free(act.activation(two(o_fm[:, hp % 2, :]), halves(pb0(jobs[0])), ACT.Copy), jobs[0])
                elif name == "expert_biasT":
                    act.wait_ge(gl_ready, 1)
                    for k in range(KC):
                        act.activation(z_fm[:, k, 0:N], z_fm[:, k, 0:N], ACT.Identity, bias=ln_bias[:, k:k + 1],
                                       scale=ln_scale[:, k:k + 1], accum_out=y_sum[:, k:k + 1]).then_inc(y_fm_ready, 1)
                    act.wait_ge(gate_e_in, 1)
                    act.activation(gate_row[0:1, NE:2 * NE], gate_row[0:1, 0:NE], ACT.Exp).then_inc(gate_e, 1)
                    pump(MOE0, MOE0 + RING)

            act.wait_ge(eb_ready, 1)

            def split_hi(it, k):
                act.wait_ge(w_landed[k % RAW], 16 * (MOE0 // RAW + 1) + 128 * it + 16 * (k // RAW))
                act.wait_ge(*moe_reader(it, k - RING))
                act.activation(w_hi[:, k % RING, :], w_raw[:, k % RAW, :], ACT.Copy).then_inc(w_hi_ready, 1)

            def moe_reader(it, k):
                i = k if k < QC else QC + (k - QC) // 2
                return filled[i % 3], MOE_USES[i % 3] + 6 * it + (i // 3 + 1)

            def quarter(it, last):
                for c in range(QC + 2):
                    if c < QC:
                        if c:
                            split_hi(it, c + RING - 1)
                        p = c % 3
                        act.wait_ge(filled[p], MOE_USES[p] + 6 * it + (c // 3 + 1))
                        act.wait_ge(g_lo, QC * it + (c + 1))
                        b = fcb[:, bass.ds(QC * it + c, 1)]
                        v = halves(1024 * p)
                        act.activation(two(gel_x[:, c % 3, :]), v, ACT.Identity, bias=b)
                        act.activation(two(gel_u[:, c % 3, :]), v, ACT.Square, bias=b).then_inc(freed[p], 1)
                    if 1 <= c <= QC:
                        act.wait_ge(g_w, QC * it + c)
                        act.activation(gel_u[:, (c - 1) % 3, :], gel_u[:, (c - 1) % 3, :], ACT.Tanh, scale=GELU_C).then_inc(g_th, 1)
                    if c >= 2:
                        act.wait_ge(g_q, QC * it + (c - 1))
                        act.activation(hid_hi[:, c - 2, :], gel_u[:, (c - 2) % 3, :], ACT.Copy, scale=0.5).then_inc(g_hi, 1)
                split_hi(it, QC + RING - 1)
                for fo in range(KC):
                    ks = [QC + 2 * fo + RING, QC + 2 * fo + RING + 1]
                    for k in ks:
                        if k < 24 or not last:
                            if k < 24 + RING:
                                split_hi(it, k)

            with act.Fori(0, 3) as it:
                quarter(it, False)
            quarter(3, True)
            act.wait_ge(gl_ready, 2)
            for k in range(KC):
                act.activation(z_fm[:, k, 0:N], z_fm[:, k, 0:N], ACT.Identity, bias=ln_bias[:, k:k + 1],
                               scale=ln_scale[:, k:k + 1]).then_inc(fin_ready, 1)

        @block.vector
        def _(dve):
            chain = Chain(dve, dve_done)
            split = [0]

            def split_lo(n_slot, n_raw):
                return dve.tensor_tensor(w_lo[:, n_slot, :], w_raw[:, n_raw, :], w_hi[:, n_slot, :].bitcast(F32), ALU.subtract)

            def pump(c, end=MOE0):
                while split[0] < min(c + RING, end):
                    n = split[0]
                    dve.wait_ge(w_hi_ready, n + 1)
                    split_lo(n % RING, n % RAW).then_inc(w_lo_ready, 1)
                    split[0] += 1

            def free(ins, key):
                ins.then_inc(freed[PAIR_OF[key][0]], 1)

            def layer_stats(src, inv):
                for t in range(NT):
                    for g in range(2):
                        ins = dve.bn_stats(stats[0:TT, 2 * t + g, :], src[:, t, 384 * g:384 * g + 384])
                chain.link(ins)
                for t in range(NT):
                    ins = dve.bn_aggr(mv[0:TT, t, :], stats[0:TT, 2 * t:2 * t + 2, :])
                chain.link(ins)
                dve.tensor_scalar(var_eps[0:TT, :], mv[0:TT, :, 1], LN_EPS, None, ALU.add).then_inc(var_ready, 1)
                dve.wait_ge(rstd_ready, inv)
                dve.scalar_tensor_tensor(out=neg_mr[0:TT, :], in0=mv[0:TT, :, 0], scalar=-1.0, in1=rstd[0:TT, :],
                                         op0=ALU.mult, op1=ALU.mult).then_inc(nmr_ready, 1)

            def global_stats(i):
                for k in range(KC):
                    for g, (c0, c1) in enumerate(((0, 313), (313, N))):
                        ins = dve.bn_stats(stats[:, 2 * k + g, :], z_fm[:, k, c0:c1])
                chain.link(ins)
                dve.bn_aggr(gl[:, 0:2], stats[:, :, :]).then_inc(gl_in, 1)
                dve.wait_ge(gl_sum, 2 * i + 1)
                chain.link(dve.tensor_scalar(gl[:, 3:4], ps[:, MISC:MISC + 1], -1.0 / 128, None, ALU.mult))
                chain.link(dve.tensor_tensor(gl[:, 6:7], gl[:, 0:1], gl[:, 3:4], ALU.add))
                dve.scalar_tensor_tensor(out=gl[:, 2:3], in0=gl[:, 6:7], scalar=gl[:, 6:7], in1=gl[:, 1:2],
                                         op0=ALU.mult, op1=ALU.add).then_inc(gl_in, 1)
                dve.wait_ge(gl_sum, 2 * i + 2)
                dve.tensor_scalar(gl[:, 4:5], ps[:, MISC + 1:MISC + 2], float(KC * N) / (N * D - 1), GLN_EPS, ALU.mult,
                                  ALU.add).then_inc(gl_var, 1)
                dve.wait_ge(gl_rstd, i + 1)
                w0 = 36 + 12 * i
                chain.link(dve.tensor_scalar(ln_scale[:, :], bias_col[:, w0:w0 + KC], gl[:, 5:6], None, ALU.mult))
                dve.scalar_tensor_tensor(out=ln_bias[:, :], in0=ln_scale[:, :], scalar=gl[:, 3:4],
                                         in1=bias_col[:, w0 + KC:w0 + 2 * KC], op0=ALU.mult, op1=ALU.add).then_inc(gl_ready, 1)

            sm_steps = [0]

            def softmax_step():
                g = sm_steps[0]
                sm_steps[0] += 1
                if g < NT * NHD:
                    j, i = divmod(g, NT)
                    dve.wait_ge(sm_low, g + 1)
                    dve.scalar_tensor_tensor(out=prob[:, i, :], in0=rows[0:TT, j % 2, 0, :], scalar=asd[:, i, j:j + 1],
                                             in1=prob[:, i, :], op0=ALU.add, op1=ALU.max).then_inc(sm_max, 1)
                if g:
                    i = (g - 1) % NT
                    dve.wait_ge(sm_exp, g)
                    dve.scalar_tensor_tensor(out=prob[:, i, :], in0=prob[:, i, :], scalar=1.0, in1=count[:, i, :],
                                             op0=ALU.min, op1=ALU.mult).then_inc(p_ready, 1)

            def head_max(j):
                layer, h = divmod(j, GH)
                dve.wait_ge(asrow_loaded[j % 2], 16 * (j // 2 + 1))
                for d in range(NT):
                    if NT * j + d >= 2:
                        dve.wait_ge(head_maxed, NT * j + d - 1)
                    dve.tensor_tensor_reduce(out=junk[:, (NT * j + d) % 2, :], in0=mask[:, d, :], in1=as_row[0:TT, j % 2, :], scale=1.0,
                                             scalar=NEG, op0=ALU.add, op1=ALU.max, accum_out=mx[:, d, h:h + 1]
                                             ).then_inc(head_maxed, 1)
                if h == GH - 1:
                    dve.wait_ge(head_maxed, NT * (j + 1))
                    ad = asd[:, :, NHD + GH * layer:NHD + GH * layer + GH]
                    chain.link(dve.tensor_tensor(z_tmp[:, :, :], mx[:, :, :], ad, ALU.add))
                    chain.link(dve.scalar_tensor_tensor(out=m_tmp[:, :, :], in0=z_tmp[:, :, :], scalar=0.2,
                                                        in1=z_tmp[:, :, :], op0=ALU.mult, op1=ALU.max))
                    dve.tensor_tensor(mz[:, layer, :, 0:GH], ad, m_tmp[:, :, :], ALU.subtract)
                    dve.scalar_tensor_tensor(out=mz[:, layer, :, GH:2 * GH], in0=ad, scalar=0.2, in1=m_tmp[:, :, :],
                                             op0=ALU.mult, op1=ALU.subtract).then_inc(mz_ready, 1)

            def lo_part(dst, hi, src, key):
                dve.wait_ge(hi_first, hf[0] + 1)
                hf[0] += 1
                free(dve.tensor_tensor(dst, src, hi.bitcast(F32), ALU.subtract), key)

            def mask_of(j):
                wait_freed(dve, ("count", j))
                dve.tensor_scalar(mask[:, j, :], count_ds[:, :], 0.0, NEG, ALU.is_equal, ALU.mult).then_inc(mask_ready, 1)

            hf, hs, first = [0], [0], []
            dve.wait_ge(e_loaded, 64)
            for w in range(2):
                ins = dve.tensor_copy(e_f[:, w, :], e_int[:, w, :])
                ins.then_inc(edges_f, 1)
            dve.wait_ge(edges_f, 2)
            for i, op in enumerate((ALU.min, ALU.max)):
                dve.tensor_reduce(stats[0:EP, 0, i:i + 1], e_f[:, 1, :], AX_X, op).then_inc(edges_f, 1)
            dve.wait_ge(consts, 3)
            dve.tensor_copy(iota[:, :], iota_f[:, :])
            dve.tensor_copy(wide[:, :], wide_f[:, :]).then_inc(consts16, 1)
            for si, (kind, name, args, n0, jobs) in enumerate(STEPS):
                if kind != "T":
                    for _ in range(SOFT[si]):
                        softmax_step()
                if kind in "FT":
                    pump(n0)
                if name == "edgesT":
                    wait_filled(dve, jobs[0])
                    b = pb0(jobs[0])
                    v = ps[:, b:b + 4 * 96].rearrange("p (w s q) -> p (w s) q", w=2, s=2)[:, :, 0:EP]
                    free(dve.tensor_copy(e_col[:, :, :, 0:EP].rearrange("p w s q -> p (w s) q"), v), jobs[0])
                    pump(RAW - RING)
                elif name == "bounds":
                    wait_filled(dve, jobs[0])
                    b = pb0(jobs[0])
                    lo, hi = ps[0:5, b:b + EP], ps[0:5, b + 96:b + 96 + EP]
                    meets = e_lo5[:, 1, 0:EP]
                    dve.wait_ge(consts, 2)
                    chain.link(dve.tensor_scalar(bsm[:, 1:2], bsm[:, 0:1], float(TT), None, ALU.add))
                    chain.link(dve.tensor_scalar(e_lo5[:, 0, 0:EP], lo, bsm[:, 1:2], None, ALU.is_lt))
                    ins = dve.scalar_tensor_tensor(out=meets, in0=hi, scalar=bsm[:, 0:1], in1=e_lo5[:, 0, 0:EP],
                                                   op0=ALU.is_ge, op1=ALU.mult)
                    free(ins, jobs[0])
                    wait_freed(dve, jobs[0])
                    for i, (shift, op) in enumerate(((-128.0, ALU.min), (1.0, ALU.max))):
                        chain.link(dve.scalar_tensor_tensor(out=e_lo5[:, 2 + i, 0:EP], in0=iota_f[0:5, 0:EP], scalar=shift,
                                                            in1=meets, op0=ALU.add, op1=ALU.mult))
                        chain.link(dve.tensor_reduce(bsm[:, 2 + i:3 + i], e_lo5[:, 2 + i, 0:EP], AX_X, op))
                    chain.link(dve.tensor_scalar(bsm[:, 4:5], bsm[:, 2:3], 128.0, float(EP - 1), ALU.add, ALU.min))
                    chain.link(dve.tensor_tensor(bsm[:, 5:6], bsm[:, 3:4], bsm[:, 4:5], ALU.subtract))
                    chain.link(dve.tensor_scalar(bsm[:, 5:6], bsm[:, 5:6], 1.0, None, ALU.max))
                    dve.tensor_copy(bounds[:, :], bsm[:, 4:6]).then_inc(bounds_ready, 1)
                    dve.wait_ge(bounds_ready, 1)
                    first += [(dve.value_load(bounds[q:q + 1, 0:1], min_val=0, max_val=EP - 1),
                               dve.value_load(bounds[q:q + 1, 1:2], min_val=1, max_val=EP)) for q in range(NT)]
                elif name == "count":
                    j = args[0]
                    start, n = first[j]
                    with dve.Fori(0, n) as q:
                        for s in range(2):
                            dve.wait_ge(oh_used[j], 2 * q + (s + 1))
                            e = bass.ds(start + q, 1)
                            dve.tensor_scalar(oh_s[:, s, :], iota[:, :], e_col[:, 0, s, e], None, ALU.is_equal)
                            dve.tensor_scalar(oh_d[:, s, 0:TT], iota[:, TT * j:TT * j + TT], e_col[:, 1, s, e], None,
                                              ALU.is_equal).then_inc(oh_ready[j], 1)
                    if j == 0:
                        dve.wait_ge(x_loaded, 32)
                        layer_stats(x_tm, 1)
                    else:
                        mask_of(j - 1)
                elif name == "biasT":
                    mask_of(NT - 1)
                    wait_filled(dve, jobs[0])
                    b = pb0(jobs[0])
                    free(dve.tensor_copy(bias_col[:, :], ps[:, b:b + 60]), jobs[0])
                    pump(0)
                elif name in ("xnT", "mT"):
                    c = args[0]
                    hi, lo = (f0_hi, f0_lo) if name == "xnT" else (f1_hi, f1_lo)
                    lo_part(lo[:, c, 0:N], hi[:, c, 0:N], tsp(pb0(jobs[0])), jobs[0])
                elif name == "ah":
                    fo, = args
                    lo_part(two(f1_lo[:, fo, :]), two(f1_hi[:, fo, :]), halves(pb0(jobs[0])), jobs[0])
                elif name == "gT":
                    layer, pr, c = args
                    k = 3 * pr + c
                    lo_part(f1_lo[:, k, 0:N], f1_hi[:, k, 0:N], tsp(pb0(jobs[0])), jobs[0])
                elif name == "h":
                    layer, g = args
                    for t in range(NT):
                        i = hs[0]
                        hs[0] += 1
                        if g == 0 and t == 0:
                            dve.wait_ge(a_loaded[layer % 2], 32 * (layer // 2 + 1))
                        wait_freed(dve, jobs[t])
                        if i >= 2:
                            dve.wait_ge(hs_summed, i - 1)
                        for w in range(2):
                            for h in range(2):
                                hd = 2 * g + h
                                ins = dve.tensor_tensor_reduce(out=junk1[:, 4 * (i % 2) + 2 * w + h, :], in0=h_st[:, i % 3, h, 0:GC],
                                                               in1=a_bc[:, layer % 2, w, GC * hd:GC * hd + GC], scale=1.0, scalar=0.0,
                                                               op0=ALU.mult, op1=ALU.add,
                                                               accum_out=asd[:, t, NHD * w + GH * layer + hd:NHD * w + GH * layer + hd + 1])
                        ins.then_inc(hs_summed, 1)
                elif name == "asT":
                    dve.wait_ge(hs_summed, 2 * NT * L)
                    dve.tensor_scalar(as02[:, :, :], asd[:, :, 0:NHD], 0.2, None, ALU.mult).then_inc(as_scaled, 1)
                elif name == "mix":
                    f, part = args
                    if f == 0 and part < 2:
                        head_max(2 * part)
                        head_max(2 * part + 1)
                    if part == 2:
                        dve.wait_ge(mix_rr, f + 1)
                        chain.link(dve.tensor_tensor(mix_t[:, 0:2], mix_sum[:, 0:4:2], mix_r[:, :], ALU.mult))
                        chain.link(dve.tensor_tensor(mix_t[:, 2:3], mix_t[:, 0:1], mix_t[:, 1:2], ALU.mult))
                        chain.link(dve.tensor_scalar(mix_t[:, 3:4], mix_t[:, 2:3], float(N), None, ALU.add))
                        chain.link(dve.reciprocal(mix_t[:, 4:5], mix_t[:, 3:4]))
                        chain.link(dve.scalar_tensor_tensor(out=mix_t[:, 5:6], in0=mix_r[:, 0:1], scalar=mix_r[:, 1:2],
                                                            in1=mix_t[:, 4:5], op0=ALU.mult, op1=ALU.mult))
                        chain.link(dve.scalar_tensor_tensor(out=t_fm[:, :], in0=q_fm[:, :], scalar=mix_t[:, 5:6], in1=k_fm[:, :],
                                                            op0=ALU.mult, op1=ALU.mult))
                        wait_filled(dve, jobs[0])
                        free(dve.scalar_tensor_tensor(out=two(k_fm[:, :]), in0=two(k_fm[:, :]), scalar=mix_r[:, 1:2],
                                                      in1=halves(pb0(jobs[0])), op0=ALU.mult, op1=ALU.mult), jobs[0])
                        wait_freed(dve, jobs[0])
                        chain.link(dve.tensor_tensor(t_fm[:, :], t_fm[:, :], k_fm[:, :], ALU.mult))
                        if f:
                            dve.wait_ge(y_stored, 32 * f)
                        chain.link(dve.tensor_copy(y_hi[:, :], t_fm[:, :]))
                        dve.tensor_tensor(y_lo[:, :], t_fm[:, :], y_hi[:, :].bitcast(F32), ALU.subtract).then_inc(y_ready, 1)
                elif name == "agg":
                    j = args[0]
                    dve.wait_ge(p_used, NT * (j + 1))
                    chain.link(dve.tensor_scalar(den[:, :], ps[0:TT, AGG:AGG + 256 * NT].rearrange("p (d c) -> p d c", d=NT)[:, :, GC],
                                                 1e-16, None, ALU.add))
                    dve.reciprocal(rden[:, :], den[:, :]).then_inc(rden_ready, 1)
                    for nxt in MAX_AT.get(j, ()):
                        head_max(nxt)
                elif name in ("wo", "proj", "qk"):
                    g = args[-1]
                    soft = SOFT[si]
                    for t in range(NT):
                        if soft:
                            softmax_step()
                            soft -= 1
                        wait_filled(dve, jobs[t])
                        b = pb0(jobs[t])
                        p = ps[0:TT, b:b + 384]
                        c = slice(384 * g, 384 * g + 384)
                        if name == "wo":
                            if args[0] == 0:
                                dve.wait_ge(gacc_set, 16 * NT)
                            free(dve.tensor_tensor(gacc[:, t, c], gacc[:, t, c], p, ALU.add), jobs[t])
                            if args[0] == L - 1:
                                wait_freed(dve, jobs[t])
                                dve.wait_ge(xr_ready, t + 1)
                                dve.scalar_tensor_tensor(out=x2[:, t, c], in0=gacc[:, t, c], scalar=0.0, in1=xr[:, t, c],
                                                         op0=ALU.max, op1=ALU.add).then_inc(x2_sum, 1)
                        elif name == "proj":
                            dve.wait_ge(x2_sum, 2 * NT)
                            free(dve.tensor_tensor(x2[:, t, c], x2[:, t, c], p, ALU.add), jobs[t])
                        else:
                            if args == (0, 0) and t == 0:
                                dve.wait_ge(late_loaded, 16)
                            dst = (q_tm, k_tm)[args[0]]
                            free(dve.tensor_tensor(dst[:, t, c], p, qk_b[:, D * args[0] + 384 * g:D * args[0] + 384 * g + 384],
                                                   ALU.add), jobs[t])
                    assert soft == 0
                    if name == "proj" and g == 1:
                        wait_freed(dve, jobs[NT - 1])
                        dve.memset(z_fm[:, :, N:TP], 0.0)
                        layer_stats(x2, 2)
                elif name == "xT":
                    c = args[0]
                    wait_freed(dve, jobs[0])
                    chain.link(dve.tensor_copy(f0_hi[:, c, 0:N], z_fm[:, c, 0:N]))
                    dve.tensor_tensor(f0_lo[:, c, 0:N], z_fm[:, c, 0:N], f0_hi[:, c, 0:N].bitcast(F32), ALU.subtract
                                      ).then_inc(x2_split, 1)
                elif name == "scores":
                    wait_filled(dve, jobs[0])
                    b = pb0(jobs[0])
                    for s in range(2):
                        r = slice(64 * s, 64 * s + 64)
                        v = ps[r, b:b + 128 * KC].rearrange("p (k c) -> p k c", k=KC)[:, :, 64 * s:64 * s + 64]
                        chain.link(dve.tensor_reduce(sm[r, 0:KC], v, AX_X, ALU.max))
                        ins = dve.tensor_tensor(w_t[r, :, r], v, sm[r, 0:KC].to_broadcast([64, KC, 64]), ALU.subtract)
                        ins.then_inc(sc_sub, 1)
                    dve.wait_ge(sc_exp, 2)
                    chain.link(dve.tensor_reduce(sm[:, KC:2 * KC], e_blk[:, :, :], AX_X, ALU.add))
                    chain.link(dve.reciprocal(sm[:, 2 * KC:3 * KC], sm[:, KC:2 * KC]))
                    dve.tensor_tensor(e_blk[:, :, :], e_blk[:, :, :], sm[:, 2 * KC:3 * KC].to_broadcast([128, KC, 128]),
                                      ALU.mult).then_inc(eblk_ready, 1)
                    free(dve.memset(sm[:, 3 * KC:3 * KC + 1], 0.0), jobs[0])
                elif name == "wT":
                    wait_filled(dve, jobs[0])
                    b = pb0(jobs[0])
                    free(dve.tensor_copy(w_t[:, :, :].rearrange("p k c -> p (k c)"), ps[:, b:b + 128 * KC]), jobs[0])
                elif name == "w2":
                    fo, = args
                    wait_filled(dve, jobs[0])
                    v = two(z_fm[:, fo, :])
                    free(dve.scalar_tensor_tensor(out=v, in0=halves(pb0(jobs[0])), scalar=bias_col[:, 30 + fo:31 + fo], in1=v,
                                                  op0=ALU.add, op1=ALU.add), jobs[0])
                    if fo == KC - 1:
                        wait_freed(dve, jobs[0])
                        global_stats(0)
                elif name == "expert_biasT":
                    gr = lambda i, n=NE: gate_row[0:1, i:i + n]
                    for k in range(KC):
                        dve.wait_ge(y_fm_ready, k + 1)
                        chain.link(dve.tensor_copy(f0_hi[:, k, 0:N], z_fm[:, k, 0:N]))
                        dve.tensor_tensor(f0_lo[:, k, 0:N], z_fm[:, k, 0:N], f0_hi[:, k, 0:N].bitcast(F32), ALU.subtract
                                          ).then_inc(y_split, 1)
                    dve.wait_ge(gate_mm, 1)
                    chain.link(dve.scalar_tensor_tensor(out=gr(40), in0=ps[0:1, MISC + 8:MISC + 16], scalar=1.0 / N,
                                                        in1=r_b[:, :], op0=ALU.mult, op1=ALU.add))
                    chain.link(dve.tensor_reduce(gr(32, 1), gr(40), AX_X, ALU.max))
                    dve.tensor_scalar(gr(0), gr(40), gr(32, 1), None, ALU.subtract).then_inc(gate_e_in, 1)
                    dve.wait_ge(gate_e, 1)
                    chain.link(dve.tensor_reduce(gr(33, 1), gr(8), AX_X, ALU.add))
                    chain.link(dve.reciprocal(gr(34, 1), gr(33, 1)))
                    chain.link(dve.tensor_scalar(gr(16), gr(8), gr(34, 1), None, ALU.mult))
                    chain.link(dve.max(gr(24), gr(16)))
                    dve.max_index(gate_idx[:, :], gr(24), gr(16)).then_inc(gate_ready, 1)
                    dve.wait_ge(gate_bc, 1)
                    for i in range(2):
                        chain.link(dve.tensor_copy(gate_col[:, i:4:2], ps[:, MISC + 16:MISC + 18]))
                    wait_filled(dve, jobs[0])
                    b = pb0(jobs[0])
                    dve.tensor_copy(fcb[:, :], ps[:, b:b + 4 * QC]).then_inc(eb_ready, 1)
                    free(dve.tensor_copy(pb[:, :], ps[:, b + 64:b + 64 + 2 * KC]), jobs[0])
                    wait_freed(dve, jobs[0])
                    chain.link(dve.tensor_scalar(ln_scale[:, :], pb[:, 0:KC], gate_col[:, 0:1], None, ALU.mult))
                    chain.link(dve.scalar_tensor_tensor(out=ln_bias[:, :], in0=pb[:, KC:2 * KC], scalar=gate_col[:, 2:3],
                                                        in1=ln_scale[:, :], op0=ALU.mult, op1=ALU.add))
                    for k in range(KC):
                        ins = dve.tensor_scalar(z_fm[:, k, :], z_fm[:, k, :], ln_bias[:, k:k + 1], None, ALU.add)
                    chain.link(ins)
                    dve.memset(gl[:, 8:9], 0.0).then_inc(g_lo, 3)
                    pump(MOE0, MOE0 + RING)

            def lo_piece(it, k):
                dve.wait_ge(w_hi_ready, MOE0 + 24 * it + (k + 1))
                split_lo(k % RING, k % RAW).then_inc(w_lo_ready, 1)

            def quarter(it, last):
                for c in range(QC + 2):
                    if c < QC:
                        if c:
                            lo_piece(it, c + RING - 1)
                        x, u = gel_x[:, c % 3, :], gel_u[:, c % 3, :]
                        dve.wait_ge(freed[c % 3], MOE_USES[c % 3] + 6 * it + (c // 3 + 1))
                        dve.tensor_scalar(u, u, GELU_A, 1.0, ALU.mult, ALU.add).then_inc(g_v, 1)
                        dve.wait_ge(g_v, QC * it + (c + 1))
                        dve.tensor_tensor(u, u, x, ALU.mult).then_inc(g_w, 1)
                    if 1 <= c <= QC:
                        x, u = gel_x[:, (c - 1) % 3, :], gel_u[:, (c - 1) % 3, :]
                        dve.wait_ge(g_th, QC * it + c)
                        dve.scalar_tensor_tensor(out=u, in0=u, scalar=1.0, in1=x, op0=ALU.add, op1=ALU.mult).then_inc(g_q, 1)
                    if c >= 2:
                        u = gel_u[:, (c - 2) % 3, :]
                        dve.wait_ge(g_hi, QC * it + (c - 1))
                        dve.scalar_tensor_tensor(out=hid_lo[:, c - 2, :], in0=u, scalar=0.5, in1=hid_hi[:, c - 2, :].bitcast(F32),
                                                 op0=ALU.mult, op1=ALU.subtract).then_inc(g_lo, 1)
                lo_piece(it, QC + RING - 1)
                for fo in range(KC):
                    p = fo % 3
                    dve.wait_ge(filled[p], MOE_USES[p] + 6 * it + (4 + fo // 3 + 1))
                    v = two(z_fm[:, fo, :])
                    dve.scalar_tensor_tensor(out=v, in0=halves(1024 * p), scalar=gate_col[:, bass.ds(it, 1)], in1=v,
                                             op0=ALU.mult, op1=ALU.add).then_inc(freed[p], 1)
                    for k in (QC + 2 * fo + RING, QC + 2 * fo + RING + 1):
                        if k < (24 if last else 24 + RING):
                            lo_piece(it, k)

            with dve.Fori(0, 3) as it:
                quarter(it, False)
            quarter(3, True)
            for p in range(3):
                dve.wait_ge(freed[p], MOE_USES[p] + 24)
            global_stats(1)
            for t in range(NT):
                p = t % 3
                dve.wait_ge(filled[p], MOE_USES[p] + 24 + t // 3 + 1)
                if t >= 2:
                    dve.wait_ge(o_left[t % 2], 32 * (t // 2))
                dve.tensor_tensor(o_tm[:, t % 2, :], ps[0:TT, 1024 * p:1024 * p + D], x2[:, t, :], ALU.add).then_inc(freed[p], 1)


def kernel(**inputs):
    import numpy as _np
    import concourse.bacc as _bacc
    from concourse import mybir as _mybir
    from concourse.bass_utils import run_bass_kernel_spmd as _run

    nc = _bacc.Bacc("TRN2", target_bir_lowering=False, num_devices=1)
    arrays, aps = {}, {}
    for name, value in inputs.items():
        if name == "edge_weight1":
            continue
        v = _np.ascontiguousarray(value)
        arrays[f"in_{name}_dram"] = v
        aps[name] = nc.dram_tensor(f"in_{name}_dram", v.shape, _mybir.dt.from_np(v.dtype), kind="ExternalInput").ap()
    out = nc.dram_tensor("out_0_dram", (N, D), _mybir.dt.float32, kind="ExternalOutput").ap()
    gnn_block(nc, aps, out)
    r = _run(nc, [arrays], core_ids=[0])
    return r.results[0]["out_0_dram"]
```

```python
from contextlib import ExitStack

import concourse.bass as bass
from concourse import mybir

ALU = mybir.AluOpType
ACT = mybir.ActivationFunctionType
F32, F32R, F16, BF16, I32, U32 = (mybir.dt.float32, mybir.dt.float32r, mybir.dt.float16, mybir.dt.bfloat16,
                                  mybir.dt.int32, mybir.dt.uint32)
AX_X = mybir.AxisListType.X

N, D, E = 625, 768, 20625
NT, TT = 5, 125
TP, HT = 626, 314
KC = D // 128
GH, GC = 4, 192
L = 3
NHD = L * GH
MH = 12
EP = (E + 255) // 256
NO_EDGE = 2000
HID, NE = 4 * D, 8
QC = HID // 2 // 128
RING, RAW = 6, 3
NEG = -1.0e30
LN_EPS, GLN_EPS = 1e-5, 1e-12
GELU_C, GELU_A = 0.7978845608028654, 0.044715

PAIRS = 3
CHUNKS = 6
SPAN = PAIRS * CHUNKS
ECW = 2 * EP + SPAN



class Psum:

    def __init__(self):
        self.at, self.last, self.when, self.uses, self.clock = {}, {}, [0] * 8, [0] * 8, 0

    def place(self, key, width, banks):
        ok = [b for b in banks if all(x in banks for x in range(b, b + width)) and (width == 1 or b % 2 == 0)]
        home = min(ok, key=lambda b: (max(self.when[b:b + width]), b))
        self.clock += 1
        before = []
        for b in range(home, home + width):
            self.when[b] = self.clock
            if b in self.last and self.last[b] not in before:
                before.append(self.last[b])
            self.last[b] = key
        self.at[key] = (home, self.uses[home], before)
        self.uses[home] += 1


def plan():
    steps, psum = [], Psum()
    slot = [0]
    banks = [0, 1, 2, 3, 6, 7]

    def f_step(name, *args):
        psum.place((name, *args), 2, banks)
        steps.append(("F", name, args, slot[0], (name, *args)))
        slot[0] += 1

    def t_step(name, *args):
        psum.place((name, *args), 1, banks)
        steps.append(("T", name, args, slot[0], (name, *args)))
        if args[-1] == NT - 1:
            slot[0] += 3

    def x_step(name, *args, width=2, where=None):
        psum.place((name, *args), width, where or banks)
        steps.append(("X", name, args, slot[0], (name, *args)))

    def mark(name, *args):
        steps.append(("M", name, args, slot[0], None))

    x_step("edgesT", width=1)
    x_step("bounds", width=1)
    for t in range(NT):
        x_step("xnT", t)
    x_step("biasT", width=1)
    todo = []
    for j in range(NT):
        for c in range(CHUNKS):
            todo.append(("chunk", j, c))
            if j and c == 0:
                todo[-1:] = [("chunk", j, c), ("countT", j - 1)]
        todo.append(("count", j))

    def some_count(n):
        while n and todo:
            name, *a = todo.pop(0)
            if name == "chunk":
                if a[1] == 0:
                    psum.place(("count", a[0]), 2, [4, 5])
                mark("chunk", *a)
                n -= 1
            elif name == "count":
                steps.append(("X", "count", (a[0],), slot[0], ("count", a[0])))
            else:
                x_step("countT", *a)

    for fo in range(KC):
        f_step("ah", fo)
        some_count(1)
    for layer in range(L):
        for g in range(2):
            for t in range(NT):
                t_step("h", layer, g, t)
                if t < NT - 1:
                    some_count(1)
    some_count(9)
    while todo:
        some_count(1)
    before_sums = []
    for b in (4, 5, 6):
        if psum.last[b] not in before_sums:
            before_sums.append(psum.last[b])
        psum.last[b] = "heads"
    banks = [0, 1, 2, 3, 7]
    x_step("asT")
    x_step("countT", NT - 1)
    fs = [("mix", f, part) for f in range(KC) for part in range(3)]

    def ft(n):
        for _ in range(n):
            f_step(*fs.pop(0))

    def wo(layer, g, t0, t1):
        for t in range(t0, t1):
            t_step("wo", layer, g, t)

    gt = lambda layer, pr, c: x_step("gT", layer, pr, c)
    agg = lambda j: mark("agg", j)
    ft(6)
    x_step("mzT", 0)
    ft(3)
    agg(0)
    ft(2)
    agg(1)
    ft(1), gt(0, 0, 0), gt(0, 0, 1), gt(0, 0, 2)
    agg(2)
    ft(1)
    x_step("mzT", 1)
    agg(3)
    ft(1), gt(0, 1, 0), gt(0, 1, 1), gt(0, 1, 2)
    agg(4)
    wo(0, 0, 0, 5)
    agg(5)
    wo(0, 1, 0, 5), gt(1, 0, 0), gt(1, 0, 1), gt(1, 0, 2)
    agg(6)
    ft(1)
    x_step("mzT", 2)
    agg(7)
    ft(1), gt(1, 1, 0), gt(1, 1, 1), gt(1, 1, 2)
    agg(8)
    wo(1, 0, 0, 5)
    agg(9)
    wo(1, 1, 0, 5), gt(2, 0, 0), gt(2, 0, 1), gt(2, 0, 2)
    agg(10)
    ft(2)
    agg(11)
    for c in range(3):
        gt(2, 1, c)
    wo(2, 0, 0, 5), wo(2, 1, 0, 5)
    banks = [0, 1, 2, 3, 4, 5, 6, 7]
    for g in range(2):
        for t in range(NT):
            t_step("proj", g, t)
            if g and t >= 2:
                x_step("xT", t - 2)
    for t in (3, 4):
        x_step("xT", t)
    for u in range(2):
        for g in range(2):
            for t in range(NT):
                t_step("qk", u, g, t)
    x_step("scores")
    f_step("v", 0)
    f_step("v", 1)
    f_step("v", 2)
    x_step("wT")
    for hp in range(MH // 2):
        if hp >= 2 and hp + 1 < KC:
            f_step("v", hp + 1)
        x_step("av", hp)
        if hp >= 3:
            x_step("mT", hp - 3)
    for t in (3, 4):
        x_step("mT", t)
    for fo in range(KC):
        f_step("w2", fo)
    banks = [0, 1, 2, 3, 4, 5]
    x_step("expert_biasT", width=1)
    return steps, slot[0], psum, before_sums


STEPS, MOE0, PSUM, BEFORE_SUMS = plan()
assert MOE0 % RING == 0
MOE_USES = [PSUM.uses[2 * p] for p in range(3)]
AGG_AT = [i for i, s in enumerate(STEPS) if s[1] == "agg"]
FIRST_MIX = next(i for i, s in enumerate(STEPS) if s[1] == "mzT")
MAX_AT = {0: (4, 5), 1: (6,), 2: (7,), 4: (8, 9), 5: (10,), 6: (11,)}
AS_ROW_AT = {0: (6, 7), 2: (8, 9), 4: (10, 11)}
MIX_AT = {1: 3, 4: 4, 10: 5}
Y_AT = {1: 3, 6: 4, 10: 5}
MZ_AT = {2: 1, 6: 2}


def softmax_schedule():
    n = [0] * len(STEPS)
    for j in range(NHD):
        lo = AGG_AT[j - 1] + 1 if j else FIRST_MIX + 1
        between = list(range(lo, AGG_AT[j]))
        early = (4 if j else 5) if between else 0
        for i in range(early):
            n[between[i * len(between) // early]] += 1
        n[AGG_AT[j]] = (6 if j == 0 else 5) - early
    return n


SOFT = softmax_schedule()


def gnn_block(nc, a, out):
    h_scr = nc.dram_tensor("h_scr", (NHD, N, GC + 1), F32).ap()
    as_scr = nc.dram_tensor("as_scr", (NHD, N), F32).ap()
    mz_scr = nc.dram_tensor("mz_scr", (L, 2 * GH, N), F32).ap()
    y_scr = nc.dram_tensor("y_scr", (2, D, TP), F32).ap()
    o_scr = nc.dram_tensor("o_scr", (D, N), F32).ap()

    base = (nc.sbuf_base + 31) // 32 * 32
    top = nc.sbuf_usable_end

    def at(name, shape, dt, off):
        size = 2 if dt in (F16, BF16) else 4
        n = size
        for s in shape[1:]:
            n *= s
        assert off % 32 == 0 and base + off + n <= top, (name, off, n)
        return nc.alloc_sbuf_tensor_at(name, shape, dt, offset=base + off)

    SLOT = D * 4
    FM = (KC * TP * 4 + 31) // 32 * 32
    w_hi = at("w_hi", [128, RING, D], F32R, 0)
    w_lo = at("w_lo", [128, RING, D], F32R, RING * SLOT)
    w_raw = at("w_raw", [128, RAW, D], F32, 2 * RING * SLOT)
    F0 = (2 * RING + RAW) * SLOT
    F1 = F0 + 2 * FM
    R = F1 + 2 * FM
    f0_hi = at("f0_hi", [128, KC, TP], F32R, F0)
    f0_lo = at("f0_lo", [128, KC, TP], F32R, F0 + FM)
    f1_hi = at("f1_hi", [128, KC, TP], F32R, F1)
    f1_lo = at("f1_lo", [128, KC, TP], F32R, F1 + FM)
    hid_hi = at("hid_hi", [128, QC, TP], F32R, F1)
    o = [R]

    def small(name, shape, dt=F32):
        n = 4
        for s in shape[1:]:
            n *= s
        t = at(name, shape, dt, o[0])
        o[0] += (n + 31) // 32 * 32
        return t

    ident = small("ident", [128, 128])
    ones = small("ones", [128, 128])
    bias_row = small("bias_row", [60, 128])
    bias_col = small("bias_col", [128, 60])
    stats = small("stats", [128, 2 * KC, 6])
    mv = small("mv", [128, NT, 2])
    var_eps = small("var_eps", [128, NT])
    neg_half = small("neg_half", [128, NT])
    rstd = small("rstd", [128, NT])
    neg_mr = small("neg_mr", [128, NT])
    asd = small("asd", [125, NT, 2 * NHD])
    as02 = small("as02", [125, NT, NHD])
    mx = small("mx", [125, NT, GH])
    z_tmp = small("z_tmp", [125, NT, GH])
    m_tmp = small("m_tmp", [125, NT, GH])
    mz = small("mz", [125, L, NT, 2 * GH])
    den = small("den", [125, NT])
    rden = small("rden", [125, NT])
    mix_sum = small("mix_sum", [128, 4])
    mix_r = small("mix_r", [128, 2])
    mix_t = small("mix_t", [128, 6])
    r_w = small("r_w", [128, KC, NE])
    r_b = small("r_b", [1, NE])
    gate_row = small("gate_row", [1, 6 * NE])
    gate_idx = small("gate_idx", [1, NE], U32)
    gate_col = small("gate_col", [128, 4])
    z_mv = small("z_mv", [128, KC, 2])
    y_mean = small("y_mean", [128, KC])
    gl = small("gl", [128, 16])
    ln_scale = small("ln_scale", [128, KC])
    ln_bias = small("ln_bias", [128, KC])
    fcb_row = small("fcb_row", [4 * QC, 128])
    pb_row = small("pb_row", [2 * KC, 128])
    fcb = small("fcb", [128, 4 * QC])
    pb = small("pb", [128, 2 * KC])
    bounds = small("bounds", [5, 2], I32)
    bsm = small("bsm", [5, 8])
    e_ends = small("e_ends", [EP, 2])
    row_t = small("row_t", [12, N])
    relu_t = small("relu_t", [128, 2, TP])
    B = o[0]

    def span(shape, dt=F32):
        n = 2 if dt in (F16, BF16) else 4
        for s in shape[1:]:
            n *= s
        return (n + 31) // 32 * 32

    o[0] = B

    def take(name, shape, dt=F32):
        t = at(name, shape, dt, o[0])
        o[0] += span(shape, dt)
        return t

    gacc = take("gacc", [125, NT, D])
    P2 = o[0]
    g_tm = take("g_tm", [125, NT, 2 * GC])
    h_tm = take("h_tm", [125, 2, NT, GC + 1])
    PH1 = o[0]
    count = take("count", [125, NT, N])
    mask = take("mask", [125, NT, N], BF16)
    P1 = o[0]
    prob = take("prob", [125, NT, N])
    rows = take("rows", [128, 2, 2, N])
    as_row = take("as_row", [128, 2, N])
    q_fm = take("q_fm", [128, TP])
    k_fm = take("k_fm", [128, TP])
    t_fm = take("t_fm", [128, TP])
    y_hi = take("y_hi", [128, TP], F32R)
    y_lo = take("y_lo", [128, TP], F32R)
    junk = take("junk", [125, 2, N], BF16)
    o[0] = B
    a_bc = take("a_bc", [125, 2, 2, D])
    o[0] = P2 if P2 > o[0] else o[0]
    e_int = take("e_int", [EP, 2, 256], I32)
    e_f = take("e_f", [EP, 2, 256])
    e_col = take("e_col", [128, 2, 2, ECW])
    e_lo5 = take("e_lo5", [5, 4, 96])
    iota = take("iota", [128, N], F16)
    oh2_s = take("oh2_s", [128, 2, N], F16)
    oh2_d = take("oh2_d", [128, 2, 126], F16)
    wide = take("wide", [125, 1126], F16)
    assert o[0] <= PH1, (o[0], PH1)
    o[0] = P1
    x_tm = take("x_tm", [125, NT, D])
    h_st = take("h_st", [125, 3, 2, GC + 1])
    junk1 = take("junk1", [125, 4, GC], BF16)
    oh_s = take("oh_s", [128, 4 * PAIRS, N], F16)
    oh_d = take("oh_d", [128, 4 * PAIRS, 126], F16)
    iota_f = at("iota_f", [128, N], F32, o[0])
    count_ds = take("count_ds", [128, N])
    x2 = at("x2", [125, NT, D], F32, P2)
    o[0] = P2 + span([125, NT, D])
    xr = take("xr", [125, NT, D])
    k_tm = at("k_tm", [125, NT, D], F32, o[0] - span([125, NT, D]))
    gel_x = at("gel_x", [128, 3, TP], F32, o[0] - span([125, NT, D]))
    gel_u = at("gel_u", [128, 3, TP], F32, o[0] - span([125, NT, D]) + span([128, 3, TP]))
    assert 2 * span([128, 3, TP]) <= span([125, NT, D])
    z_fm = take("z_fm", [128, KC, TP])
    LATE = o[0]
    hid_lo = at("hid_lo", [128, QC, TP], F32R, LATE)
    xl_tm = take("xl_tm", [125, NT, D])
    v_fm = at("v_fm", [128, KC, TP], F32, LATE)
    qk_b = take("qk_b", [125, 2 * D])
    pj_b = take("pj_b", [125, D])
    e_blk = take("e_blk", [128, KC, 128])
    w_t = take("w_t", [128, KC, 128])
    o_fm = at("o_fm", [128, 2, TP], F32, B - span([128, 2, TP]))
    sm = take("sm", [128, 8 * KC])
    q_tm = at("q_tm", [125, NT, D], F32, B)
    m_tm = at("m_tm", [125, NT, D], F32, B)
    o_tm = at("o_tm", [125, 2, D], F32, B)

    ctx = ExitStack()
    with ctx:
        ps = ctx.enter_context(nc.psum_tensor("ps", [128, 4096], F32))
        AGG = 2048
        MISC = 3584
        sem = lambda name: ctx.enter_context(nc.semaphore(name))

        filled = [sem(f"filled{i}") for i in range(8)]
        freed = [sem(f"freed{i}") for i in range(8)]
        w_landed = [sem(f"w_landed{i}") for i in range(RAW)]
        w_hi_ready, w_lo_ready = sem("w_hi_ready"), sem("w_lo_ready")
        ln_stats, ln_mv = sem("ln_stats"), sem("ln_mv")
        pads, e_col_set, chunk_tile, chunk_used = sem("pads"), sem("e_col_set"), sem("chunk_tile"), sem("chunk_used")
        x_loaded = [sem(f"x_loaded{t}") for t in range(NT)]
        e_loaded, c_loaded = sem("e_loaded"), sem("c_loaded")
        e_pad = sem("e_pad")
        consts, consts16 = sem("consts"), sem("consts16")
        act_done, dve_done, pool_done = sem("act_done"), sem("dve_done"), sem("pool_done")
        var_ready, rstd_ready, nmr_ready = sem("var_ready"), sem("rstd_ready"), sem("nmr_ready")
        ln_out = sem("ln_out")
        hi_first = sem("hi_first")
        relu_split = sem("relu_split")
        y_split = sem("y_split")
        edges_f, bounds_ready = sem("edges_f"), sem("bounds_ready")
        oh_ready = [sem(f"oh_ready{j}") for j in range(NT)]
        oh_used = [sem(f"oh_used{j}") for j in range(NT)]
        mask_ready = sem("mask_ready")
        a_loaded = [sem("a_loaded0"), sem("a_loaded1")]
        hs_summed = sem("hs_summed")
        hs_stored = [sem(f"hs_stored{i}") for i in range(3)]
        row_stored = sem("row_stored")
        asrow_loaded = [sem("asrow_loaded0"), sem("asrow_loaded1")]
        rows_loaded = [sem("rows_loaded0"), sem("rows_loaded1")]
        h_loaded = [sem("h_loaded0"), sem("h_loaded1")]
        gacc_set = sem("gacc_set")
        head_maxed, mz_ready = sem("head_maxed"), sem("mz_ready")
        as_scaled = sem("as_scaled")
        sm_low, sm_max, sm_exp, p_ready, p_used = (sem("sm_low"), sem("sm_max"), sem("sm_exp"), sem("p_ready"),
                                                   sem("p_used"))
        rden_ready, agg_freed, x2_sum = sem("rden_ready"), sem("agg_freed"), sem("x2_sum")
        mix_rr, y_ready, y_stored = sem("mix_rr"), sem("y_ready"), sem("y_stored")
        y_loaded, xr_loaded, xr_ready = sem("y_loaded"), sem("xr_loaded"), sem("xr_ready")
        late_loaded = sem("late_loaded")
        sc_sub, sc_exp, eblk_ready = sem("sc_sub"), sem("sc_exp"), sem("eblk_ready")
        o_stored = [sem("o_stored0"), sem("o_stored1")]
        m_loaded = [sem(f"m_loaded{t}") for t in range(NT)]
        gl_in, gl_sum, gl_var, gl_rstd, gl_ready = (sem("gl_in"), sem("gl_sum"), sem("gl_var"), sem("gl_rstd"),
                                                    sem("gl_ready"))
        y_fm_ready, z_set = sem("y_fm_ready"), sem("z_set")
        gate_in, gate_mm, gate_e_in, gate_e, gate_ready, gate_bc = (sem("gate_in"), sem("gate_mm"), sem("gate_e_in"), sem("gate_e"),
                                                           sem("gate_ready"), sem("gate_bc"))
        eb_loaded, eb_ready = sem("eb_loaded"), sem("eb_ready")
        g_v, g_w, g_th, g_q, g_hi, g_lo = (sem("g_v"), sem("g_w"), sem("g_th"), sem("g_q"), sem("g_hi"),
                                           sem("g_lo"))
        fin_ready, o_left = sem("fin_ready"), [sem("o_left0"), sem("o_left1")]
        block = ctx.enter_context(nc.Block())

        def pb0(key):
            return 512 * PSUM.at[key][0]

        def halves(b, m=128):
            return ps[0:m, b + 2:b + 1024].rearrange("p (h c) -> p h c", h=2)[:, :, 0:HT - 1]

        def two(ap):
            return ap.rearrange("p (h c) -> p h c", h=2)

        def tsp(b, m=128):
            return ps[0:m, b + 12:b + 12 + N]

        def wait_filled(eng, key):
            p, u, _ = PSUM.at[key]
            eng.wait_ge(filled[p], u + 1)

        def wait_freed(eng, key):
            p, u, _ = PSUM.at[key]
            eng.wait_ge(freed[p], u + 1)

        class Chain:

            def __init__(self, eng, s):
                self.eng, self.s, self.n = eng, s, 0

            def link(self, ins):
                ins.then_inc(self.s, 1)
                self.n += 1
                self.eng.wait_ge(self.s, self.n)

        last_reader = {}
        for kind, _, _, n0, job in STEPS:
            for i in range({"F": 1, "T": 3}.get(kind, 0)):
                last_reader[n0 + i] = job

        def slot_free(eng, n):
            if n >= RING:
                wait_filled(eng, last_reader[n - RING])

        def cols(w, c0, c):
            return w.rearrange("(k p) n -> p k n", p=128)[:, :, c0:c0 + c]

        def f_piece(name, args):
            if name == "ah":
                return cols(a["L0_gnn_W_ah"], 128 * args[0], 128)
            if name == "mix":
                return cols(a["L0_mix_w_qkv"], D * args[1] + 128 * args[0], 128)
            if name == "v":
                return cols(a["L0_ffn_W1_w"], 2 * D + 128 * args[0], 128)
            return cols(a["L0_ffn_W2_w"], 128 * args[0], 128)

        def t_piece(name, args, i):
            g = args[-2]
            if name == "h":
                w, r0, c0 = a[f"L0_gnn_W{args[0]}"], 0, 0
            elif name == "wo":
                w, r0, c0 = a["L0_gnn_W_out"], D * args[0], 0
            elif name == "proj":
                w, r0, c0 = a["L0_mix_w_proj"], 0, 0
            else:
                w, r0, c0 = a["L0_ffn_W1_w"], 0, D * args[0]
            return w[r0:r0 + D, :].rearrange("(k p) n -> p k n", p=128)[:, 2 * i:2 * i + 2, c0 + 384 * g:c0 + 384 * g + 384]

        pieces = []
        for kind, name, args, n0, _ in STEPS:
            if kind == "F":
                pieces.append((f_piece(name, args), 128))
            elif kind == "T" and args[-1] == 0:
                pieces += [(t_piece(name, args, i), 384) for i in range(3)]
        assert len(pieces) == MOE0

        @block.sync
        def _(sp):
            for t in range(NT):
                for p0, p1 in ((0, 112), (112, 125)):
                    sp.dma_start(x_tm[p0:p1, t, :], a["x"][TT * t + p0:TT * t + p1, :]).then_inc(x_loaded[t], 16)
            for n, (src, c) in enumerate(pieces):
                if n >= RAW:
                    sp.wait_ge(w_lo_ready, n - RAW + 1)
                sp.dma_start(w_raw[:, n % RAW, :].rearrange("p (k n) -> p k n", n=c), src).then_inc(w_landed[n % RAW], 16)
            sp.wait_ge(gate_ready, 1)
            e = [sp.value_load(gate_idx[0:1, i:i + 1], min_val=0, max_val=NE - 1) for i in range(2)]
            n = MOE0
            for it in range(4):
                fc = a["L0_ffn_fc_w"][bass.ds(e[it // 2], 1)].rearrange("a (k p) n -> (a p) k n", p=128)
                pj = a["L0_ffn_proj_w"][bass.ds(e[it // 2], 1)].rearrange("a (k p) n -> (a p) k n", p=128)
                srcs = [fc[:, :, 128 * (QC * (it % 2) + c):128 * (QC * (it % 2) + c + 1)] for c in range(QC)]
                srcs += [pj[:, QC * (it % 2) + KC * i:QC * (it % 2) + KC * i + KC, 128 * fo:128 * fo + 128]
                         for fo in range(KC) for i in range(2)]
                for src in srcs:
                    sp.wait_ge(w_lo_ready, n - RAW + 1)
                    sp.dma_start(w_raw[:, n % RAW, :].rearrange("p (k n) -> p k n", n=128), src).then_inc(w_landed[n % RAW], 16)
                    n += 1
            for t in range(NT):
                sp.wait_ge(freed[2 * (t % 3)], MOE_USES[t % 3] + 24 + t // 3 + 1)
                for p0, p1 in ((0, 112), (112, 125)):
                    sp.dma_start(out[TT * t + p0:TT * t + p1, :], o_tm[p0:p1, t % 2, :]).then_inc(o_left[t % 2], 16)
            sp.wait_ge(o_left[0], 32 * 3)
            sp.wait_ge(o_left[1], 32 * 2)

        @block.gpsimd
        def _(pool):
            chain = Chain(pool, pool_done)
            pool.memset(e_int[64:EP, :, :], NO_EDGE).then_inc(e_pad, 1)
            pool.wait_ge(e_pad, 1)
            pool.memset(neg_half[:, :], -0.5)
            chain.link(pool.memset(ident[:, :], 0.0))
            pool.affine_select(out=ident[:, :], in_=ident[:, :], compare_op=ALU.not_equal, fill=1.0, base=0,
                               pattern=[[-1, 128]], channel_multiplier=1).then_inc(consts, 1)
            pool.memset(e_col[:, :, :, EP:ECW], float(NO_EDGE)).then_inc(e_col_set, 1)
            pool.iota(iota_f[:, :], pattern=[[1, N]], base=0, channel_multiplier=0, allow_small_or_imprecise_dtypes=True)
            pool.iota(bsm[:, 0:1], pattern=[[1, 1]], base=0, channel_multiplier=TT,
                      allow_small_or_imprecise_dtypes=True).then_inc(consts, 1)

            def rstd_of(n):
                t = n % NT
                pool.wait_ge(var_ready, n + 1)
                pool.tensor_tensor(rstd[0:TT, t:t + 1], var_eps[0:TT, t:t + 1], neg_half[0:TT, 0:1], ALU.pow).then_inc(rstd_ready, 1)

            chain.link(pool.memset(wide[:, :], 0.0))
            pool.affine_select(out=wide[:, :], in_=wide[:, :], compare_op=ALU.not_equal, fill=1.0, base=500,
                               pattern=[[-1, 1126]], channel_multiplier=1).then_inc(consts, 1)
            for t in range(NT):
                rstd_of(t)
            for t in (f0_hi, f0_lo, f1_hi, f1_lo):
                last = pool.memset(t[:, :, N:TP].bitcast(F32), 0.0)
            last.then_inc(pads, 1)
            pool.memset(ones[:, :], 1.0)
            pool.memset(h_st[:, :, :, GC:GC + 1], 1.0).then_inc(pads, 1)

            def load_a(layer):
                if layer >= 2:
                    pool.wait_ge(hs_summed, 2 * NT * (layer - 1))
                for w, name in enumerate((f"L0_gnn_a_src{layer}", f"L0_gnn_a_dst{layer}")):
                    pool.dma_start(a_bc[:, layer % 2, w, :],
                                   a[name].rearrange("h c -> (h c)").rearrange("(a n) -> a n", a=1).to_broadcast([TT, D])
                                   ).then_inc(a_loaded[layer % 2], 16)

            load_a(0)
            load_a(1)
            pool.wait_ge(pads, 2)
            i = 0
            for layer in range(L):
                if layer == 2:
                    load_a(2)
                for g in range(2):
                    for t in range(NT):
                        wait_freed(pool, ("h", layer, g, t))
                        pool.dma_start(h_scr[GH * layer + 2 * g:GH * layer + 2 * g + 2, TT * t:TT * t + TT, :].rearrange("h p c -> p h c"),
                                       h_st[:, i % 3]).then_inc(hs_stored[i % 3], 16)
                        i += 1

            def load_as_row(j):
                if j >= 2:
                    pool.wait_ge(head_maxed, NT * (j - 1))
                pool.dma_start(as_row[:, j % 2, :], as_scr[j:j + 1, :].to_broadcast([128, N])).then_inc(asrow_loaded[j % 2], 16)

            def load_rows(j):
                layer, h = divmod(j, GH)
                if j >= 2:
                    pool.wait_ge(sm_max, NT * (j - 1))
                for k in range(2):
                    pool.dma_start(rows[:, j % 2, k, :], mz_scr[layer, k * GH + h:k * GH + h + 1, :].to_broadcast([128, N])
                                   ).then_inc(rows_loaded[j % 2], 16)

            def load_h(j):
                if j >= 2:
                    pool.wait_ge(p_used, NT * (j - 1))
                pool.dma_start(h_tm[:, j % 2], h_scr[j].rearrange("(t p) c -> p t c", p=TT)).then_inc(h_loaded[j % 2], 16)

            def mix_pow(f):
                wait_freed(pool, ("mix", f, 1))
                pool.tensor_tensor(mix_r[:, :], mix_sum[:, 1:4:2], neg_half[:, 0:2], ALU.pow).then_inc(mix_rr, 1)

            def store_y(f):
                pool.wait_ge(y_ready, f + 1)
                for i, t in enumerate((y_hi, y_lo)):
                    pool.dma_start(y_scr[i, 128 * f:128 * f + 128, :], t[:, :].bitcast(F32)).then_inc(y_stored, 16)

            def store_mz(layer):
                wait_freed(pool, ("mzT", layer))
                pool.dma_start(mz_scr[layer], row_t[0:2 * GH, :]).then_inc(row_stored, 16)
                pool.wait_ge(row_stored, 16 * (layer + 2))

            wait_freed(pool, ("asT",))
            pool.dma_start(as_scr, row_t[:, :]).then_inc(row_stored, 16)
            pool.wait_ge(hs_summed, 2 * NT * L)
            for t in range(NT):
                pool.dma_start(gacc[:, t, :], a["L0_gnn_b_out"].rearrange("(a n) -> a n", a=1).to_broadcast([TT, D])).then_inc(gacc_set, 16)
            for q in hs_stored:
                pool.wait_ge(q, 16 * (2 * NT * L // 3))
            pool.wait_ge(row_stored, 16)
            for j in range(2):
                load_as_row(j)
                load_h(j)
            load_as_row(2)
            load_as_row(3)
            mix_pow(0)
            store_y(0)
            mix_pow(1)
            store_mz(0)
            load_rows(0)
            load_rows(1)
            store_y(1)
            load_as_row(4)
            load_as_row(5)
            mix_pow(2)
            store_y(2)
            for j in range(NHD):
                if j + 2 < NHD:
                    load_h(j + 2)
                for nxt in AS_ROW_AT.get(j, ()):
                    load_as_row(nxt)
                if j in MIX_AT:
                    mix_pow(MIX_AT[j])
                if j in MZ_AT:
                    store_mz(MZ_AT[j])
                if j + 2 < NHD:
                    load_rows(j + 2)
                if j in Y_AT:
                    store_y(Y_AT[j])
            wait_filled(pool, ("mix", KC - 1, 2))
            pool.wait_ge(y_stored, 32 * KC)
            for i, t in enumerate((f0_hi, f0_lo)):
                pool.dma_start(t[:, :, :].bitcast(F32), y_scr[i].rearrange("(k p) n -> p k n", p=128)).then_inc(y_loaded, 16)
            pool.wait_ge(agg_freed, NHD)
            pool.wait_ge(p_used, NT * NHD)
            wait_filled(pool, ("gT", L - 1, 1, 2))
            for p0, p1 in ((0, 112), (112, 125)):
                pool.dma_start(xr[p0:p1], a["x"].rearrange("(t p) n -> p t n", p=TT)[p0:p1]).then_inc(xr_loaded, 16)
            pool.dma_start(pj_b[:, :], a["L0_mix_b_proj"].rearrange("(a n) -> a n", a=1).to_broadcast([TT, D])).then_inc(xr_loaded, 16)
            pool.dma_start(qk_b[:, :], a["L0_ffn_W1_b"][0:2 * D].rearrange("(a n) -> a n", a=1).to_broadcast([TT, 2 * D])).then_inc(late_loaded, 16)
            pool.wait_ge(xr_loaded, 48)
            for t in range(NT):
                pool.tensor_tensor(xr[:, t, :], xr[:, t, :], pj_b[:, :], ALU.add).then_inc(xr_ready, 1)
            pool.memset(e_blk[:, :, :], 0.0).then_inc(xr_ready, 1)
            for t in range(NT):
                rstd_of(NT + t)
            for t in range(NT):
                wait_freed(pool, ("xT", t))
            for k in range(KC):
                pool.tensor_tensor(z_fm[:, k, 0:N], f0_hi[:, k, 0:N].bitcast(F32), f0_lo[:, k, 0:N].bitcast(F32), ALU.add
                                   ).then_inc(z_set, 1)
            flat = o_scr.rearrange("d n -> (d n)").rearrange("(t p n) -> t p n", p=TT, n=D)
            for hp in range(MH // 2):
                wait_freed(pool, ("av", hp))
                pool.dma_start(o_scr[128 * hp:128 * hp + 128, :], o_fm[:, hp % 2, 0:N]).then_inc(o_stored[hp % 2], 16)
                if hp == 0:
                    continue
                t = hp - 1
                assert TT * D * (t + 1) <= 128 * N * (hp + 1)
                pool.wait_ge(o_stored[0], 16 * (hp // 2 + 1))
                pool.wait_ge(o_stored[1], 16 * ((hp + 1) // 2))
                for p0, p1 in ((0, 112), (112, 125)):
                    pool.dma_start(m_tm[p0:p1, t, :], flat[t, p0:p1, :]).then_inc(m_loaded[t], 16)
            pool.wait_ge(gl_var, 1)
            pool.tensor_tensor(gl[:, 5:6], gl[:, 4:5], neg_half[:, 0:1], ALU.pow).then_inc(gl_rstd, 1)
            pool.wait_ge(gate_ready, 1)
            e = [pool.value_load(gate_idx[0:1, i:i + 1], min_val=0, max_val=NE - 1) for i in range(2)]
            for i in range(2):
                pool.dma_start(fcb_row[2 * QC * i:2 * QC * i + 2 * QC, :],
                               a["L0_ffn_fc_b"][bass.ds(e[i], 1)].rearrange("a (k p) -> (a k) p", p=128)).then_inc(eb_loaded, 16)
                pool.dma_start(pb_row[KC * i:KC * i + KC, :],
                               a["L0_ffn_proj_b"][bass.ds(e[i], 1)].rearrange("a (k p) -> (a k) p", p=128)).then_inc(eb_loaded, 16)
            pool.wait_ge(gl_var, 2)
            pool.tensor_tensor(gl[:, 5:6], gl[:, 4:5], neg_half[:, 0:1], ALU.pow).then_inc(gl_rstd, 1)

        @block.tensor
        def _(pe):
            def begin(key):
                home, _, before = PSUM.at[key]
                for k in before:
                    if k == "heads":
                        pe.wait_ge(agg_freed, NHD)
                    else:
                        wait_freed(pe, k)
                return 512 * home

            def f_product(b, slots, nk, xh, xl, k0=0, first=True, last=True, wait_k=None):
                for k in range(nk):
                    if wait_k:
                        wait_k(k)
                    wh = w_hi[:, slots[k // KC], 128 * (k % KC):128 * (k % KC) + 128]
                    wl = w_lo[:, slots[k // KC], 128 * (k % KC):128 * (k % KC) + 128]
                    for i, (w, x) in enumerate(((wh, xh), (wh, xl), (wl, xh))):
                        for o, c0 in ((2, 0), (512, TP - HT)):
                            ins = pe.matmul(ps[:, b + o:b + o + HT], w, x[:, k, c0:c0 + HT],
                                            start=(k == 0 and i == 0), stop=(k == nk - 1 and i == 2))
                return ins

            def t_product(b, n0, xh, xl, t):
                for k in range(KC):
                    s, c = (n0 + k // 2) % RING, 384 * (k % 2)
                    wh, wl = w_hi[:, s, c:c + 384], w_lo[:, s, c:c + 384]
                    h, lo = xh[:, k, TT * t:TT * t + TT], xl[:, k, TT * t:TT * t + TT]
                    for i, (x, w) in enumerate(((h, wh), (h, wl), (lo, wh))):
                        ins = pe.matmul(ps[0:TT, b:b + 384], x, w, start=(k == 0 and i == 0), stop=(k == KC - 1 and i == 2))
                return ins

            def chunk_transposes(b, src):
                for c in range(KC):
                    ins = pe.transpose(ps[:, b + 12 + TT * c:b + 12 + TT * c + TT], src[:, 128 * c:128 * c + 128], ident[0:TT, 0:TT])
                return ins

            def transposes(b, src, m=128):
                for t in range(NT):
                    ins = pe.transpose(ps[0:m, b + 12 + TT * t:b + 12 + TT * t + TT], src(t), ident[0:TT, 0:TT])
                return ins

            operands = {"ah": (f0_hi, f0_lo), "h": (f1_hi, f1_lo), "mix": (f0_hi, f0_lo), "wo": (f1_hi, f1_lo),
                        "proj": (f0_hi, f0_lo), "qk": (f0_hi, f0_lo), "v": (f0_hi, f0_lo), "w2": (f1_hi, f1_lo)}
            trips = []

            def operand_ready(name, args):
                made = {"ah": "xnT", "mix": "xnT", "qk": "xT", "v": "xT", "w2": "mT"}
                if name == "ah" and args[0] == 0:
                    pe.wait_ge(pads, 1)
                if name in made:
                    for t in ((args[-1],) if name == "qk" else range(NT)):
                        wait_freed(pe, (made[name], t))
                elif name == "h":
                    if args[1:] == (0, 0):
                        pe.wait_ge(relu_split, KC)
                elif name == "wo":
                    if args[1:] == (0, 0):
                        pe.wait_ge(relu_split, KC * (args[0] + 2))
                elif args == (0, 0):
                    pe.wait_ge(y_loaded, 32)

            for kind, name, args, n0, job in STEPS:
                b = begin(job) if job and name != "count" else 0
                if kind in "FT":
                    xh, xl = operands[name]
                    operand_ready(name, args)
                if kind == "F":
                    pe.wait_ge(w_lo_ready, n0 + 1)
                    f_product(b, [n0 % RING], KC, xh, xl).then_inc(filled[b // 512], 1)
                elif kind == "T":
                    if args[-1] == 0:
                        pe.wait_ge(w_lo_ready, n0 + 3)
                    t_product(b, n0, xh, xl, args[-1]).then_inc(filled[b // 512], 1)
                elif name == "agg":
                    j = args[0]
                    if j == 0:
                        for k in BEFORE_SUMS:
                            wait_freed(pe, k)
                    else:
                        pe.wait_ge(agg_freed, j)
                    pe.wait_ge(h_loaded[j % 2], 16 * (j // 2 + 1))
                    for i in range(NT):
                        pe.wait_ge(p_ready, NT * j + i + 1)
                        for d in range(NT):
                            ins = pe.matmul(ps[0:TT, AGG + 256 * d:AGG + 256 * d + GC + 1], prob[:, i, TT * d:TT * d + TT],
                                            h_tm[:, j % 2, i, :], start=(i == 0 and d % 2 == 0), stop=(i == NT - 1),
                                            skip_group_check=True)
                        ins.then_inc(p_used, 1)
                elif name == "edgesT":
                    pe.wait_ge(consts, 1)
                    pe.wait_ge(edges_f, 2)
                    for w in range(2):
                        for s in range(2):
                            ins = pe.transpose(ps[:, b + 96 * (2 * w + s):b + 96 * (2 * w + s) + EP],
                                               e_f[:, w, 128 * s:128 * s + 128], ident[0:EP, 0:EP])
                    ins.then_inc(filled[b // 512], 1)
                elif name == "bounds":
                    pe.wait_ge(edges_f, 4)
                    for w in range(2):
                        ins = pe.matmul(ps[0:5, b + 96 * w:b + 96 * w + EP], e_ends[0:EP, w:w + 1].to_broadcast([EP, 5]),
                                        ident[0:EP, 0:EP], start=True, stop=True)
                    ins.then_inc(filled[b // 512], 1)
                elif name == "biasT":
                    pe.wait_ge(c_loaded, 16 * 12)
                    pe.transpose(ps[:, b:b + 60], bias_row[:, :], ident[0:60, 0:60]).then_inc(filled[b // 512], 1)
                elif name == "chunk":
                    j, c = args
                    if c == 0:
                        b = begin(("count", j))
                        if j == 0:
                            pe.wait_ge(consts, 3)
                        for c0, w in ((0, 512), (512, N - 512)):
                            ins = pe.matmul(ps[0:TT, b + c0:b + c0 + w], wide[:, 500:500 + TT],
                                            wide[:, 500 - TT * j + c0:500 - TT * j + c0 + w], start=True, stop=False,
                                            skip_group_check=True)
                        ins.then_inc(oh_used[j], 2)
                    b = pb0(("count", j))
                    n = CHUNKS * j + c
                    for i in range(2 * PAIRS):
                        o = 2 * PAIRS * (n % 2) + i
                        pe.wait_ge(chunk_tile, 2 * PAIRS * n + i + 1)
                        for c0, w in ((0, 512), (512, N - 512)):
                            ins = pe.matmul(ps[0:TT, b + c0:b + c0 + w], oh_d[:, o, 0:TT], oh_s[:, o, c0:c0 + w],
                                            start=False, stop=False, skip_group_check=True)
                    ins.then_inc(chunk_used, 1)
                elif name == "count":
                    j, = args
                    b = pb0(job)
                    if j == 0:
                        pe.wait_ge(bounds_ready, 1)
                        trips += [pe.value_load(bounds[q:q + 1, 1:2], min_val=1, max_val=EP) for q in range(NT)]
                    with pe.Fori(0, trips[j]) as q:
                        for s in range(2):
                            pe.wait_ge(oh_ready[j], 2 * q + (s + 1))
                            for c0, w in ((0, 512), (512, N - 512)):
                                ins = pe.matmul(ps[0:TT, b + c0:b + c0 + w], oh2_d[:, s, 0:TT], oh2_s[:, s, c0:c0 + w],
                                                start=False, stop=False, skip_group_check=True)
                            ins.then_inc(oh_used[j], 1)
                    for c0, w in ((0, 512), (512, N - 512)):
                        ins = pe.matmul(ps[0:TT, b + c0:b + c0 + w], wide[:, 1000:1000 + TT], wide[:, 0:w],
                                        start=False, stop=True, skip_group_check=True)
                    ins.then_inc(filled[b // 512], 1)
                elif name == "countT":
                    j, = args
                    wait_freed(pe, ("count", j))
                    transposes(b, lambda i: count_ds[0:TT, TT * i:TT * i + TT], TT).then_inc(filled[b // 512], 1)
                elif name == "xnT":
                    t, = args
                    pe.wait_ge(consts, 1)
                    pe.wait_ge(ln_out, t + 1)
                    chunk_transposes(b, x_tm[:, t, :]).then_inc(filled[b // 512], 1)
                elif name == "asT":
                    pe.wait_ge(hs_summed, 2 * NT * L)
                    transposes(b, lambda t: asd[:, t, 0:NHD], NHD).then_inc(filled[b // 512], 1)
                elif name == "mzT":
                    layer = args[0]
                    pe.wait_ge(mz_ready, layer + 1)
                    transposes(b, lambda t: mz[:, layer, t, :], 2 * GH).then_inc(filled[b // 512], 1)
                elif name == "gT":
                    layer, pr, c = args
                    pe.wait_ge(agg_freed, layer * GH + 2 * pr + 2)
                    transposes(b, lambda d: g_tm[:, d, 128 * c:128 * c + 128]).then_inc(filled[b // 512], 1)
                elif name == "xT":
                    t, = args
                    pe.wait_ge(ln_out, NT + t + 1)
                    chunk_transposes(b, xl_tm[:, t, :]).then_inc(filled[b // 512], 1)
                elif name == "scores":
                    for u in range(2):
                        for g in range(2):
                            for t in range(NT):
                                wait_freed(pe, ("qk", u, g, t))
                    for hp in range(MH // 2):
                        for t in range(NT):
                            ins = pe.matmul(ps[:, b + 128 * hp:b + 128 * hp + 128], q_tm[:, t, 128 * hp:128 * hp + 128],
                                            k_tm[:, t, 128 * hp:128 * hp + 128], start=(t == 0), stop=(t == NT - 1))
                    ins.then_inc(filled[b // 512], 1)
                elif name == "wT":
                    pe.wait_ge(eblk_ready, 1)
                    for hp in range(MH // 2):
                        ins = pe.transpose(ps[:, b + 128 * hp:b + 128 * hp + 128], e_blk[:, hp, :], ident[:, :])
                    ins.then_inc(filled[b // 512], 1)
                elif name == "av":
                    hp = args[0]
                    wait_freed(pe, ("wT",))
                    wait_freed(pe, ("v", hp))
                    for o, c0 in ((2, 0), (512, TP - HT)):
                        ins = pe.matmul(ps[:, b + o:b + o + HT], w_t[:, hp, :], v_fm[:, hp, c0:c0 + HT],
                                        start=True, stop=True)
                    ins.then_inc(filled[b // 512], 1)
                elif name == "mT":
                    t, = args
                    pe.wait_ge(m_loaded[t], 32)
                    chunk_transposes(b, m_tm[:, t, :]).then_inc(filled[b // 512], 1)
                elif name == "expert_biasT":
                    for i in range(2):
                        pe.wait_ge(gl_in, i + 1)
                        pe.matmul(ps[:, MISC + i:MISC + i + 1], ones[:, :], gl[:, 2 * i:2 * i + 1], start=True, stop=True
                                  ).then_inc(gl_sum, 1)
                    pe.wait_ge(gate_in, 1)
                    for k in range(KC):
                        ins = pe.matmul(ps[0:1, MISC + 8:MISC + 16], y_mean[:, k:k + 1], r_w[:, k, :], start=(k == 0), stop=(k == KC - 1))
                    ins.then_inc(gate_mm, 1)
                    pe.wait_ge(gate_ready, 1)
                    pe.matmul(ps[:, MISC + 16:MISC + 18], ones[0:1, :], gate_row[0:1, 3 * NE:3 * NE + 2], start=True, stop=True
                              ).then_inc(gate_bc, 1)
                    pe.wait_ge(eb_loaded, 64)
                    pe.transpose(ps[:, b:b + 4 * QC], fcb_row[:, :], ident[0:4 * QC, 0:4 * QC])
                    pe.transpose(ps[:, b + 64:b + 64 + 2 * KC], pb_row[:, :], ident[0:2 * KC, 0:2 * KC]).then_inc(filled[b // 512], 1)

            for q in range(6):
                wait_freed(pe, PSUM.last[q])
            pe.wait_ge(y_split, KC)

            def quarter(it):
                n0 = MOE0 + 24 * it
                for c in range(QC):
                    p = c % 3
                    pe.wait_ge(w_lo_ready, n0 + (c + 1))
                    pe.wait_ge(freed[2 * p], MOE_USES[p] + 6 * it + c // 3)
                    f_product(1024 * p, [c % RING], KC, f0_hi, f0_lo).then_inc(filled[2 * p], 1)
                for fo in range(KC):
                    p = fo % 3
                    pe.wait_ge(w_lo_ready, n0 + (QC + 2 * fo + 2))
                    pe.wait_ge(freed[2 * p], MOE_USES[p] + 6 * it + (4 + fo // 3))
                    hidden = (lambda k: pe.wait_ge(g_lo, QC * it + (k + 4))) if fo == 0 else None
                    f_product(1024 * p, [(2 * fo) % RING, (2 * fo + 1) % RING], QC, hid_hi, hid_lo, wait_k=hidden
                              ).then_inc(filled[2 * p], 1)

            with pe.Fori(0, 4) as it:
                quarter(it)
            for i in range(2):
                pe.wait_ge(gl_in, i + 3)
                pe.matmul(ps[:, MISC + i:MISC + i + 1], ones[:, :], gl[:, 2 * i:2 * i + 1], start=True, stop=True
                          ).then_inc(gl_sum, 1)
            pe.wait_ge(fin_ready, KC)
            for t in range(NT):
                p = t % 3
                pe.wait_ge(freed[2 * p], MOE_USES[p] + 24 + t // 3)
                for c in range(KC):
                    ins = pe.transpose(ps[0:TT, 1024 * p + 128 * c:1024 * p + 128 * c + 128], z_fm[:, c, TT * t:TT * t + TT], ident[:, :])
                ins.then_inc(filled[2 * p], 1)

        @block.scalar
        def _(act):
            chain = Chain(act, act_done)
            full = E // 256
            act.wait_ge(e_pad, 1)
            for i, name in enumerate(("src", "dst")):
                act.dma_start(e_int[0:full, i, :], a[name][0:full * 256].rearrange("(p n) -> p n", n=256)).then_inc(e_loaded, 16)
                act.dma_start(e_int[full:EP, i, 0:E - full * 256],
                               a[name][full * 256:E].rearrange("(a n) -> a n", a=1)).then_inc(e_loaded, 16)
            row = 0
            for name, sub in (("L0_gnn_b_ah", None), ("L0_gnn_b0", None), ("L0_gnn_b1", None), ("L0_gnn_b2", None),
                              ("L0_ffn_W1_b", slice(2 * D, 3 * D)), ("L0_ffn_W2_b", None), ("L0_ffn_ln1_w", None),
                              ("L0_ffn_ln1_b", None), ("L0_ffn_ln2_w", None), ("L0_ffn_ln2_b", None)):
                src = a[name] if sub is None else a[name][sub]
                act.dma_start(bias_row[row:row + KC, :], src.rearrange("(k p) -> k p", p=128)).then_inc(c_loaded, 16)
                row += KC
            act.dma_start(r_w[:, :, :], a["L0_ffn_r_w"].rearrange("(k p) n -> p k n", p=128)).then_inc(c_loaded, 16)
            act.dma_start(r_b[:, :], a["L0_ffn_r_b"].rearrange("(a n) -> a n", a=1)).then_inc(c_loaded, 16)
            split = [0]

            def pump(c, end=MOE0):
                while split[0] < min(c + RING, end):
                    n = split[0]
                    act.wait_ge(w_landed[n % RAW], 16 * (n // RAW + 1))
                    slot_free(act, n)
                    act.activation(w_hi[:, n % RING, :], w_raw[:, n % RAW, :], ACT.Copy).then_inc(w_hi_ready, 1)
                    split[0] += 1

            def free(ins, key):
                ins.then_inc(freed[PSUM.at[key][0]], 1)

            sm_steps = [0]

            def softmax_step():
                g = sm_steps[0]
                sm_steps[0] += 1
                if g < NT * NHD:
                    j, i = divmod(g, NT)
                    if g == 0:
                        act.wait_ge(as_scaled, 1)
                    if i == 0:
                        act.wait_ge(rows_loaded[j % 2], 32 * (j // 2 + 1))
                    if g >= NT:
                        act.wait_ge(p_used, g - NT + 1)
                    act.activation(prob[:, i, :], rows[0:TT, j % 2, 1, :], ACT.Identity, bias=as02[:, i, j:j + 1]
                                   ).then_inc(sm_low, 1)
                if g:
                    act.wait_ge(sm_max, g)
                    act.activation(prob[:, (g - 1) % NT, :], prob[:, (g - 1) % NT, :], ACT.Exp).then_inc(sm_exp, 1)

            def normalize(n, src, dst):
                t = n % NT
                act.wait_ge(nmr_ready, n + 1)
                act.activation(dst[:, t, :], src[:, t, :], ACT.Identity, bias=neg_mr[0:TT, t:t + 1],
                               scale=rstd[0:TT, t:t + 1]).then_inc(ln_out, 1)

            def chunks_of(b):
                return ps[:, b + 12:b + 12 + TT * KC].rearrange("p (k n) -> p k n", k=KC)

            def relu_parts(hi, src, bias, key):
                n = relus[0]
                relus[0] += 1
                if n >= 2:
                    act.wait_ge(relu_split, n - 1)
                t = relu_t[:, n % 2, :]
                t = two(t) if len(src.shape) == 3 else t[:, 0:N]
                free(act.activation(t, src, ACT.Relu, bias=bias), key)
                wait_freed(act, key)
                act.activation(hi, t, ACT.Copy).then_inc(hi_first, 1)

            relus = [0]
            hs = 0
            for si, (kind, name, args, n0, job) in enumerate(STEPS):
                for _ in range(SOFT[si]):
                    softmax_step()
                if kind in "FT":
                    pump(n0)
                b = pb0(job) if job else 0
                if name == "edgesT":
                    pump(RAW - RING)
                elif name == "bounds":
                    normalize(0, x_tm, x_tm)
                elif name == "biasT":
                    pump(0)
                elif name == "count":
                    j, = args
                    wait_filled(act, job)
                    if j:
                        wait_filled(act, ("countT", j - 1))
                        act.wait_ge(mask_ready, j)
                    free(act.activation(count_ds[0:TT, :], ps[0:TT, b:b + N], ACT.Copy), job)
                elif name == "countT":
                    j, = args
                    wait_filled(act, job)
                    free(act.activation(count[:, :, TT * j:TT * j + TT],
                                        tsp(b, TT).rearrange("p (i d) -> p i d", i=NT), ACT.Copy), job)
                elif name in ("xnT", "xT", "mT"):
                    t, = args
                    if name == "xnT" and t + 1 < NT:
                        normalize(t + 1, x_tm, x_tm)
                    dst = f1_hi if name == "mT" else f0_hi
                    wait_filled(act, job)
                    act.activation(dst[:, :, TT * t:TT * t + TT], chunks_of(b), ACT.Copy).then_inc(hi_first, 1)
                elif name == "ah":
                    fo, = args
                    wait_filled(act, job)
                    wait_freed(act, ("biasT",))
                    relu_parts(two(f1_hi[:, fo, :]), halves(b), bias_col[:, fo:fo + 1], job)
                elif name == "h":
                    i = hs
                    hs += 1
                    if i >= 3:
                        act.wait_ge(hs_stored[i % 3], 16 * (i // 3))
                        act.wait_ge(hs_summed, i - 2)
                    wait_filled(act, job)
                    free(act.activation(h_st[:, i % 3, :, 0:GC], ps[0:TT, b:b + 384].rearrange("p (h c) -> p h c", h=2), ACT.Copy), job)
                elif name in ("asT", "mzT"):
                    i = 0 if name == "asT" else args[0] + 1
                    wait_filled(act, job)
                    if i:
                        act.wait_ge(row_stored, 16 * i)
                    r = NHD if name == "asT" else 2 * GH
                    free(act.activation(row_t[0:r, :], tsp(b, r), ACT.Copy), job)
                elif name == "mix":
                    f, part = args
                    if part < 2:
                        dst = (q_fm, k_fm)[part]
                        wait_filled(act, job)
                        if f:
                            act.wait_ge(y_ready, f)
                        elif part == 0:
                            for q in hs_stored:
                                act.wait_ge(q, 16 * (2 * NT * L // 3))
                            act.wait_ge(hs_summed, 2 * NT * L)
                        v = halves(b)
                        chain.link(act.activation(two(dst[:, :]), v, ACT.Identity, accum_out=mix_sum[:, 2 * part:2 * part + 1]))
                        free(act.activation(v, v, ACT.Square, accum_out=mix_sum[:, 2 * part + 1:2 * part + 2]), job)
                elif name == "gT":
                    layer, pr, c = args
                    k = 3 * pr + c
                    wait_filled(act, job)
                    if k == 0 and layer:
                        wait_filled(act, ("wo", layer - 1, 1, NT - 1))
                    k0 = KC * (1 + layer) + k
                    relu_parts(f1_hi[:, k, 0:N], tsp(b), bias_col[:, k0:k0 + 1], job)
                elif name == "agg":
                    j = args[0]
                    act.wait_ge(rden_ready, j + 1)
                    if j % 2 == 0 and j:
                        wait_filled(act, ("gT", (j - 1) // GH, ((j - 1) % GH) // 2, 2))
                    for d in range(NT):
                        ins = act.activation(g_tm[:, d, GC * (j % 2):GC * (j % 2) + GC], ps[0:TT, AGG + 256 * d:AGG + 256 * d + GC],
                                             ACT.Copy, scale=rden[:, d:d + 1])
                    ins.then_inc(agg_freed, 1)
                elif name == "proj" and args[0] == 1:
                    normalize(NT + args[1], x2, xl_tm)
                elif name == "v":
                    fo, = args
                    wait_filled(act, job)
                    free(act.activation(two(v_fm[:, fo, :]), halves(b), ACT.Identity, bias=bias_col[:, 24 + fo:25 + fo]), job)
                elif name == "scores":
                    act.wait_ge(sc_sub, 2)
                    act.wait_ge(xr_ready, NT + 1)
                    for s in range(2):
                        r = slice(64 * s, 64 * s + 64)
                        act.activation(e_blk[r, :, r], w_t[r, :, r], ACT.Exp, scale=1.0 / float(N) ** 0.5).then_inc(sc_exp, 1)
                elif name == "av":
                    hp, = args
                    wait_filled(act, job)
                    if hp >= 2:
                        act.wait_ge(o_stored[hp % 2], 16 * (hp // 2))
                    free(act.activation(two(o_fm[:, hp % 2, :]), halves(b), ACT.Copy), job)
                elif name == "expert_biasT":
                    act.wait_ge(gl_ready, 1)
                    for k in range(KC):
                        act.activation(z_fm[:, k, 0:N], z_fm[:, k, 0:N], ACT.Identity, bias=ln_bias[:, k:k + 1],
                                       scale=ln_scale[:, k:k + 1]).then_inc(y_fm_ready, 1)
                        if k == 1:
                            act.wait_ge(gate_e_in, 1)
                            act.activation(gate_row[0:1, NE:2 * NE], gate_row[0:1, 0:NE], ACT.Exp).then_inc(gate_e, 1)
                    pump(MOE0, MOE0 + RING)

            act.wait_ge(eb_ready, 1)

            def split_hi(it, k):
                act.wait_ge(w_landed[k % RAW], 16 * (MOE0 // RAW + 1) + 128 * it + 16 * (k // RAW))
                act.wait_ge(*moe_reader(it, k - RING))
                act.activation(w_hi[:, k % RING, :], w_raw[:, k % RAW, :], ACT.Copy).then_inc(w_hi_ready, 1)

            def moe_reader(it, k):
                i = k if k < QC else QC + (k - QC) // 2
                return filled[2 * (i % 3)], MOE_USES[i % 3] + 6 * it + (i // 3 + 1)

            def quarter(it, last):
                for c in range(QC + 2):
                    if c < QC:
                        if c:
                            split_hi(it, c + RING - 1)
                        p = c % 3
                        act.wait_ge(filled[2 * p], MOE_USES[p] + 6 * it + (c // 3 + 1))
                        act.wait_ge(g_lo, QC * it + (c + 1))
                        b = fcb[:, bass.ds(QC * it + c, 1)]
                        v = halves(1024 * p)
                        act.activation(two(gel_x[:, c % 3, :]), v, ACT.Identity, bias=b)
                        act.activation(two(gel_u[:, c % 3, :]), v, ACT.Square, bias=b).then_inc(freed[2 * p], 1)
                    if 1 <= c <= QC:
                        act.wait_ge(g_w, QC * it + c)
                        act.activation(gel_u[:, (c - 1) % 3, :], gel_u[:, (c - 1) % 3, :], ACT.Tanh, scale=GELU_C).then_inc(g_th, 1)
                    if c >= 2:
                        act.wait_ge(g_q, QC * it + (c - 1))
                        act.activation(hid_hi[:, c - 2, :], gel_u[:, (c - 2) % 3, :], ACT.Copy, scale=0.5).then_inc(g_hi, 1)
                split_hi(it, QC + RING - 1)
                for fo in range(KC):
                    ks = [QC + 2 * fo + RING, QC + 2 * fo + RING + 1]
                    for k in ks:
                        if k < 24 or not last:
                            if k < 24 + RING:
                                split_hi(it, k)

            with act.Fori(0, 3) as it:
                quarter(it, False)
            quarter(3, True)
            act.wait_ge(gl_ready, 2)
            for k in range(KC):
                act.activation(z_fm[:, k, 0:N], z_fm[:, k, 0:N], ACT.Identity, bias=ln_bias[:, k:k + 1],
                               scale=ln_scale[:, k:k + 1]).then_inc(fin_ready, 1)

        @block.vector
        def _(dve):
            chain = Chain(dve, dve_done)
            split = [0]

            def split_lo(n_slot, n_raw):
                return dve.tensor_tensor(w_lo[:, n_slot, :], w_raw[:, n_raw, :], w_hi[:, n_slot, :].bitcast(F32), ALU.subtract)

            def pump(c, end=MOE0):
                while split[0] < min(c + RING, end):
                    n = split[0]
                    dve.wait_ge(w_hi_ready, n + 1)
                    split_lo(n % RING, n % RAW).then_inc(w_lo_ready, 1)
                    split[0] += 1

            def free(ins, key):
                ins.then_inc(freed[PSUM.at[key][0]], 1)

            def ln_mr(n):
                t = n % NT
                dve.wait_ge(rstd_ready, n + 1)
                dve.scalar_tensor_tensor(out=neg_mr[0:TT, t:t + 1], in0=mv[0:TT, t, 0:1], scalar=-1.0, in1=rstd[0:TT, t:t + 1],
                                         op0=ALU.mult, op1=ALU.mult).then_inc(nmr_ready, 1)

            def ln_tile(n, src):
                t = n % NT
                for g in range(2):
                    ins = dve.bn_stats(stats[0:TT, 2 * t + g, :], src[:, t, 384 * g:384 * g + 384])
                ins.then_inc(ln_stats, 1)
                dve.wait_ge(ln_stats, n + 1)
                dve.bn_aggr(mv[0:TT, t, :], stats[0:TT, 2 * t:2 * t + 2, :]).then_inc(ln_mv, 1)
                dve.wait_ge(ln_mv, n + 1)
                dve.tensor_scalar(var_eps[0:TT, t:t + 1], mv[0:TT, t, 1:2], LN_EPS, None, ALU.add).then_inc(var_ready, 1)

            def chunk_stats(k):
                for g, (c0, c1) in enumerate(((0, 313), (313, N))):
                    ins = dve.bn_stats(stats[:, 2 * k + g, :], z_fm[:, k, c0:c1])
                return ins

            def global_stats(i):
                dve.bn_aggr(gl[:, 0:2], stats[:, :, :]).then_inc(gl_in, 1)
                dve.wait_ge(gl_sum, 2 * i + 1)
                chain.link(dve.tensor_scalar(gl[:, 3:4], ps[:, MISC:MISC + 1], -1.0 / 128, None, ALU.mult))
                chain.link(dve.tensor_tensor(gl[:, 6:7], gl[:, 0:1], gl[:, 3:4], ALU.add))
                dve.scalar_tensor_tensor(out=gl[:, 2:3], in0=gl[:, 6:7], scalar=gl[:, 6:7], in1=gl[:, 1:2],
                                         op0=ALU.mult, op1=ALU.add).then_inc(gl_in, 1)
                dve.wait_ge(gl_sum, 2 * i + 2)
                dve.tensor_scalar(gl[:, 4:5], ps[:, MISC + 1:MISC + 2], float(KC * N) / (N * D - 1), GLN_EPS, ALU.mult,
                                  ALU.add).then_inc(gl_var, 1)
                dve.wait_ge(gl_rstd, i + 1)
                w0 = 36 + 12 * i
                chain.link(dve.tensor_scalar(ln_scale[:, :], bias_col[:, w0:w0 + KC], gl[:, 5:6], None, ALU.mult))
                dve.scalar_tensor_tensor(out=ln_bias[:, :], in0=ln_scale[:, :], scalar=gl[:, 3:4],
                                         in1=bias_col[:, w0 + KC:w0 + 2 * KC], op0=ALU.mult, op1=ALU.add).then_inc(gl_ready, 1)

            sm_steps = [0]

            def softmax_step():
                g = sm_steps[0]
                sm_steps[0] += 1
                if g < NT * NHD:
                    j, i = divmod(g, NT)
                    dve.wait_ge(sm_low, g + 1)
                    dve.scalar_tensor_tensor(out=prob[:, i, :], in0=rows[0:TT, j % 2, 0, :], scalar=asd[:, i, j:j + 1],
                                             in1=prob[:, i, :], op0=ALU.add, op1=ALU.max).then_inc(sm_max, 1)
                if g:
                    i = (g - 1) % NT
                    dve.wait_ge(sm_exp, g)
                    dve.scalar_tensor_tensor(out=prob[:, i, :], in0=prob[:, i, :], scalar=1.0, in1=count[:, i, :],
                                             op0=ALU.min, op1=ALU.mult).then_inc(p_ready, 1)

            def head_max(j):
                layer, h = divmod(j, GH)
                dve.wait_ge(asrow_loaded[j % 2], 16 * (j // 2 + 1))
                for d in range(NT):
                    if NT * j + d >= 2:
                        dve.wait_ge(head_maxed, NT * j + d - 1)
                    dve.tensor_tensor_reduce(out=junk[:, (NT * j + d) % 2, :], in0=mask[:, d, :], in1=as_row[0:TT, j % 2, :], scale=1.0,
                                             scalar=NEG, op0=ALU.add, op1=ALU.max, accum_out=mx[:, d, h:h + 1]
                                             ).then_inc(head_maxed, 1)
                if h == GH - 1:
                    dve.wait_ge(head_maxed, NT * (j + 1))
                    ad = asd[:, :, NHD + GH * layer:NHD + GH * layer + GH]
                    chain.link(dve.tensor_tensor(z_tmp[:, :, :], mx[:, :, :], ad, ALU.add))
                    chain.link(dve.scalar_tensor_tensor(out=m_tmp[:, :, :], in0=z_tmp[:, :, :], scalar=0.2,
                                                        in1=z_tmp[:, :, :], op0=ALU.mult, op1=ALU.max))
                    dve.tensor_tensor(mz[:, layer, :, 0:GH], ad, m_tmp[:, :, :], ALU.subtract)
                    dve.scalar_tensor_tensor(out=mz[:, layer, :, GH:2 * GH], in0=ad, scalar=0.2, in1=m_tmp[:, :, :],
                                             op0=ALU.mult, op1=ALU.subtract).then_inc(mz_ready, 1)

            def lo_part(dst, hi, src, key):
                dve.wait_ge(hi_first, hf[0] + 1)
                hf[0] += 1
                free(dve.tensor_tensor(dst, src, hi.bitcast(F32), ALU.subtract), key)

            def relu_lo_part(lo, hi, n):
                dve.wait_ge(hi_first, hf[0] + 1)
                hf[0] += 1
                dve.tensor_tensor(lo, relu_t[:, n % 2, 0:lo.shape[-1]], hi.bitcast(F32), ALU.subtract).then_inc(relu_split, 1)

            def make_chunk(n):
                j, c = divmod(n, CHUNKS)
                if n >= 2:
                    dve.wait_ge(chunk_used, n - 1)
                for i in range(2 * PAIRS):
                    o = 2 * PAIRS * (n % 2) + i
                    e = bass.ds(first[j][0] + (PAIRS * c + i // 2), 1)
                    dve.tensor_scalar(oh_s[:, o, :], iota[:, :], e_col[:, 0, i % 2, e], None, ALU.is_equal)
                    dve.tensor_scalar(oh_d[:, o, 0:TT], iota[:, TT * j:TT * j + TT], e_col[:, 1, i % 2, e], None,
                                      ALU.is_equal).then_inc(chunk_tile, 1)

            def mask_of(j):
                wait_freed(dve, ("count", j))
                dve.tensor_scalar(mask[:, j, :], count_ds[0:TT, :], 0.0, NEG, ALU.is_equal, ALU.mult).then_inc(mask_ready, 1)

            def chunks_of(b):
                return ps[:, b + 12:b + 12 + TT * KC].rearrange("p (k n) -> p k n", k=KC)

            hf, hs, first = [0], 0, []
            dve.wait_ge(e_loaded, 64)
            for w in range(2):
                dve.tensor_copy(e_f[:, w, :], e_int[:, w, :]).then_inc(edges_f, 1)
            dve.wait_ge(edges_f, 2)
            for i, op in enumerate((ALU.min, ALU.max)):
                dve.tensor_reduce(e_ends[0:EP, i:i + 1], e_f[:, 1, :], AX_X, op).then_inc(edges_f, 1)
            dve.wait_ge(consts, 3)
            dve.tensor_copy(iota[:, :], iota_f[:, :])
            for si, (kind, name, args, n0, job) in enumerate(STEPS):
                for _ in range(SOFT[si]):
                    softmax_step()
                if kind in "FT":
                    pump(n0)
                b = pb0(job) if job else 0
                if name == "edgesT":
                    wait_filled(dve, job)
                    dve.wait_ge(e_col_set, 1)
                    v = ps[:, b:b + 4 * 96].rearrange("p (w s q) -> p (w s) q", w=2, s=2)[:, :, 0:EP]
                    free(dve.tensor_copy(e_col[:, :, :, 0:EP].rearrange("p w s q -> p (w s) q"), v), job)
                    for t in range(2):
                        dve.wait_ge(x_loaded[t], 32)
                        ln_tile(t, x_tm)
                        if t:
                            ln_mr(t - 1)
                elif name == "bounds":
                    wait_filled(dve, job)
                    lo, hi = ps[0:5, b:b + EP], ps[0:5, b + 96:b + 96 + EP]
                    meets = e_lo5[:, 1, 0:EP]
                    dve.wait_ge(consts, 2)
                    chain.link(dve.tensor_scalar(bsm[:, 1:2], bsm[:, 0:1], float(TT), None, ALU.add))
                    chain.link(dve.tensor_scalar(e_lo5[:, 0, 0:EP], lo, bsm[:, 1:2], None, ALU.is_lt))
                    free(dve.scalar_tensor_tensor(out=meets, in0=hi, scalar=bsm[:, 0:1], in1=e_lo5[:, 0, 0:EP],
                                                  op0=ALU.is_ge, op1=ALU.mult), job)
                    wait_freed(dve, job)
                    for i, (shift, op) in enumerate(((-128.0, ALU.min), (1.0, ALU.max))):
                        chain.link(dve.scalar_tensor_tensor(out=e_lo5[:, 2 + i, 0:EP], in0=iota_f[0:5, 0:EP], scalar=shift,
                                                            in1=meets, op0=ALU.add, op1=ALU.mult))
                        chain.link(dve.tensor_reduce(bsm[:, 2 + i:3 + i], e_lo5[:, 2 + i, 0:EP], AX_X, op))
                    chain.link(dve.tensor_scalar(bsm[:, 4:5], bsm[:, 2:3], 128.0, float(EP - 1), ALU.add, ALU.min))
                    chain.link(dve.tensor_tensor(bsm[:, 5:6], bsm[:, 3:4], bsm[:, 4:5], ALU.subtract))
                    chain.link(dve.tensor_scalar(bsm[:, 5:6], bsm[:, 5:6], float(-SPAN), 1.0, ALU.add, ALU.max))
                    dve.tensor_copy(bounds[:, :], bsm[:, 4:6]).then_inc(bounds_ready, 1)
                    ln_mr(1)
                    for t in range(2, NT):
                        dve.wait_ge(x_loaded[t], 32)
                        ln_tile(t, x_tm)
                        if t > 2:
                            ln_mr(t - 1)
                    ln_mr(NT - 1)
                    dve.wait_ge(bounds_ready, 1)
                    first += [(dve.value_load(bounds[q:q + 1, 0:1], min_val=0, max_val=EP - 1),
                               dve.value_load(bounds[q:q + 1, 1:2], min_val=1, max_val=EP)) for q in range(NT)]
                    pump(RAW - RING)
                elif name == "biasT":
                    wait_filled(dve, job)
                    free(dve.tensor_copy(bias_col[:, :], ps[:, b:b + 60]), job)
                    make_chunk(0)
                    pump(0)
                elif name == "chunk":
                    n = CHUNKS * args[0] + args[1] + 1
                    if n < CHUNKS * NT:
                        make_chunk(n)
                elif name == "count":
                    j, = args
                    start, trips = first[j]
                    with dve.Fori(0, trips) as q:
                        for s in range(2):
                            dve.wait_ge(oh_used[j], 2 * q + (s + 1))
                            e = bass.ds(start + q + SPAN, 1)
                            dve.tensor_scalar(oh2_s[:, s, :], iota[:, :], e_col[:, 0, s, e], None, ALU.is_equal)
                            dve.tensor_scalar(oh2_d[:, s, 0:TT], iota[:, TT * j:TT * j + TT], e_col[:, 1, s, e], None,
                                              ALU.is_equal).then_inc(oh_ready[j], 1)
                elif name == "countT":
                    mask_of(args[0])
                elif name in ("xnT", "xT", "mT"):
                    t, = args
                    if name == "xT" and t + 2 < NT:
                        ln_mr(NT + t + 2)
                    hi, lo = (f1_hi, f1_lo) if name == "mT" else (f0_hi, f0_lo)
                    c = slice(TT * t, TT * t + TT)
                    lo_part(lo[:, :, c], hi[:, :, c], chunks_of(b), job)
                elif name == "ah":
                    fo, = args
                    relu_lo_part(f1_lo[:, fo, :], f1_hi[:, fo, :], fo)
                elif name == "gT":
                    layer, pr, c = args
                    k = 3 * pr + c
                    relu_lo_part(f1_lo[:, k, 0:N], f1_hi[:, k, 0:N], KC * (1 + layer) + k)
                elif name == "h":
                    layer, g, t = args
                    i = hs
                    hs += 1
                    if g == 0 and t == 0:
                        dve.wait_ge(a_loaded[layer % 2], 32 * (layer // 2 + 1))
                    wait_freed(dve, job)
                    if i:
                        dve.wait_ge(hs_summed, i)
                    for w in range(2):
                        for h in range(2):
                            hd = 2 * g + h
                            ins = dve.tensor_tensor_reduce(out=junk1[:, 2 * w + h, :], in0=h_st[:, i % 3, h, 0:GC],
                                                           in1=a_bc[:, layer % 2, w, GC * hd:GC * hd + GC], scale=1.0, scalar=0.0,
                                                           op0=ALU.mult, op1=ALU.add,
                                                           accum_out=asd[:, t, NHD * w + GH * layer + hd:NHD * w + GH * layer + hd + 1])
                    ins.then_inc(hs_summed, 1)
                elif name == "asT":
                    dve.wait_ge(hs_summed, 2 * NT * L)
                    dve.tensor_scalar(as02[:, :, :], asd[:, :, 0:NHD], 0.2, None, ALU.mult).then_inc(as_scaled, 1)
                elif name == "mix":
                    f, part = args
                    if f == 0 and part == 0:
                        dve.wait_ge(mask_ready, NT)
                        wait_filled(dve, ("countT", NT - 1))
                    if f == 0 and part < 2:
                        head_max(2 * part)
                        head_max(2 * part + 1)
                    if part == 2:
                        dve.wait_ge(mix_rr, f + 1)
                        chain.link(dve.tensor_tensor(mix_t[:, 0:2], mix_sum[:, 0:4:2], mix_r[:, :], ALU.mult))
                        chain.link(dve.tensor_tensor(mix_t[:, 2:3], mix_t[:, 0:1], mix_t[:, 1:2], ALU.mult))
                        chain.link(dve.tensor_scalar(mix_t[:, 3:4], mix_t[:, 2:3], float(N), None, ALU.add))
                        chain.link(dve.reciprocal(mix_t[:, 4:5], mix_t[:, 3:4]))
                        chain.link(dve.scalar_tensor_tensor(out=mix_t[:, 5:6], in0=mix_r[:, 0:1], scalar=mix_r[:, 1:2],
                                                            in1=mix_t[:, 4:5], op0=ALU.mult, op1=ALU.mult))
                        chain.link(dve.scalar_tensor_tensor(out=t_fm[:, :], in0=q_fm[:, :], scalar=mix_t[:, 5:6], in1=k_fm[:, :],
                                                            op0=ALU.mult, op1=ALU.mult))
                        wait_filled(dve, job)
                        free(dve.scalar_tensor_tensor(out=two(k_fm[:, :]), in0=two(k_fm[:, :]), scalar=mix_r[:, 1:2],
                                                      in1=halves(b), op0=ALU.mult, op1=ALU.mult), job)
                        wait_freed(dve, job)
                        chain.link(dve.tensor_tensor(t_fm[:, :], t_fm[:, :], k_fm[:, :], ALU.mult))
                        if f:
                            dve.wait_ge(y_stored, 32 * f)
                        chain.link(dve.tensor_copy(y_hi[:, :], t_fm[:, :]))
                        dve.tensor_tensor(y_lo[:, :], t_fm[:, :], y_hi[:, :].bitcast(F32), ALU.subtract).then_inc(y_ready, 1)
                elif name == "agg":
                    j = args[0]
                    dve.wait_ge(p_used, NT * (j + 1))
                    chain.link(dve.tensor_scalar(den[:, :], ps[0:TT, AGG:AGG + 256 * NT].rearrange("p (d c) -> p d c", d=NT)[:, :, GC],
                                                 1e-16, None, ALU.add))
                    dve.reciprocal(rden[:, :], den[:, :]).then_inc(rden_ready, 1)
                    for nxt in MAX_AT.get(j, ()):
                        head_max(nxt)
                elif name == "wo":
                    layer, g, t = args
                    c = slice(384 * g, 384 * g + 384)
                    wait_filled(dve, job)
                    if layer == 0:
                        dve.wait_ge(gacc_set, 16 * NT)
                    free(dve.tensor_tensor(gacc[:, t, c], gacc[:, t, c], ps[0:TT, b:b + 384], ALU.add), job)
                elif name == "proj":
                    g, t = args
                    c = slice(384 * g, 384 * g + 384)
                    dve.wait_ge(xr_ready, t + 1)
                    wait_freed(dve, ("wo", L - 1, g, t))
                    chain.link(dve.scalar_tensor_tensor(out=x2[:, t, c], in0=gacc[:, t, c], scalar=0.0, in1=xr[:, t, c],
                                                        op0=ALU.max, op1=ALU.add))
                    wait_filled(dve, job)
                    free(dve.tensor_tensor(x2[:, t, c], x2[:, t, c], ps[0:TT, b:b + 384], ALU.add), job)
                    if g == 1:
                        if t in (1, 2):
                            ln_mr(NT + t - 1)
                        wait_freed(dve, ("proj", 0, t))
                        wait_freed(dve, job)
                        ln_tile(NT + t, x2)
                elif name == "qk":
                    u, g, t = args
                    wait_filled(dve, job)
                    if args == (0, 0, 0):
                        dve.wait_ge(late_loaded, 16)
                        dve.memset(z_fm[:, :, N:TP], 0.0)
                    free(dve.tensor_tensor((q_tm, k_tm)[u][:, t, 384 * g:384 * g + 384], ps[0:TT, b:b + 384],
                                           qk_b[:, D * u + 384 * g:D * u + 384 * g + 384], ALU.add), job)
                elif name == "scores":
                    wait_filled(dve, job)
                    for s in range(2):
                        r = slice(64 * s, 64 * s + 64)
                        v = ps[r, b:b + 128 * KC].rearrange("p (k c) -> p k c", k=KC)[:, :, 64 * s:64 * s + 64]
                        chain.link(dve.tensor_reduce(sm[r, 0:KC], v, AX_X, ALU.max))
                        ins = dve.tensor_tensor(w_t[r, :, r], v, sm[r, 0:KC].to_broadcast([64, KC, 64]), ALU.subtract)
                        ins.then_inc(sc_sub, 1)
                    dve.wait_ge(sc_exp, 2)
                    chain.link(dve.tensor_reduce(sm[:, KC:2 * KC], e_blk[:, :, :], AX_X, ALU.add))
                    chain.link(dve.reciprocal(sm[:, 2 * KC:3 * KC], sm[:, KC:2 * KC]))
                    dve.tensor_tensor(e_blk[:, :, :], e_blk[:, :, :], sm[:, 2 * KC:3 * KC].to_broadcast([128, KC, 128]),
                                      ALU.mult).then_inc(eblk_ready, 1)
                    free(dve.memset(sm[:, 3 * KC:3 * KC + 1], 0.0), job)
                elif name == "wT":
                    wait_filled(dve, job)
                    free(dve.tensor_copy(w_t[:, :, :].rearrange("p k c -> p (k c)"), ps[:, b:b + 128 * KC]), job)
                elif name == "w2":
                    fo, = args
                    wait_filled(dve, job)
                    dve.wait_ge(z_set, fo + 1)
                    v = two(z_fm[:, fo, :])
                    free(dve.scalar_tensor_tensor(out=v, in0=halves(b), scalar=bias_col[:, 30 + fo:31 + fo], in1=v,
                                                  op0=ALU.add, op1=ALU.add), job)
                    wait_freed(dve, job)
                    chain.link(chunk_stats(fo))
                    ins = dve.bn_aggr(z_mv[:, fo, :], stats[:, 2 * fo:2 * fo + 2, :])
                    if fo == KC - 1:
                        chain.link(ins)
                        global_stats(0)
                elif name == "expert_biasT":
                    gr = lambda i, n=NE: gate_row[0:1, i:i + n]

                    def split_y(k):
                        dve.wait_ge(y_fm_ready, k + 1)
                        chain.link(dve.tensor_copy(f0_hi[:, k, 0:N], z_fm[:, k, 0:N]))
                        dve.tensor_tensor(f0_lo[:, k, 0:N], z_fm[:, k, 0:N], f0_hi[:, k, 0:N].bitcast(F32), ALU.subtract
                                          ).then_inc(y_split, 1)

                    dve.wait_ge(gl_ready, 1)
                    chain.link(dve.tensor_tensor(y_mean[:, :], z_mv[:, :, 0], ln_scale[:, :], ALU.mult))
                    dve.tensor_tensor(y_mean[:, :], y_mean[:, :], ln_bias[:, :], ALU.add).then_inc(gate_in, 1)
                    split_y(0)
                    dve.wait_ge(gate_mm, 1)
                    chain.link(dve.tensor_tensor(gr(40), ps[0:1, MISC + 8:MISC + 16], r_b[:, :], ALU.add))
                    chain.link(dve.tensor_reduce(gr(32, 1), gr(40), AX_X, ALU.max))
                    dve.tensor_scalar(gr(0), gr(40), gr(32, 1), None, ALU.subtract).then_inc(gate_e_in, 1)
                    split_y(1)
                    dve.wait_ge(gate_e, 1)
                    chain.link(dve.tensor_reduce(gr(33, 1), gr(8), AX_X, ALU.add))
                    chain.link(dve.reciprocal(gr(34, 1), gr(33, 1)))
                    chain.link(dve.tensor_scalar(gr(16), gr(8), gr(34, 1), None, ALU.mult))
                    chain.link(dve.max(gr(24), gr(16)))
                    dve.max_index(gate_idx[:, :], gr(24), gr(16)).then_inc(gate_ready, 1)
                    for k in range(2, KC):
                        split_y(k)
                    pump(MOE0, MOE0 + RING)
                    dve.wait_ge(gate_bc, 1)
                    for i in range(2):
                        chain.link(dve.tensor_copy(gate_col[:, i:4:2], ps[:, MISC + 16:MISC + 18]))
                    wait_filled(dve, job)
                    dve.tensor_copy(fcb[:, :], ps[:, b:b + 4 * QC]).then_inc(eb_ready, 1)
                    free(dve.tensor_copy(pb[:, :], ps[:, b + 64:b + 64 + 2 * KC]), job)
                    wait_freed(dve, job)
                    chain.link(dve.tensor_scalar(ln_scale[:, :], pb[:, 0:KC], gate_col[:, 0:1], None, ALU.mult))
                    chain.link(dve.scalar_tensor_tensor(out=ln_bias[:, :], in0=pb[:, KC:2 * KC], scalar=gate_col[:, 2:3],
                                                        in1=ln_scale[:, :], op0=ALU.mult, op1=ALU.add))
                    for k in range(KC):
                        ins = dve.tensor_scalar(z_fm[:, k, :], z_fm[:, k, :], ln_bias[:, k:k + 1], None, ALU.add)
                    chain.link(ins)
                    dve.memset(gl[:, 8:9], 0.0).then_inc(g_lo, 3)

            def lo_piece(it, k):
                dve.wait_ge(w_hi_ready, MOE0 + 24 * it + (k + 1))
                split_lo(k % RING, k % RAW).then_inc(w_lo_ready, 1)

            def quarter(it, last):
                ins = None
                for c in range(QC + 2):
                    if c < QC:
                        if c:
                            lo_piece(it, c + RING - 1)
                        x, u = gel_x[:, c % 3, :], gel_u[:, c % 3, :]
                        dve.wait_ge(freed[2 * (c % 3)], MOE_USES[c % 3] + 6 * it + (c // 3 + 1))
                        dve.tensor_scalar(u, u, GELU_A, 1.0, ALU.mult, ALU.add).then_inc(g_v, 1)
                        dve.wait_ge(g_v, QC * it + (c + 1))
                        dve.tensor_tensor(u, u, x, ALU.mult).then_inc(g_w, 1)
                    if 1 <= c <= QC:
                        x, u = gel_x[:, (c - 1) % 3, :], gel_u[:, (c - 1) % 3, :]
                        dve.wait_ge(g_th, QC * it + c)
                        dve.scalar_tensor_tensor(out=u, in0=u, scalar=1.0, in1=x, op0=ALU.add, op1=ALU.mult).then_inc(g_q, 1)
                    if c >= 2:
                        u = gel_u[:, (c - 2) % 3, :]
                        dve.wait_ge(g_hi, QC * it + (c - 1))
                        dve.scalar_tensor_tensor(out=hid_lo[:, c - 2, :], in0=u, scalar=0.5, in1=hid_hi[:, c - 2, :].bitcast(F32),
                                                 op0=ALU.mult, op1=ALU.subtract).then_inc(g_lo, 1)
                lo_piece(it, QC + RING - 1)
                for fo in range(KC):
                    p = fo % 3
                    dve.wait_ge(filled[2 * p], MOE_USES[p] + 6 * it + (4 + fo // 3 + 1))
                    v = two(z_fm[:, fo, :])
                    dve.scalar_tensor_tensor(out=v, in0=halves(1024 * p), scalar=gate_col[:, bass.ds(it, 1)], in1=v,
                                             op0=ALU.mult, op1=ALU.add).then_inc(freed[2 * p], 1)
                    if last:
                        dve.wait_ge(freed[2 * p], MOE_USES[p] + 6 * it + (4 + fo // 3 + 1))
                        ins = chunk_stats(fo)
                    for k in (QC + 2 * fo + RING, QC + 2 * fo + RING + 1):
                        if k < (24 if last else 24 + RING):
                            lo_piece(it, k)
                return ins

            with dve.Fori(0, 3) as it:
                quarter(it, False)
            chain.link(quarter(3, True))
            global_stats(1)
            for t in range(NT):
                p = t % 3
                dve.wait_ge(filled[2 * p], MOE_USES[p] + 24 + t // 3 + 1)
                if t >= 2:
                    dve.wait_ge(o_left[t % 2], 32 * (t // 2))
                dve.tensor_tensor(o_tm[:, t % 2, :], ps[0:TT, 1024 * p:1024 * p + D], x2[:, t, :], ALU.add).then_inc(freed[2 * p], 1)


def kernel(**inputs):
    import numpy as _np
    import concourse.bacc as _bacc
    from concourse import mybir as _mybir
    from concourse.bass_utils import run_bass_kernel_spmd as _run

    nc = _bacc.Bacc("TRN2", target_bir_lowering=False, num_devices=1)
    arrays, aps = {}, {}
    for name, value in inputs.items():
        if name == "edge_weight1":
            continue
        v = _np.ascontiguousarray(value)
        arrays[f"in_{name}_dram"] = v
        aps[name] = nc.dram_tensor(f"in_{name}_dram", v.shape, _mybir.dt.from_np(v.dtype), kind="ExternalInput").ap()
    out = nc.dram_tensor("out_0_dram", (N, D), _mybir.dt.float32, kind="ExternalOutput").ap()
    gnn_block(nc, aps, out)
    r = _run(nc, [arrays], core_ids=[0])
    return r.results[0]["out_0_dram"]
```

```python
from contextlib import ExitStack

import concourse.bass as bass
from concourse import mybir

ALU = mybir.AluOpType
ACT = mybir.ActivationFunctionType
F32, F32R, F16, BF16, I32, U32 = (mybir.dt.float32, mybir.dt.float32r, mybir.dt.float16, mybir.dt.bfloat16,
                                  mybir.dt.int32, mybir.dt.uint32)
AX_X = mybir.AxisListType.X

N, D, E = 625, 768, 20625
NT, TT = 5, 125
TP, HT = 626, 314
KC = D // 128
GH, GC = 4, 192
L = 3
NHD = L * GH
MH = 12
EP = (E + 255) // 256
NO_EDGE = 2000
HID, NE = 4 * D, 8
QC = HID // 2 // 128
RING, RAW = 6, 3
GAT0, GAT1 = KC, KC + 3 * 2 * L
NEG = -1.0e30
LN_EPS, GLN_EPS = 1e-5, 1e-12
GELU_C, GELU_A = 0.7978845608028654, 0.044715

PAIRS = 3
CHUNKS = 6
SPAN = PAIRS * CHUNKS
ECW = 2 * EP + SPAN



class Psum:

    def __init__(self):
        self.at, self.last, self.when, self.uses, self.clock = {}, {}, [0] * 8, [0] * 8, 0

    def place(self, key, width, banks):
        ok = [b for b in banks if all(x in banks for x in range(b, b + width)) and (width == 1 or b % 2 == 0)]
        home = min(ok, key=lambda b: (max(self.when[b:b + width]), b))
        self.clock += 1
        before = []
        for b in range(home, home + width):
            self.when[b] = self.clock
            if b in self.last and self.last[b] not in before:
                before.append(self.last[b])
            self.last[b] = key
        self.at[key] = (home, self.uses[home], before)
        self.uses[home] += 1


def plan():
    steps, psum = [], Psum()
    slot = [0]
    banks = [0, 1, 2, 3, 6, 7]

    def f_step(name, *args):
        psum.place((name, *args), 2, banks)
        steps.append(("F", name, args, slot[0], (name, *args)))
        slot[0] += 1

    def t_step(name, *args):
        psum.place((name, *args), 1, banks)
        steps.append(("T", name, args, slot[0], (name, *args)))
        if args[-1] == NT - 1:
            slot[0] += 3

    def h_steps(name, between):
        for half in range(2):
            for fo in range(KC):
                psum.place((name, fo, half), 1, banks)
                steps.append(("H", name, (fo, half), slot[0] + fo, (name, fo, half)))
                if (half, fo) in between:
                    between[half, fo]()
        slot[0] += KC

    def x_step(name, *args, width=2, where=None):
        psum.place((name, *args), width, where or banks)
        steps.append(("X", name, args, slot[0], (name, *args)))

    def mark(name, *args):
        steps.append(("M", name, args, slot[0], None))

    x_step("edgesT", width=1)
    x_step("bounds", width=1)
    for t in range(3):
        x_step("xnT", t)
    x_step("biasT", width=1)
    todo = []
    for j in range(NT):
        for c in range(CHUNKS):
            todo.append(("chunk", j, c))
            if j and c == 0:
                todo[-1:] = [("chunk", j, c), ("countT", j - 1)]
        todo.append(("count", j))

    def some_count(n):
        while n and todo:
            name, *a = todo.pop(0)
            if name == "chunk":
                if a[1] == 0:
                    psum.place(("count", a[0]), 2, [4, 5])
                mark("chunk", *a)
                n -= 1
            elif name == "count":
                steps.append(("X", "count", (a[0],), slot[0], ("count", a[0])))
                n -= 1
            else:
                x_step("countT", *a)

    between = {(half, fo): (lambda: some_count(1)) for half in range(2) for fo in (1, 3, 5)}
    between.pop((0, 1))
    between |= {(0, 0): lambda: x_step("xnT", 3), (0, 1): lambda: x_step("xnT", 4), (0, 2): lambda: some_count(1)}
    h_steps("ah", between)
    for layer in range(L):
        for g in range(2):
            for t in range(NT):
                t_step("h", layer, g, t)
                some_count(1)
    while todo:
        some_count(1)
    before_sums = []
    for b in (4, 5, 6):
        if psum.last[b] not in before_sums:
            before_sums.append(psum.last[b])
        psum.last[b] = "heads"
    banks = [0, 1, 2, 3, 7]
    x_step("asT")
    x_step("countT", NT - 1)
    fs = [("mix", f, part) for f in range(KC) for part in range(3)]

    def ft(n):
        for _ in range(n):
            f_step(*fs.pop(0))

    def wo(layer, g, t0, t1):
        for t in range(t0, t1):
            t_step("wo", layer, g, t)

    gt = lambda layer, pr, c: x_step("gT", layer, pr, c)
    agg = lambda j: mark("agg", j)
    ft(6)
    x_step("mzT", 0)
    ft(3)
    agg(0)
    ft(2)
    agg(1)
    ft(1), gt(0, 0, 0), gt(0, 0, 1), gt(0, 0, 2)
    x_step("mzT", 1)
    agg(2)
    ft(1)
    agg(3)
    ft(1), gt(0, 1, 0), gt(0, 1, 1), gt(0, 1, 2)
    agg(4)
    wo(0, 0, 0, 5)
    agg(5)
    wo(0, 1, 0, 5), gt(1, 0, 0), gt(1, 0, 1), gt(1, 0, 2)
    x_step("mzT", 2)
    agg(6)
    ft(1)
    agg(7)
    ft(1), gt(1, 1, 0), gt(1, 1, 1), gt(1, 1, 2)
    agg(8)
    wo(1, 0, 0, 5)
    agg(9)
    wo(1, 1, 0, 5), gt(2, 0, 0), gt(2, 0, 1), gt(2, 0, 2)
    agg(10)
    ft(1)
    agg(11)
    ft(1)
    for c in range(3):
        gt(2, 1, c)
    wo(2, 0, 0, 5), wo(2, 1, 0, 5)
    banks = [0, 1, 2, 3, 4, 5, 6, 7]
    for g in range(2):
        for t in range(NT):
            t_step("proj", g, t)
            if g and t >= 2:
                x_step("xT", t - 2)
    for t in (3, 4):
        x_step("xT", t)
    for u in range(2):
        for g in range(2):
            for t in range(NT):
                t_step("qk", u, g, t)
    x_step("scores")
    x_step("expert_biasT", width=1)
    f_step("v", 0)
    f_step("v", 1)
    f_step("v", 2)
    x_step("wT")
    for hp in range(MH // 2):
        if hp >= 2 and hp + 1 < KC:
            f_step("v", hp + 1)
        x_step("av", hp)
        if hp >= 3:
            x_step("mT", hp - 3)
    h_steps("w2", {(0, 2): lambda: x_step("mT", 3), (0, 5): lambda: x_step("mT", 4)})
    mark("gate")
    return steps, slot[0], psum, before_sums


STEPS, MOE0, PSUM, BEFORE_SUMS = plan()
assert MOE0 % RING == 0
MOE_USES = [PSUM.uses[2 * p] for p in range(3)]
AGG_AT = [i for i, s in enumerate(STEPS) if s[1] == "agg"]
FIRST_MIX = next(i for i, s in enumerate(STEPS) if s[1] == "mzT")
MAX_AFTER = {("mix", 0, 0): (0,), ("mix", 0, 1): (1,), ("mix", 1, 0): (2,), ("mix", 1, 1): (3,),
             ("mix", 2, 0): (4,), ("mix", 3, 0): (5,), ("mix", 3, 1): (6,), ("agg", 1): (7,),
             ("wo", 0, 0, 1): (8,), ("wo", 0, 0, 3): (9,), ("agg", 5): (10,), ("wo", 0, 1, 2): (11,)}
AS_ROW_AT = {0: (7,), 2: (8, 9), 4: (10, 11)}
MIX_AT = {1: 3, 4: 4, 10: 5}
Y_AT = {1: 3, 6: 4, 11: 5}


def softmax_schedule():
    ops = [""] * len(STEPS)
    for j in range(NHD):
        if j:
            ops[AGG_AT[j - 1]] += "a"
        lo = AGG_AT[j - 1] + 1 if j else FIRST_MIX + 1
        between = range(lo, AGG_AT[j] + 1)[:-1] or range(AGG_AT[j], AGG_AT[j] + 1)
        parts = ("" if j else "a") + "ssssf"
        for i, part in enumerate(parts):
            ops[between[i * len(between) // len(parts) if len(between) > 2 else 0]] += part
    return ops


SOFT = softmax_schedule()


def gnn_block(nc, a, out):
    h_scr = nc.dram_tensor("h_scr", (NHD, N, GC + 1), F32).ap()
    as_scr = nc.dram_tensor("as_scr", (NHD, N), F32).ap()
    mz_scr = nc.dram_tensor("mz_scr", (L, 2 * GH, N), F32).ap()
    y_scr = nc.dram_tensor("y_scr", (2, D, TP), F32).ap()
    o_scr = nc.dram_tensor("o_scr", (D, N), F32).ap()

    base = (nc.sbuf_base + 31) // 32 * 32
    top = nc.sbuf_usable_end

    def at(name, shape, dt, off):
        size = 2 if dt in (F16, BF16) else 4
        n = size
        for s in shape[1:]:
            n *= s
        assert off % 32 == 0 and base + off + n <= top, (name, off, n)
        return nc.alloc_sbuf_tensor_at(name, shape, dt, offset=base + off)

    SLOT = D * 4
    FM = (KC * TP * 4 + 31) // 32 * 32
    w_hi = at("w_hi", [128, RING, D], F32R, 0)
    w_lo = at("w_lo", [128, RING, D], F32R, RING * SLOT)
    w_raw = at("w_raw", [128, RAW, D], F32, 2 * RING * SLOT)
    F0 = (2 * RING + RAW) * SLOT
    F1 = F0 + 2 * FM
    R = F1 + 2 * FM
    f0_hi = at("f0_hi", [128, KC, TP], F32R, F0)
    f0_lo = at("f0_lo", [128, KC, TP], F32R, F0 + FM)
    f1_hi = at("f1_hi", [128, KC, TP], F32R, F1)
    f1_lo = at("f1_lo", [128, KC, TP], F32R, F1 + FM)
    hid_hi = at("hid_hi", [128, QC, TP], F32R, F1)
    o = [R]

    def small(name, shape, dt=F32):
        n = 4
        for s in shape[1:]:
            n *= s
        t = at(name, shape, dt, o[0])
        o[0] += (n + 31) // 32 * 32
        return t

    ident = small("ident", [128, 128])
    ones = small("ones", [128, 128])
    bias_row = small("bias_row", [60, 128])
    bias_col = small("bias_col", [128, 60])
    stats = small("stats", [128, 2 * KC, 6])
    mv = small("mv", [128, NT, 2])
    var_eps = small("var_eps", [128, NT])
    neg_half = small("neg_half", [128, NT])
    rstd = small("rstd", [128, NT])
    neg_mr = small("neg_mr", [128, NT])
    asd = small("asd", [125, NT, 2 * NHD])
    n_as = small("n_as", [125, NT, NHD])
    n_as02 = small("n_as02", [125, NT, NHD])
    mx = small("mx", [125, NT, GH])
    z_tmp = small("z_tmp", [125, NT, GH])
    m_tmp = small("m_tmp", [125, NT, GH])
    mz = small("mz", [125, L, NT, 2 * GH])
    den = small("den", [125, NT])
    rden = small("rden", [125, NT])
    mix_sum = small("mix_sum", [128, 4])
    mix_r = small("mix_r", [128, 2])
    mix_t = small("mix_t", [128, 6])
    mix_c = small("mix_c", [128, 1])
    neg_one = small("neg_one", [128, 1])
    r_w = small("r_w", [128, KC, NE])
    r_b = small("r_b", [1, NE])
    gate_row = small("gate_row", [1, 6 * NE])
    gate_idx = small("gate_idx", [1, NE], U32)
    gate_col = small("gate_col", [128, 4])
    z_mv = small("z_mv", [128, KC, 2])
    y_mean = small("y_mean", [128, KC])
    gl = small("gl", [128, 16])
    ln_scale = small("ln_scale", [128, KC])
    ln_bias = small("ln_bias", [128, KC])
    fcb_all = small("fcb_all", [128, 2 * QC * NE])
    pb_all = small("pb_all", [128, KC * NE])
    fcb = small("fcb", [128, 4 * QC])
    pb = small("pb", [128, 2 * KC])
    bounds = small("bounds", [5, 2], I32)
    bsm = small("bsm", [5, 8])
    e_ends = small("e_ends", [EP, 2])
    row_t = small("row_t", [12, N])
    relu_t = small("relu_t", [128, 2, TP])
    B = o[0]

    def span(shape, dt=F32):
        n = 2 if dt in (F16, BF16) else 4
        for s in shape[1:]:
            n *= s
        return (n + 31) // 32 * 32

    o[0] = B

    def take(name, shape, dt=F32):
        t = at(name, shape, dt, o[0])
        o[0] += span(shape, dt)
        return t

    gacc = take("gacc", [125, NT, D])
    P2 = o[0]
    g_tm = take("g_tm", [125, NT, 2 * GC])
    h_tm = take("h_tm", [125, 2, NT, GC + 1])
    PH1 = o[0]
    count = take("count", [125, NT, N])
    mask = take("mask", [125, NT, N], BF16)
    P1 = o[0]
    prob = take("prob", [125, NT, N])
    rows = take("rows", [128, 2, 2, N])
    as_row = take("as_row", [128, 2, N])
    q_fm = take("q_fm", [128, TP])
    k_fm = take("k_fm", [128, TP])
    t_fm = take("t_fm", [128, TP])
    y_hi = take("y_hi", [128, TP], F32R)
    y_lo = take("y_lo", [128, TP], F32R)
    junk = take("junk", [125, 2, N], BF16)
    o[0] = B
    a_bc = take("a_bc", [125, 2, 2, D])
    o[0] = P2 if P2 > o[0] else o[0]
    e_int = take("e_int", [EP, 2, 256], I32)
    e_f = take("e_f", [EP, 2, 256])
    e_col = take("e_col", [128, 2, 2, ECW])
    e_lo5 = take("e_lo5", [5, 4, 96])
    iota = take("iota", [128, N], F16)
    oh2_s = take("oh2_s", [128, 2, N], F16)
    oh2_d = take("oh2_d", [128, 2, 126], F16)
    wide = take("wide", [125, 1126], F16)
    assert o[0] <= PH1, (o[0], PH1)
    o[0] = P1
    x_tm = take("x_tm", [125, NT, D])
    h_st = take("h_st", [125, 3, 2, GC + 1])
    junk1 = take("junk1", [125, 4, GC], BF16)
    oh_s = take("oh_s", [128, 4 * PAIRS, N], F16)
    oh_d = take("oh_d", [128, 4 * PAIRS, 126], F16)
    iota_f = at("iota_f", [128, N], F32, o[0])
    count_ds = take("count_ds", [128, N])
    x2 = at("x2", [125, NT, D], F32, P2)
    o[0] = P2 + span([125, NT, D])
    xr = take("xr", [125, NT, D])
    k_tm = at("k_tm", [125, NT, D], F32, o[0] - span([125, NT, D]))
    gel_x = at("gel_x", [128, 3, TP], F32, o[0] - span([125, NT, D]))
    gel_u = at("gel_u", [128, 3, TP], F32, o[0] - span([125, NT, D]) + span([128, 3, TP]))
    assert 2 * span([128, 3, TP]) <= span([125, NT, D])
    z_fm = take("z_fm", [128, KC, TP])
    LATE = o[0]
    hid_lo = at("hid_lo", [128, QC, TP], F32R, LATE)
    xl_tm = take("xl_tm", [125, NT, D])
    v_fm = at("v_fm", [128, KC, TP], F32, LATE)
    qk_b = take("qk_b", [125, 2 * D])
    pj_b = take("pj_b", [125, D])
    e_blk = take("e_blk", [128, KC, 128])
    w_t = take("w_t", [128, KC, 128])
    o_fm = at("o_fm", [128, 2, TP], F32, B - span([128, 2, TP]))
    fcb_row = at("fcb_row", [QC * NE, 2, 128], F32, B - span([128, 2, TP]))
    pb_row = at("pb_row", [KC * NE, 128], F32, B - span([128, 2, TP]) + span([128, 2, 128]))
    sm = take("sm", [128, 8 * KC])
    q_tm = at("q_tm", [125, NT, D], F32, B)
    m_tm = at("m_tm", [125, NT, D], F32, B)
    o_tm = at("o_tm", [125, 2, D], F32, B)

    ctx = ExitStack()
    with ctx:
        ps = ctx.enter_context(nc.psum_tensor("ps", [128, 4096], F32))
        AGG = 2048
        MISC = 3584
        sem = lambda name: ctx.enter_context(nc.semaphore(name))

        filled = [sem(f"filled{i}") for i in range(8)]
        freed = [sem(f"freed{i}") for i in range(8)]
        w_landed = [sem(f"w_landed{i}") for i in range(RAW)]
        w_hi_ready, w_lo_ready = sem("w_hi_ready"), sem("w_lo_ready")
        ln_stats, ln_mv = sem("ln_stats"), sem("ln_mv")
        pads, e_col_set, chunk_tile, chunk_used = sem("pads"), sem("e_col_set"), sem("chunk_tile"), sem("chunk_used")
        x_loaded = [sem(f"x_loaded{t}") for t in range(NT)]
        e_loaded, c_loaded = sem("e_loaded"), sem("c_loaded")
        e_pad = sem("e_pad")
        consts = sem("consts")
        act_done, dve_done, pool_done = sem("act_done"), sem("dve_done"), sem("pool_done")
        var_ready, rstd_ready, nmr_ready = sem("var_ready"), sem("rstd_ready"), sem("nmr_ready")
        ln_out = sem("ln_out")
        hi_first = sem("hi_first")
        relu_split = sem("relu_split")
        y_split = sem("y_split")
        edges_f, bounds_ready = sem("edges_f"), sem("bounds_ready")
        oh_ready = [sem(f"oh_ready{j}") for j in range(NT)]
        oh_used = [sem(f"oh_used{j}") for j in range(NT)]
        mask_ready = sem("mask_ready")
        a_loaded = [sem("a_loaded0"), sem("a_loaded1")]
        hs_summed = sem("hs_summed")
        hs_stored = [sem(f"hs_stored{i}") for i in range(3)]
        row_stored = sem("row_stored")
        asrow_loaded = [sem("asrow_loaded0"), sem("asrow_loaded1")]
        rows_loaded = [sem("rows_loaded0"), sem("rows_loaded1")]
        h_loaded = [sem("h_loaded0"), sem("h_loaded1")]
        gacc_set = sem("gacc_set")
        head_maxed, mz_ready = sem("head_maxed"), sem("mz_ready")
        as_scaled = sem("as_scaled")
        sm_up, sm_min, sm_exp, p_ready, p_used = (sem("sm_up"), sem("sm_min"), sem("sm_exp"), sem("p_ready"),
                                                   sem("p_used"))
        rden_ready, agg_freed = sem("rden_ready"), sem("agg_freed")
        mix_rr, y_ready, y_stored = sem("mix_rr"), sem("y_ready"), sem("y_stored")
        y_loaded, xr_loaded, xr_ready = sem("y_loaded"), sem("xr_loaded"), sem("xr_ready")
        late_loaded = sem("late_loaded")
        sc_sub, sc_exp, eblk_ready = sem("sc_sub"), sem("sc_exp"), sem("eblk_ready")
        o_stored = [sem("o_stored0"), sem("o_stored1")]
        m_loaded = [sem(f"m_loaded{t}") for t in range(NT)]
        gl_in, gl_sum, gl_var, gl_rstd, gl_ready = (sem("gl_in"), sem("gl_sum"), sem("gl_var"), sem("gl_rstd"),
                                                    sem("gl_ready"))
        y_hi_ready = sem("y_hi_ready")
        y_fm_ready, z_set = sem("y_fm_ready"), sem("z_set")
        gate_in, gate_mm, gate_e_in, gate_e, gate_ready, gate_bc = (sem("gate_in"), sem("gate_mm"), sem("gate_e_in"), sem("gate_e"),
                                                           sem("gate_ready"), sem("gate_bc"))
        eb_loaded, eb_ready = sem("eb_loaded"), sem("eb_ready")
        g_v, g_w, g_th, g_q, g_hi, g_lo = (sem("g_v"), sem("g_w"), sem("g_th"), sem("g_q"), sem("g_hi"),
                                           sem("g_lo"))
        fin_ready, fin_ready_v, o_left = sem("fin_ready"), sem("fin_ready_v"), [sem("o_left0"), sem("o_left1")]
        block = ctx.enter_context(nc.Block())

        def pb0(key):
            return 512 * PSUM.at[key][0]

        def halves(b, m=128):
            return ps[0:m, b + 2:b + 1024].rearrange("p (h c) -> p h c", h=2)[:, :, 0:HT - 1]

        def two(ap):
            return ap.rearrange("p (h c) -> p h c", h=2)

        def tsp(b, m=128):
            return ps[0:m, b + 12:b + 12 + N]

        def wait_filled(eng, key):
            p, u, _ = PSUM.at[key]
            eng.wait_ge(filled[p], u + 1)

        def wait_freed(eng, key):
            p, u, _ = PSUM.at[key]
            eng.wait_ge(freed[p], u + 1)

        class Chain:

            def __init__(self, eng, s):
                self.eng, self.s, self.n = eng, s, 0

            def link(self, ins):
                ins.then_inc(self.s, 1)
                self.n += 1
                self.eng.wait_ge(self.s, self.n)

        last_reader = {}
        for kind, _, _, n0, job in STEPS:
            for i in range({"F": 1, "H": 1, "T": 3}.get(kind, 0)):
                last_reader[n0 + i] = job

        def slot_free(eng, n):
            if n >= RING:
                wait_filled(eng, last_reader[n - RING])

        def cols(w, c0, c):
            return w.rearrange("(k p) n -> p k n", p=128)[:, :, c0:c0 + c]

        def f_piece(name, args):
            if name == "ah":
                return cols(a["L0_gnn_W_ah"], 128 * args[0], 128)
            if name == "mix":
                return cols(a["L0_mix_w_qkv"], D * args[1] + 128 * args[0], 128)
            if name == "v":
                return cols(a["L0_ffn_W1_w"], 2 * D + 128 * args[0], 128)
            return cols(a["L0_ffn_W2_w"], 128 * args[0], 128)

        def t_piece(name, args, i):
            g = args[-2]
            if name == "h":
                w, r0, c0 = a[f"L0_gnn_W{args[0]}"], 0, 0
            elif name == "wo":
                w, r0, c0 = a["L0_gnn_W_out"], D * args[0], 0
            elif name == "proj":
                w, r0, c0 = a["L0_mix_w_proj"], 0, 0
            else:
                w, r0, c0 = a["L0_ffn_W1_w"], 0, D * args[0]
            return w[r0:r0 + D, :].rearrange("(k p) n -> p k n", p=128)[:, 2 * i:2 * i + 2, c0 + 384 * g:c0 + 384 * g + 384]

        pieces = []
        for kind, name, args, n0, _ in STEPS:
            if kind == "F" or kind == "H" and args[1] == 0:
                pieces.append((f_piece(name, args), 128))
            elif kind == "T" and args[-1] == 0:
                pieces += [(t_piece(name, args, i), 384) for i in range(3)]
        assert len(pieces) == MOE0

        @block.sync
        def _(sp):
            for t in range(NT):
                for p0, p1 in ((0, 112), (112, 125)):
                    sp.dma_start(x_tm[p0:p1, t, :], a["x"][TT * t + p0:TT * t + p1, :]).then_inc(x_loaded[t], 16)
            for n, (src, c) in enumerate(pieces):
                if n >= RAW:
                    sp.wait_ge(w_lo_ready, n - RAW + 1)
                sp.dma_start(w_raw[:, n % RAW, :].rearrange("p (k n) -> p k n", n=c), src).then_inc(w_landed[n % RAW], 16)
                if n == RAW - 1:
                    row = 0
                    for name, sub in (("L0_gnn_b_ah", None), ("L0_gnn_b0", None), ("L0_gnn_b1", None), ("L0_gnn_b2", None),
                                      ("L0_ffn_W1_b", slice(2 * D, 3 * D)), ("L0_ffn_W2_b", None), ("L0_ffn_ln1_w", None),
                                      ("L0_ffn_ln1_b", None), ("L0_ffn_ln2_w", None), ("L0_ffn_ln2_b", None)):
                        src = a[name] if sub is None else a[name][sub]
                        sp.dma_start(bias_row[row:row + KC, :], src.rearrange("(k p) -> k p", p=128)).then_inc(c_loaded, 16)
                        row += KC
                    sp.dma_start(r_w[:, :, :], a["L0_ffn_r_w"].rearrange("(k p) n -> p k n", p=128)).then_inc(c_loaded, 16)
                    sp.dma_start(r_b[:, :], a["L0_ffn_r_b"].rearrange("(a n) -> a n", a=1)).then_inc(c_loaded, 16)
            sp.wait_ge(gate_ready, 1)
            n = MOE0
            for it in range(4):
                if it % 2 == 0:
                    e = sp.value_load(gate_idx[0:1, it // 2:it // 2 + 1], min_val=0, max_val=NE - 1)
                fc = a["L0_ffn_fc_w"][bass.ds(e, 1)].rearrange("a (k p) n -> (a p) k n", p=128)
                pj = a["L0_ffn_proj_w"][bass.ds(e, 1)].rearrange("a (k p) n -> (a p) k n", p=128)
                srcs = [fc[:, :, 128 * (QC * (it % 2) + c):128 * (QC * (it % 2) + c + 1)] for c in range(QC)]
                srcs += [pj[:, QC * (it % 2) + KC * i:QC * (it % 2) + KC * i + KC, 128 * fo:128 * fo + 128]
                         for fo in range(KC) for i in range(2)]
                for src in srcs:
                    sp.wait_ge(w_lo_ready, n - RAW + 1)
                    sp.dma_start(w_raw[:, n % RAW, :].rearrange("p (k n) -> p k n", n=128), src).then_inc(w_landed[n % RAW], 16)
                    n += 1
            for t in range(NT):
                sp.wait_ge(freed[2 * (t % 3)], MOE_USES[t % 3] + 24 + t // 3 + 1)
                for p0, p1 in ((0, 112), (112, 125)):
                    sp.dma_start(out[TT * t + p0:TT * t + p1, :], o_tm[p0:p1, t % 2, :]).then_inc(o_left[t % 2], 16)
            sp.wait_ge(o_left[0], 32 * 3)
            sp.wait_ge(o_left[1], 32 * 2)

        @block.gpsimd
        def _(pool):
            chain = Chain(pool, pool_done)
            pool.memset(e_int[64:EP, :, :], NO_EDGE).then_inc(e_pad, 1)
            pool.wait_ge(e_pad, 1)
            pool.memset(neg_half[:, :], -0.5)
            pool.memset(neg_one[:, :], -1.0)
            chain.link(pool.memset(ident[:, :], 0.0))
            pool.affine_select(out=ident[:, :], in_=ident[:, :], compare_op=ALU.not_equal, fill=1.0, base=0,
                               pattern=[[-1, 128]], channel_multiplier=1).then_inc(consts, 1)
            pool.memset(e_col[:, :, :, EP:ECW], float(NO_EDGE)).then_inc(e_col_set, 1)
            pool.iota(iota_f[:, :], pattern=[[1, N]], base=0, channel_multiplier=0, allow_small_or_imprecise_dtypes=True)
            pool.iota(bsm[:, 0:1], pattern=[[1, 1]], base=0, channel_multiplier=TT,
                      allow_small_or_imprecise_dtypes=True).then_inc(consts, 1)

            def rstd_of(n):
                t = n % NT
                pool.wait_ge(var_ready, n + 1)
                pool.tensor_tensor(rstd[0:TT, t:t + 1], var_eps[0:TT, t:t + 1], neg_half[0:TT, 0:1], ALU.pow).then_inc(rstd_ready, 1)

            chain.link(pool.memset(wide[:, :], 0.0))
            pool.affine_select(out=wide[:, :], in_=wide[:, :], compare_op=ALU.not_equal, fill=1.0, base=500,
                               pattern=[[-1, 1126]], channel_multiplier=1).then_inc(consts, 1)
            for t in range(NT):
                rstd_of(t)
            for t in (f0_hi, f0_lo, f1_hi, f1_lo):
                last = pool.memset(t[:, :, N:TP].bitcast(F32), 0.0)
            last.then_inc(pads, 1)
            pool.memset(ones[:, :], 1.0)
            pool.memset(h_st[:, :, :, GC:GC + 1], 1.0).then_inc(pads, 1)

            def load_a(layer):
                if layer >= 2:
                    pool.wait_ge(hs_summed, 2 * NT * (layer - 1))
                for w, name in enumerate((f"L0_gnn_a_src{layer}", f"L0_gnn_a_dst{layer}")):
                    pool.dma_start(a_bc[:, layer % 2, w, :],
                                   a[name].rearrange("h c -> (h c)").rearrange("(a n) -> a n", a=1).to_broadcast([TT, D])
                                   ).then_inc(a_loaded[layer % 2], 16)

            load_a(0)
            load_a(1)
            pool.wait_ge(pads, 2)
            i, n = 0, GAT0
            for layer in range(L):
                if layer == 2:
                    load_a(2)
                for g in range(2):
                    while n < min(GAT0 + 3 * (2 * layer + g) + RING, GAT1):
                        if n == GAT0:
                            pool.wait_ge(w_lo_ready, GAT0)
                        pool.wait_ge(w_hi_ready, n + 1)
                        pool.tensor_tensor(w_lo[:, n % RING, :], w_raw[:, n % RAW, :], w_hi[:, n % RING, :].bitcast(F32),
                                           ALU.subtract).then_inc(w_lo_ready, 1)
                        n += 1
                    for t in range(NT):
                        wait_freed(pool, ("h", layer, g, t))
                        pool.dma_start(h_scr[GH * layer + 2 * g:GH * layer + 2 * g + 2, TT * t:TT * t + TT, :].rearrange("h p c -> p h c"),
                                       h_st[:, i % 3]).then_inc(hs_stored[i % 3], 16)
                        i += 1

            def load_as_row(j):
                if j >= 2:
                    pool.wait_ge(head_maxed, NT * (j - 1))
                pool.dma_start(as_row[:, j % 2, :], as_scr[j:j + 1, :].to_broadcast([128, N])).then_inc(asrow_loaded[j % 2], 16)

            def load_rows(j):
                layer, h = divmod(j, GH)
                if j >= 2:
                    pool.wait_ge(sm_min, NT * (j - 1))
                for k in range(2):
                    pool.dma_start(rows[:, j % 2, k, :], mz_scr[layer, k * GH + h:k * GH + h + 1, :].to_broadcast([128, N])
                                   ).then_inc(rows_loaded[j % 2], 16)

            def load_h(j):
                if j >= 2:
                    pool.wait_ge(p_used, NT * (j - 1))
                pool.dma_start(h_tm[:, j % 2], h_scr[j].rearrange("(t p) c -> p t c", p=TT)).then_inc(h_loaded[j % 2], 16)

            def mix_factors(f):
                wait_freed(pool, ("mix", f, 1))
                chain.link(pool.tensor_tensor(mix_r[:, :], mix_sum[:, 1:4:2], neg_half[:, 0:2], ALU.pow))
                chain.link(pool.tensor_tensor(mix_t[:, 0:2], mix_sum[:, 0:4:2], mix_r[:, :], ALU.mult))
                chain.link(pool.tensor_tensor(mix_t[:, 2:3], mix_t[:, 0:1], mix_t[:, 1:2], ALU.mult))
                chain.link(pool.tensor_scalar(mix_t[:, 3:4], mix_t[:, 2:3], float(N), None, ALU.add))
                chain.link(pool.tensor_tensor(mix_t[:, 4:5], mix_t[:, 3:4], neg_one[:, :], ALU.pow))
                chain.link(pool.tensor_tensor(mix_t[:, 5:6], mix_r[:, 0:1], mix_r[:, 1:2], ALU.mult))
                pool.tensor_tensor(mix_c[:, :], mix_t[:, 4:5], mix_t[:, 5:6], ALU.mult).then_inc(mix_rr, 1)

            def store_y(f):
                pool.wait_ge(y_ready, f + 1)
                for i, t in enumerate((y_hi, y_lo)):
                    pool.dma_start(y_scr[i, 128 * f:128 * f + 128, :], t[:, :].bitcast(F32)).then_inc(y_stored, 16)

            def store_mz(layer):
                wait_freed(pool, ("mzT", layer))
                pool.dma_start(mz_scr[layer], row_t[0:2 * GH, :]).then_inc(row_stored, 16)
                pool.wait_ge(row_stored, 16 * (layer + 2))

            wait_freed(pool, ("asT",))
            pool.dma_start(as_scr, row_t[:, :]).then_inc(row_stored, 16)
            pool.wait_ge(row_stored, 16)
            load_as_row(0)
            load_as_row(1)
            for q in hs_stored:
                pool.wait_ge(q, 16 * (2 * NT * L // 3))
            load_as_row(2)
            mix_factors(0)
            load_as_row(3)
            load_h(0)
            load_h(1)
            store_y(0)
            mix_factors(1)
            store_mz(0)
            load_rows(0)
            load_rows(1)
            load_as_row(4)
            load_as_row(5)
            store_y(1)
            mix_factors(2)
            load_as_row(6)
            store_y(2)
            pool.wait_ge(hs_summed, 2 * NT * L)
            for t in range(NT):
                pool.dma_start(gacc[:, t, :], a["L0_gnn_b_out"].rearrange("(a n) -> a n", a=1).to_broadcast([TT, D])).then_inc(gacc_set, 16)
            for j in range(NHD):
                if j + 2 < NHD:
                    load_h(j + 2)
                if j in MIX_AT:
                    mix_factors(MIX_AT[j])
                if j + 2 < NHD:
                    if (j + 2) % GH == 0:
                        store_mz((j + 2) // GH)
                    load_rows(j + 2)
                for nxt in AS_ROW_AT.get(j, ()):
                    load_as_row(nxt)
                if j in Y_AT:
                    store_y(Y_AT[j])
            wait_filled(pool, ("mix", KC - 1, 2))
            pool.wait_ge(y_stored, 32 * KC)
            for i, t in enumerate((f0_hi, f0_lo)):
                pool.dma_start(t[:, :, :].bitcast(F32), y_scr[i].rearrange("(k p) n -> p k n", p=128)).then_inc(y_loaded, 16)
            pool.wait_ge(agg_freed, NHD)
            pool.wait_ge(p_used, NT * NHD)
            wait_filled(pool, ("gT", L - 1, 1, 2))
            for p0, p1 in ((0, 112), (112, 125)):
                pool.dma_start(xr[p0:p1], a["x"].rearrange("(t p) n -> p t n", p=TT)[p0:p1]).then_inc(xr_loaded, 16)
            pool.wait_ge(relu_split, KC * (L + 2))
            pool.dma_start(fcb_row[:, :, :], a["L0_ffn_fc_b"].rearrange("(h e) (k p) -> (e k) h p", p=128, h=2)).then_inc(eb_loaded, 16)
            pool.dma_start(pb_row[:, :], a["L0_ffn_proj_b"].rearrange("e (k p) -> (e k) p", p=128)).then_inc(eb_loaded, 16)
            pool.dma_start(pj_b[:, :], a["L0_mix_b_proj"].rearrange("(a n) -> a n", a=1).to_broadcast([TT, D])).then_inc(xr_loaded, 16)
            pool.dma_start(qk_b[:, :], a["L0_ffn_W1_b"][0:2 * D].rearrange("(a n) -> a n", a=1).to_broadcast([TT, 2 * D])).then_inc(late_loaded, 16)
            pool.wait_ge(xr_loaded, 48)
            for t in range(NT):
                pool.tensor_tensor(xr[:, t, :], xr[:, t, :], pj_b[:, :], ALU.add).then_inc(xr_ready, 1)
            pool.memset(e_blk[:, :, :], 0.0).then_inc(xr_ready, 1)
            for t in range(NT):
                rstd_of(NT + t)
            for t in range(NT):
                wait_freed(pool, ("xT", t))
            for k in range(KC):
                pool.tensor_tensor(z_fm[:, k, 0:N], f0_hi[:, k, 0:N].bitcast(F32), f0_lo[:, k, 0:N].bitcast(F32), ALU.add
                                   ).then_inc(z_set, 1)
            flat = o_scr.rearrange("d n -> (d n)").rearrange("(t p n) -> t p n", p=TT, n=D)
            for hp in range(MH // 2):
                wait_freed(pool, ("av", hp))
                pool.dma_start(o_scr[128 * hp:128 * hp + 128, :], o_fm[:, hp % 2, 0:N]).then_inc(o_stored[hp % 2], 16)
                if hp == 0:
                    continue
                t = hp - 1
                assert TT * D * (t + 1) <= 128 * N * (hp + 1)
                pool.wait_ge(o_stored[0], 16 * (hp // 2 + 1))
                pool.wait_ge(o_stored[1], 16 * ((hp + 1) // 2))
                for p0, p1 in ((0, 112), (112, 125)):
                    pool.dma_start(m_tm[p0:p1, t, :], flat[t, p0:p1, :]).then_inc(m_loaded[t], 16)
            pool.wait_ge(gl_var, 1)
            pool.tensor_tensor(gl[:, 5:6], gl[:, 4:5], neg_half[:, 0:1], ALU.pow).then_inc(gl_rstd, 1)
            pool.wait_ge(gl_var, 2)
            pool.tensor_tensor(gl[:, 5:6], gl[:, 4:5], neg_half[:, 0:1], ALU.pow).then_inc(gl_rstd, 1)

        @block.tensor
        def _(pe):
            def begin(key):
                home, _, before = PSUM.at[key]
                for k in before:
                    if k == "heads":
                        pe.wait_ge(agg_freed, NHD)
                    else:
                        wait_freed(pe, k)
                return 512 * home

            def f_product(b, slots, nk, xh, xl, wait_k=None, halves=((2, 0), (512, TP - HT))):
                for k in range(nk):
                    if wait_k:
                        wait_k(k)
                    wh = w_hi[:, slots[k // KC], 128 * (k % KC):128 * (k % KC) + 128]
                    wl = w_lo[:, slots[k // KC], 128 * (k % KC):128 * (k % KC) + 128]
                    for i, (w, x) in enumerate(((wh, xh), (wh, xl), (wl, xh))):
                        for o, c0 in halves:
                            ins = pe.matmul(ps[:, b + o:b + o + HT], w, x[:, k, c0:c0 + HT],
                                            start=(k == 0 and i == 0), stop=(k == nk - 1 and i == 2))
                return ins

            def t_product(b, n0, xh, xl, t):
                for k in range(KC):
                    s, c = (n0 + k // 2) % RING, 384 * (k % 2)
                    wh, wl = w_hi[:, s, c:c + 384], w_lo[:, s, c:c + 384]
                    h, lo = xh[:, k, TT * t:TT * t + TT], xl[:, k, TT * t:TT * t + TT]
                    for i, (x, w) in enumerate(((h, wh), (h, wl), (lo, wh))):
                        ins = pe.matmul(ps[0:TT, b:b + 384], x, w, start=(k == 0 and i == 0), stop=(k == KC - 1 and i == 2))
                return ins

            def chunk_transposes(b, src):
                for c in range(KC):
                    ins = pe.transpose(ps[:, b + 12 + TT * c:b + 12 + TT * c + TT], src[:, 128 * c:128 * c + 128], ident[0:TT, 0:TT])
                return ins

            def transposes(b, src, m=128):
                for t in range(NT):
                    ins = pe.transpose(ps[0:m, b + 12 + TT * t:b + 12 + TT * t + TT], src(t), ident[0:TT, 0:TT])
                return ins

            operands = {"ah": (f0_hi, f0_lo), "h": (f1_hi, f1_lo), "mix": (f0_hi, f0_lo), "wo": (f1_hi, f1_lo),
                        "proj": (f0_hi, f0_lo), "qk": (f0_hi, f0_lo), "v": (f0_hi, f0_lo), "w2": (f1_hi, f1_lo)}

            def operand_ready(kind, name, args):
                made = {"ah": "xnT", "mix": "xnT", "qk": "xT", "v": "xT", "w2": "mT"}
                tiles = (args[-1],) if name == "qk" else range(3) if kind == "H" and args[1] == 0 else range(NT)
                if name == "ah" and args[0] == 0:
                    pe.wait_ge(pads, 1)
                if name in made:
                    for t in tiles:
                        wait_freed(pe, (made[name], t))
                elif name == "h":
                    if args[1:] == (0, 0):
                        pe.wait_ge(relu_split, 2 * KC)
                elif name == "wo":
                    if args[1:] == (0, 0):
                        pe.wait_ge(relu_split, KC * (args[0] + 3))
                elif args == (0, 0):
                    pe.wait_ge(y_loaded, 32)

            for kind, name, args, n0, job in STEPS:
                b = begin(job) if job and name != "count" else 0
                if kind in "FTH":
                    xh, xl = operands[name]
                    operand_ready(kind, name, args)
                if kind == "F":
                    pe.wait_ge(w_lo_ready, n0 + 1)
                    f_product(b, [n0 % RING], KC, xh, xl).then_inc(filled[b // 512], 1)
                elif kind == "H":
                    pe.wait_ge(w_lo_ready, n0 + 1)
                    f_product(b, [n0 % RING], KC, xh, xl, halves=((0, (TP - HT) * args[1]),)).then_inc(filled[b // 512], 1)
                elif kind == "T":
                    if args[-1] == 0:
                        pe.wait_ge(w_lo_ready, n0 + 3)
                    t_product(b, n0, xh, xl, args[-1]).then_inc(filled[b // 512], 1)
                elif name == "agg":
                    j = args[0]
                    if j == 0:
                        for k in BEFORE_SUMS:
                            wait_freed(pe, k)
                    else:
                        pe.wait_ge(agg_freed, j)
                    pe.wait_ge(h_loaded[j % 2], 16 * (j // 2 + 1))
                    for i in range(NT):
                        pe.wait_ge(p_ready, NT * j + i + 1)
                        for d in range(NT):
                            ins = pe.matmul(ps[0:TT, AGG + 256 * d:AGG + 256 * d + GC + 1], prob[:, i, TT * d:TT * d + TT],
                                            h_tm[:, j % 2, i, :], start=(i == 0 and d % 2 == 0), stop=(i == NT - 1),
                                            skip_group_check=True)
                        ins.then_inc(p_used, 1)
                elif name == "edgesT":
                    pe.wait_ge(consts, 1)
                    pe.wait_ge(edges_f, 2)
                    for w in range(2):
                        for s in range(2):
                            ins = pe.transpose(ps[:, b + 96 * (2 * w + s):b + 96 * (2 * w + s) + EP],
                                               e_f[:, w, 128 * s:128 * s + 128], ident[0:EP, 0:EP])
                    ins.then_inc(filled[b // 512], 1)
                elif name == "bounds":
                    pe.wait_ge(edges_f, 4)
                    for w in range(2):
                        ins = pe.matmul(ps[0:5, b + 96 * w:b + 96 * w + EP], e_ends[0:EP, w:w + 1].to_broadcast([EP, 5]),
                                        ident[0:EP, 0:EP], start=True, stop=True)
                    ins.then_inc(filled[b // 512], 1)
                elif name == "biasT":
                    pe.wait_ge(c_loaded, 16 * 12)
                    pe.transpose(ps[:, b:b + 60], bias_row[:, :], ident[0:60, 0:60]).then_inc(filled[b // 512], 1)
                elif name == "chunk":
                    j, c = args
                    if c == 0:
                        b = begin(("count", j))
                        if j == 0:
                            pe.wait_ge(consts, 3)
                        for c0, w in ((0, 512), (512, N - 512)):
                            ins = pe.matmul(ps[0:TT, b + c0:b + c0 + w], wide[:, 500:500 + TT],
                                            wide[:, 500 - TT * j + c0:500 - TT * j + c0 + w], start=True, stop=False,
                                            skip_group_check=True)
                        ins.then_inc(oh_used[j], 2)
                    b = pb0(("count", j))
                    n = CHUNKS * j + c
                    for i in range(2 * PAIRS):
                        o = 2 * PAIRS * (n % 2) + i
                        pe.wait_ge(chunk_tile, 2 * PAIRS * n + i + 1)
                        for c0, w in ((0, 512), (512, N - 512)):
                            ins = pe.matmul(ps[0:TT, b + c0:b + c0 + w], oh_d[:, o, 0:TT], oh_s[:, o, c0:c0 + w],
                                            start=False, stop=False, skip_group_check=True)
                    ins.then_inc(chunk_used, 1)
                elif name == "count":
                    j, = args
                    b = pb0(job)
                    pe.wait_ge(bounds_ready, 1)
                    trips = pe.value_load(bounds[j:j + 1, 1:2], min_val=1, max_val=EP)
                    with pe.Fori(0, trips) as q:
                        for s in range(2):
                            pe.wait_ge(oh_ready[j], 2 * q + (s + 1))
                            for c0, w in ((0, 512), (512, N - 512)):
                                ins = pe.matmul(ps[0:TT, b + c0:b + c0 + w], oh2_d[:, s, 0:TT], oh2_s[:, s, c0:c0 + w],
                                                start=False, stop=False, skip_group_check=True)
                            ins.then_inc(oh_used[j], 1)
                    for c0, w in ((0, 512), (512, N - 512)):
                        ins = pe.matmul(ps[0:TT, b + c0:b + c0 + w], wide[:, 1000:1000 + TT], wide[:, 0:w],
                                        start=False, stop=True, skip_group_check=True)
                    ins.then_inc(filled[b // 512], 1)
                elif name == "countT":
                    j, = args
                    wait_freed(pe, ("count", j))
                    transposes(b, lambda i: count_ds[0:TT, TT * i:TT * i + TT], TT).then_inc(filled[b // 512], 1)
                elif name == "xnT":
                    t, = args
                    pe.wait_ge(consts, 1)
                    pe.wait_ge(ln_out, t + 1)
                    chunk_transposes(b, x_tm[:, t, :]).then_inc(filled[b // 512], 1)
                elif name == "asT":
                    pe.wait_ge(hs_summed, 2 * NT * L)
                    transposes(b, lambda t: asd[:, t, 0:NHD], NHD).then_inc(filled[b // 512], 1)
                elif name == "mzT":
                    layer = args[0]
                    pe.wait_ge(mz_ready, layer + 1)
                    transposes(b, lambda t: mz[:, layer, t, :], 2 * GH).then_inc(filled[b // 512], 1)
                elif name == "gT":
                    layer, pr, c = args
                    pe.wait_ge(agg_freed, layer * GH + 2 * pr + 2)
                    transposes(b, lambda d: g_tm[:, d, 128 * c:128 * c + 128]).then_inc(filled[b // 512], 1)
                elif name == "xT":
                    t, = args
                    pe.wait_ge(ln_out, NT + t + 1)
                    chunk_transposes(b, xl_tm[:, t, :]).then_inc(filled[b // 512], 1)
                elif name == "scores":
                    for u in range(2):
                        for g in range(2):
                            for t in range(NT):
                                wait_freed(pe, ("qk", u, g, t))
                    for hp in range(MH // 2):
                        for t in range(NT):
                            ins = pe.matmul(ps[:, b + 128 * hp:b + 128 * hp + 128], q_tm[:, t, 128 * hp:128 * hp + 128],
                                            k_tm[:, t, 128 * hp:128 * hp + 128], start=(t == 0), stop=(t == NT - 1))
                    ins.then_inc(filled[b // 512], 1)
                elif name == "wT":
                    pe.wait_ge(eblk_ready, 1)
                    for hp in range(MH // 2):
                        ins = pe.transpose(ps[:, b + 128 * hp:b + 128 * hp + 128], e_blk[:, hp, :], ident[:, :])
                    ins.then_inc(filled[b // 512], 1)
                elif name == "av":
                    hp = args[0]
                    wait_freed(pe, ("wT",))
                    wait_freed(pe, ("v", hp))
                    for o, c0 in ((2, 0), (512, TP - HT)):
                        ins = pe.matmul(ps[:, b + o:b + o + HT], w_t[:, hp, :], v_fm[:, hp, c0:c0 + HT],
                                        start=True, stop=True)
                    ins.then_inc(filled[b // 512], 1)
                elif name == "mT":
                    t, = args
                    pe.wait_ge(m_loaded[t], 32)
                    chunk_transposes(b, m_tm[:, t, :]).then_inc(filled[b // 512], 1)
                elif name == "expert_biasT":
                    pe.wait_ge(eb_loaded, 32)
                    for h in range(2):
                        pe.transpose(ps[:, b + QC * NE * h:b + QC * NE * (h + 1)], fcb_row[:, h, :], ident[0:QC * NE, 0:QC * NE])
                    pe.transpose(ps[:, b + 2 * QC * NE:b + 2 * QC * NE + KC * NE], pb_row[:, :], ident[0:KC * NE, 0:KC * NE]
                                 ).then_inc(filled[b // 512], 1)
                elif name == "gate":
                    wait_freed(pe, PSUM.last[7])
                    for i in range(2):
                        pe.wait_ge(gl_in, i + 1)
                        pe.matmul(ps[:, MISC + i:MISC + i + 1], ones[:, :], gl[:, 2 * i:2 * i + 1], start=True, stop=True
                                  ).then_inc(gl_sum, 1)
                    pe.wait_ge(gate_in, 1)
                    for k in range(KC):
                        ins = pe.matmul(ps[0:1, MISC + 8:MISC + 16], y_mean[:, k:k + 1], r_w[:, k, :], start=(k == 0), stop=(k == KC - 1))
                    ins.then_inc(gate_mm, 1)
                    pe.wait_ge(gate_ready, 1)
                    pe.matmul(ps[:, MISC + 16:MISC + 18], ones[0:1, :], gate_row[0:1, 3 * NE:3 * NE + 2], start=True, stop=True
                              ).then_inc(gate_bc, 1)

            for q in range(6):
                wait_freed(pe, PSUM.last[q])
            pe.wait_ge(y_split, KC)

            def quarter(it):
                n0 = MOE0 + 24 * it
                for c in range(QC):
                    p = c % 3
                    pe.wait_ge(w_lo_ready, n0 + (c + 1))
                    pe.wait_ge(freed[2 * p], MOE_USES[p] + 6 * it + c // 3)
                    f_product(1024 * p, [c % RING], KC, f0_hi, f0_lo).then_inc(filled[2 * p], 1)
                for fo in range(KC):
                    p = fo % 3
                    pe.wait_ge(w_lo_ready, n0 + (QC + 2 * fo + 2))
                    pe.wait_ge(freed[2 * p], MOE_USES[p] + 6 * it + (4 + fo // 3))
                    hidden = (lambda k: pe.wait_ge(g_lo, QC * it + (k + 4))) if fo == 0 else None
                    f_product(1024 * p, [(2 * fo) % RING, (2 * fo + 1) % RING], QC, hid_hi, hid_lo, wait_k=hidden
                              ).then_inc(filled[2 * p], 1)

            with pe.Fori(0, 4) as it:
                quarter(it)
            for i in range(2):
                pe.wait_ge(gl_in, i + 3)
                pe.matmul(ps[:, MISC + i:MISC + i + 1], ones[:, :], gl[:, 2 * i:2 * i + 1], start=True, stop=True
                          ).then_inc(gl_sum, 1)
            pe.wait_ge(fin_ready, KC // 2)
            pe.wait_ge(fin_ready_v, KC // 2)
            for t in range(NT):
                p = t % 3
                pe.wait_ge(freed[2 * p], MOE_USES[p] + 24 + t // 3)
                for c in range(KC):
                    ins = pe.transpose(ps[0:TT, 1024 * p + 128 * c:1024 * p + 128 * c + 128], z_fm[:, c, TT * t:TT * t + TT], ident[:, :])
                ins.then_inc(filled[2 * p], 1)

        @block.scalar
        def _(act):
            chain = Chain(act, act_done)
            act.wait_ge(consts, 1)
            act.activation(gl[:, 9:10], ident[:, 0:1], ACT.Copy)
            full = E // 256
            act.wait_ge(e_pad, 1)
            for i, name in enumerate(("src", "dst")):
                act.dma_start(e_int[0:full, i, :], a[name][0:full * 256].rearrange("(p n) -> p n", n=256)).then_inc(e_loaded, 16)
                act.dma_start(e_int[full:EP, i, 0:E - full * 256],
                               a[name][full * 256:E].rearrange("(a n) -> a n", a=1)).then_inc(e_loaded, 16)
            split = [0]

            def pump(c, end=MOE0):
                while split[0] < min(c + RING, end):
                    n = split[0]
                    act.wait_ge(w_landed[n % RAW], 16 * (n // RAW + 1))
                    slot_free(act, n)
                    act.activation(w_hi[:, n % RING, :], w_raw[:, n % RAW, :], ACT.Copy).then_inc(w_hi_ready, 1)
                    split[0] += 1

            def free(ins, key):
                ins.then_inc(freed[PSUM.at[key][0]], 1)

            entered, finished = [0], [0]

            def softmax_start():
                g = entered[0]
                entered[0] += 1
                j, i = divmod(g, NT)
                if g == 0:
                    act.wait_ge(as_scaled, 2)
                if i == 0:
                    act.wait_ge(rows_loaded[j % 2], 32 * (j // 2 + 1))
                if g >= NT:
                    act.wait_ge(p_used, g - NT + 1)
                act.activation(prob[:, i, :], rows[0:TT, j % 2, 0, :], ACT.Relu, bias=n_as[:, i, j:j + 1]).then_inc(sm_up, 1)

            def softmax_finish():
                g = finished[0]
                finished[0] += 1
                act.wait_ge(sm_min, g + 1)
                act.activation(prob[:, g % NT, :], prob[:, g % NT, :], ACT.Exp, scale=-1.0).then_inc(sm_exp, 1)

            def normalize(n, src, dst):
                t = n % NT
                act.wait_ge(nmr_ready, n + 1)
                act.activation(dst[:, t, :], src[:, t, :], ACT.Identity, bias=neg_mr[0:TT, t:t + 1],
                               scale=rstd[0:TT, t:t + 1]).then_inc(ln_out, 1)

            def chunks_of(b):
                return ps[:, b + 12:b + 12 + TT * KC].rearrange("p (k n) -> p k n", k=KC)

            def relu_parts(hi, src, bias, key):
                n = relus[0]
                relus[0] += 1
                if n >= 2:
                    act.wait_ge(relu_split, n - 1)
                t = relu_t[:, n % 2, 0:src.shape[-1]]
                free(act.activation(t, src, ACT.Relu, bias=bias), key)
                wait_freed(act, key)
                act.activation(hi, t, ACT.Copy).then_inc(hi_first, 1)

            relus = [0]
            hs = 0
            for si, (kind, name, args, n0, job) in enumerate(STEPS):
                for part in SOFT[si]:
                    if part in "as":
                        softmax_start()
                    if part in "fs":
                        softmax_finish()
                if kind in "FTH":
                    pump(n0 - args[0] if kind == "H" and args[1] == 0 else n0)
                b = pb0(job) if job else 0
                if name == "edgesT":
                    normalize(0, x_tm, x_tm)
                elif name == "biasT":
                    normalize(4, x_tm, x_tm)
                    pump(RAW - RING)
                elif name == "count":
                    j, = args
                    wait_filled(act, job)
                    if j:
                        wait_filled(act, ("countT", j - 1))
                        act.wait_ge(mask_ready, j)
                    free(act.activation(count_ds[0:TT, :], ps[0:TT, b:b + N], ACT.Copy), job)
                elif name == "countT":
                    j, = args
                    wait_filled(act, job)
                    free(act.activation(count[:, :, TT * j:TT * j + TT],
                                        tsp(b, TT).rearrange("p (i d) -> p i d", i=NT), ACT.Copy), job)
                elif name in ("xnT", "xT", "mT"):
                    t, = args
                    if name == "xnT" and t + 1 < NT - 1:
                        normalize(t + 1, x_tm, x_tm)
                    dst = f1_hi if name == "mT" else f0_hi
                    wait_filled(act, job)
                    act.activation(dst[:, :, TT * t:TT * t + TT], chunks_of(b), ACT.Copy).then_inc(hi_first, 1)
                elif name == "ah":
                    fo, half = args
                    wait_filled(act, job)
                    wait_freed(act, ("biasT",))
                    relu_parts(f1_hi[:, fo, 313 * half:313 * half + 313], ps[:, b + half:b + half + 313], bias_col[:, fo:fo + 1], job)
                elif name == "h":
                    i = hs
                    hs += 1
                    if i >= 3:
                        act.wait_ge(hs_stored[i % 3], 16 * (i // 3))
                        act.wait_ge(hs_summed, i - 2)
                    wait_filled(act, job)
                    free(act.activation(h_st[:, i % 3, :, 0:GC], ps[0:TT, b:b + 384].rearrange("p (h c) -> p h c", h=2), ACT.Copy), job)
                elif name in ("asT", "mzT"):
                    i = 0 if name == "asT" else args[0] + 1
                    wait_filled(act, job)
                    if i:
                        act.wait_ge(row_stored, 16 * i)
                    r = NHD if name == "asT" else 2 * GH
                    free(act.activation(row_t[0:r, :], tsp(b, r), ACT.Copy), job)
                elif name == "mix":
                    f, part = args
                    if part < 2:
                        dst = (q_fm, k_fm)[part]
                        wait_filled(act, job)
                        if f:
                            act.wait_ge(y_ready, f)
                        elif part == 0:
                            for q in hs_stored:
                                act.wait_ge(q, 16 * (2 * NT * L // 3))
                            act.wait_ge(hs_summed, 2 * NT * L)
                        v = halves(b)
                        chain.link(act.activation(two(dst[:, :]), v, ACT.Identity, accum_out=mix_sum[:, 2 * part:2 * part + 1]))
                        free(act.activation(v, v, ACT.Square, accum_out=mix_sum[:, 2 * part + 1:2 * part + 2]), job)
                elif name == "gT":
                    layer, pr, c = args
                    k = 3 * pr + c
                    wait_filled(act, job)
                    if k == 0 and layer:
                        wait_filled(act, ("wo", layer - 1, 1, NT - 1))
                    k0 = KC * (1 + layer) + k
                    relu_parts(f1_hi[:, k, 0:N], tsp(b), bias_col[:, k0:k0 + 1], job)
                elif name == "agg":
                    j = args[0]
                    act.wait_ge(rden_ready, j + 1)
                    if j % 2 == 0 and j:
                        wait_filled(act, ("gT", (j - 1) // GH, ((j - 1) % GH) // 2, 2))
                    for d in range(NT):
                        ins = act.activation(g_tm[:, d, GC * (j % 2):GC * (j % 2) + GC], ps[0:TT, AGG + 256 * d:AGG + 256 * d + GC],
                                             ACT.Copy, scale=rden[:, d:d + 1])
                    ins.then_inc(agg_freed, 1)
                elif name == "proj" and args[0] == 1:
                    normalize(NT + args[1], x2, xl_tm)
                elif name == "v":
                    fo, = args
                    wait_filled(act, job)
                    free(act.activation(two(v_fm[:, fo, :]), halves(b), ACT.Identity, bias=bias_col[:, 24 + fo:25 + fo]), job)
                elif name == "scores":
                    act.wait_ge(sc_sub, 2)
                    act.wait_ge(xr_ready, NT + 1)
                    for s in range(2):
                        r = slice(64 * s, 64 * s + 64)
                        act.activation(e_blk[r, :, r], w_t[r, :, r], ACT.Exp, scale=1.0 / float(N) ** 0.5).then_inc(sc_exp, 1)
                elif name == "av":
                    hp, = args
                    wait_filled(act, job)
                    if hp >= 2:
                        act.wait_ge(o_stored[hp % 2], 16 * (hp // 2))
                    free(act.activation(two(o_fm[:, hp % 2, :]), halves(b), ACT.Copy), job)
                elif name == "gate":
                    act.wait_ge(gl_ready, 1)
                    for k in range(KC):
                        act.activation(z_fm[:, k, 0:N], z_fm[:, k, 0:N], ACT.Identity, bias=ln_bias[:, k:k + 1],
                                       scale=ln_scale[:, k:k + 1]).then_inc(y_fm_ready, 1)
                        if k == 1:
                            act.wait_ge(gate_e_in, 1)
                            act.activation(gate_row[0:1, NE:2 * NE], gate_row[0:1, 0:NE], ACT.Exp).then_inc(gate_e, 1)
                        if k >= KC // 2:
                            act.wait_ge(y_fm_ready, k + 1)
                            act.activation(f0_hi[:, k, 0:N], z_fm[:, k, 0:N], ACT.Copy).then_inc(y_hi_ready, 1)
                    pump(MOE0, MOE0 + RING)

            act.wait_ge(eb_ready, 1)

            def split_hi(it, k):
                act.wait_ge(w_landed[k % RAW], 16 * (MOE0 // RAW + 1) + 128 * it + 16 * (k // RAW))
                act.wait_ge(*moe_reader(it, k - RING))
                act.activation(w_hi[:, k % RING, :], w_raw[:, k % RAW, :], ACT.Copy).then_inc(w_hi_ready, 1)

            def moe_reader(it, k):
                i = k if k < QC else QC + (k - QC) // 2
                return filled[2 * (i % 3)], MOE_USES[i % 3] + 6 * it + (i // 3 + 1)

            def quarter(it, last):
                for c in range(QC + 2):
                    if c < QC:
                        if c:
                            split_hi(it, c + RING - 1)
                        p = c % 3
                        act.wait_ge(filled[2 * p], MOE_USES[p] + 6 * it + (c // 3 + 1))
                        act.wait_ge(g_lo, QC * it + (c + 1))
                        b = fcb[:, bass.ds(QC * it + c, 1)]
                        v = halves(1024 * p)
                        act.activation(two(gel_x[:, c % 3, :]), v, ACT.Identity, bias=b)
                        act.activation(two(gel_u[:, c % 3, :]), v, ACT.Square, bias=b).then_inc(freed[2 * p], 1)
                    if 1 <= c <= QC:
                        act.wait_ge(g_w, QC * it + c)
                        act.activation(gel_u[:, (c - 1) % 3, :], gel_u[:, (c - 1) % 3, :], ACT.Tanh, scale=GELU_C).then_inc(g_th, 1)
                    if c >= 2:
                        act.wait_ge(g_q, QC * it + (c - 1))
                        act.activation(hid_hi[:, c - 2, :], gel_u[:, (c - 2) % 3, :], ACT.Copy, scale=0.5).then_inc(g_hi, 1)
                split_hi(it, QC + RING - 1)
                for fo in range(KC):
                    ks = [QC + 2 * fo + RING, QC + 2 * fo + RING + 1]
                    for k in ks:
                        if k < 24 or not last:
                            if k < 24 + RING:
                                split_hi(it, k)

            with act.Fori(0, 3) as it:
                quarter(it, False)
            quarter(3, True)
            act.wait_ge(gl_ready, 2)
            for k in range(KC // 2):
                act.activation(z_fm[:, k, 0:N], z_fm[:, k, 0:N], ACT.Identity, bias=ln_bias[:, k:k + 1],
                               scale=ln_scale[:, k:k + 1]).then_inc(fin_ready, 1)

        @block.vector
        def _(dve):
            chain = Chain(dve, dve_done)
            split = [0]

            def split_lo(n_slot, n_raw):
                return dve.tensor_tensor(w_lo[:, n_slot, :], w_raw[:, n_raw, :], w_hi[:, n_slot, :].bitcast(F32), ALU.subtract)

            def pump(c, end=MOE0):
                while split[0] < min(c + RING, end):
                    n = split[0]
                    split[0] += 1
                    if GAT0 <= n < GAT1:
                        continue
                    if n == GAT1:
                        dve.wait_ge(w_lo_ready, GAT1)
                    dve.wait_ge(w_hi_ready, n + 1)
                    split_lo(n % RING, n % RAW).then_inc(w_lo_ready, 1)

            def free(ins, key):
                ins.then_inc(freed[PSUM.at[key][0]], 1)

            def ln_mr(n):
                t = n % NT
                dve.wait_ge(rstd_ready, n + 1)
                dve.scalar_tensor_tensor(out=neg_mr[0:TT, t:t + 1], in0=mv[0:TT, t, 0:1], scalar=-1.0, in1=rstd[0:TT, t:t + 1],
                                         op0=ALU.mult, op1=ALU.mult).then_inc(nmr_ready, 1)

            def ln_tile(n, src):
                t = n % NT
                for g in range(2):
                    ins = dve.bn_stats(stats[0:TT, 2 * t + g, :], src[:, t, 384 * g:384 * g + 384])
                ins.then_inc(ln_stats, 1)
                dve.wait_ge(ln_stats, n + 1)
                dve.bn_aggr(mv[0:TT, t, :], stats[0:TT, 2 * t:2 * t + 2, :]).then_inc(ln_mv, 1)
                dve.wait_ge(ln_mv, n + 1)
                dve.tensor_scalar(var_eps[0:TT, t:t + 1], mv[0:TT, t, 1:2], LN_EPS, None, ALU.add).then_inc(var_ready, 1)

            def chunk_stats(k):
                for g, (c0, c1) in enumerate(((0, 313), (313, N))):
                    ins = dve.bn_stats(stats[:, 2 * k + g, :], z_fm[:, k, c0:c1])
                return ins

            def global_stats(i):
                dve.bn_aggr(gl[:, 0:2], stats[:, :, :]).then_inc(gl_in, 1)
                dve.wait_ge(gl_sum, 2 * i + 1)
                chain.link(dve.tensor_scalar(gl[:, 3:4], ps[:, MISC:MISC + 1], -1.0 / 128, None, ALU.mult))
                chain.link(dve.tensor_tensor(gl[:, 6:7], gl[:, 0:1], gl[:, 3:4], ALU.add))
                dve.scalar_tensor_tensor(out=gl[:, 2:3], in0=gl[:, 6:7], scalar=gl[:, 6:7], in1=gl[:, 1:2],
                                         op0=ALU.mult, op1=ALU.add).then_inc(gl_in, 1)
                dve.wait_ge(gl_sum, 2 * i + 2)
                dve.tensor_scalar(gl[:, 4:5], ps[:, MISC + 1:MISC + 2], float(KC * N) / (N * D - 1), GLN_EPS, ALU.mult,
                                  ALU.add).then_inc(gl_var, 1)
                dve.wait_ge(gl_rstd, i + 1)
                w0 = 36 + 12 * i
                chain.link(dve.tensor_scalar(ln_scale[:, :], bias_col[:, w0:w0 + KC], gl[:, 5:6], None, ALU.mult))
                dve.scalar_tensor_tensor(out=ln_bias[:, :], in0=ln_scale[:, :], scalar=gl[:, 3:4],
                                         in1=bias_col[:, w0 + KC:w0 + 2 * KC], op0=ALU.mult, op1=ALU.add).then_inc(gl_ready, 1)

            entered, finished = [0], [0]

            def softmax_start():
                g = entered[0]
                entered[0] += 1
                j, i = divmod(g, NT)
                dve.wait_ge(sm_up, g + 1)
                dve.scalar_tensor_tensor(out=prob[:, i, :], in0=rows[0:TT, j % 2, 1, :], scalar=n_as02[:, i, j:j + 1],
                                         in1=prob[:, i, :], op0=ALU.add, op1=ALU.min).then_inc(sm_min, 1)

            def softmax_finish():
                g = finished[0]
                finished[0] += 1
                dve.wait_ge(sm_exp, g + 1)
                dve.scalar_tensor_tensor(out=prob[:, g % NT, :], in0=prob[:, g % NT, :], scalar=1.0, in1=count[:, g % NT, :],
                                         op0=ALU.min, op1=ALU.mult).then_inc(p_ready, 1)

            def head_max(j):
                layer, h = divmod(j, GH)
                dve.wait_ge(asrow_loaded[j % 2], 16 * (j // 2 + 1))
                for d in range(NT):
                    if NT * j + d >= 2:
                        dve.wait_ge(head_maxed, NT * j + d - 1)
                    dve.tensor_tensor_reduce(out=junk[:, (NT * j + d) % 2, :], in0=mask[:, d, :], in1=as_row[0:TT, j % 2, :], scale=1.0,
                                             scalar=NEG, op0=ALU.add, op1=ALU.max, accum_out=mx[:, d, h:h + 1]
                                             ).then_inc(head_maxed, 1)
                if h == GH - 1:
                    dve.wait_ge(head_maxed, NT * (j + 1))
                    ad = asd[:, :, NHD + GH * layer:NHD + GH * layer + GH]
                    chain.link(dve.tensor_tensor(z_tmp[:, :, :], mx[:, :, :], ad, ALU.add))
                    chain.link(dve.scalar_tensor_tensor(out=m_tmp[:, :, :], in0=z_tmp[:, :, :], scalar=0.2,
                                                        in1=z_tmp[:, :, :], op0=ALU.mult, op1=ALU.max))
                    dve.tensor_tensor(mz[:, layer, :, 0:GH], m_tmp[:, :, :], ad, ALU.subtract)
                    dve.scalar_tensor_tensor(out=mz[:, layer, :, GH:2 * GH], in0=ad, scalar=-0.2, in1=m_tmp[:, :, :],
                                             op0=ALU.mult, op1=ALU.add).then_inc(mz_ready, 1)

            def lo_part(dst, hi, src, key):
                dve.wait_ge(hi_first, hf[0] + 1)
                hf[0] += 1
                free(dve.tensor_tensor(dst, src, hi.bitcast(F32), ALU.subtract), key)

            relus = [0]

            def relu_lo_part(lo, hi):
                dve.wait_ge(hi_first, hf[0] + 1)
                hf[0] += 1
                dve.tensor_tensor(lo, relu_t[:, relus[0] % 2, 0:lo.shape[-1]], hi.bitcast(F32), ALU.subtract).then_inc(relu_split, 1)
                relus[0] += 1

            def make_chunk(n):
                j, c = divmod(n, CHUNKS)
                if c == 0:
                    first.append(dve.value_load(bounds[j:j + 1, 0:1], min_val=0, max_val=EP - 1))
                if n >= 2:
                    dve.wait_ge(chunk_used, n - 1)
                for i in range(2 * PAIRS):
                    o = 2 * PAIRS * (n % 2) + i
                    e = bass.ds(first[j] + (PAIRS * c + i // 2), 1)
                    dve.tensor_scalar(oh_s[:, o, :], iota[:, :], e_col[:, 0, i % 2, e], None, ALU.is_equal)
                    dve.tensor_scalar(oh_d[:, o, 0:TT], iota[:, TT * j:TT * j + TT], e_col[:, 1, i % 2, e], None,
                                      ALU.is_equal).then_inc(chunk_tile, 1)

            def mask_of(j):
                wait_freed(dve, ("count", j))
                dve.tensor_scalar(mask[:, j, :], count_ds[0:TT, :], 0.0, NEG, ALU.is_equal, ALU.mult).then_inc(mask_ready, 1)

            def chunks_of(b):
                return ps[:, b + 12:b + 12 + TT * KC].rearrange("p (k n) -> p k n", k=KC)

            hf, hs, first = [0], 0, []
            def x_tile(t):
                dve.wait_ge(x_loaded[t], 32)
                ln_tile(t, x_tm)
                if t:
                    ln_mr(t - 1)

            x_tile(0)
            dve.wait_ge(e_loaded, 64)
            for w in range(2):
                dve.tensor_copy(e_f[:, w, :], e_int[:, w, :]).then_inc(edges_f, 1)
            x_tile(1)
            dve.wait_ge(edges_f, 2)
            for i, op in enumerate((ALU.min, ALU.max)):
                dve.tensor_reduce(e_ends[0:EP, i:i + 1], e_f[:, 1, :], AX_X, op).then_inc(edges_f, 1)
            dve.wait_ge(consts, 3)
            dve.tensor_copy(iota[:, :], iota_f[:, :])
            for si, (kind, name, args, n0, job) in enumerate(STEPS):
                for part in SOFT[si]:
                    if part in "as":
                        softmax_start()
                    if part in "fs":
                        softmax_finish()
                if kind in "FTH":
                    pump(n0 - args[0] if kind == "H" and args[1] == 0 else n0)
                b = pb0(job) if job else 0
                if name == "edgesT":
                    wait_filled(dve, job)
                    dve.wait_ge(e_col_set, 1)
                    v = ps[:, b:b + 4 * 96].rearrange("p (w s q) -> p (w s) q", w=2, s=2)[:, :, 0:EP]
                    free(dve.tensor_copy(e_col[:, :, :, 0:EP].rearrange("p w s q -> p (w s) q"), v), job)
                    x_tile(2)
                elif name == "bounds":
                    wait_filled(dve, job)
                    lo, hi = ps[0:5, b:b + EP], ps[0:5, b + 96:b + 96 + EP]
                    meets = e_lo5[:, 1, 0:EP]
                    dve.wait_ge(consts, 2)
                    chain.link(dve.tensor_scalar(bsm[:, 1:2], bsm[:, 0:1], float(TT), None, ALU.add))
                    chain.link(dve.tensor_scalar(e_lo5[:, 0, 0:EP], lo, bsm[:, 1:2], None, ALU.is_lt))
                    free(dve.scalar_tensor_tensor(out=meets, in0=hi, scalar=bsm[:, 0:1], in1=e_lo5[:, 0, 0:EP],
                                                  op0=ALU.is_ge, op1=ALU.mult), job)
                    wait_freed(dve, job)
                    for i, (shift, op) in enumerate(((-128.0, ALU.min), (1.0, ALU.max))):
                        chain.link(dve.scalar_tensor_tensor(out=e_lo5[:, 2 + i, 0:EP], in0=iota_f[0:5, 0:EP], scalar=shift,
                                                            in1=meets, op0=ALU.add, op1=ALU.mult))
                        chain.link(dve.tensor_reduce(bsm[:, 2 + i:3 + i], e_lo5[:, 2 + i, 0:EP], AX_X, op))
                    chain.link(dve.tensor_scalar(bsm[:, 4:5], bsm[:, 2:3], 128.0, float(EP - 1), ALU.add, ALU.min))
                    chain.link(dve.tensor_tensor(bsm[:, 5:6], bsm[:, 3:4], bsm[:, 4:5], ALU.subtract))
                    chain.link(dve.tensor_scalar(bsm[:, 5:6], bsm[:, 5:6], float(-SPAN), 1.0, ALU.add, ALU.max))
                    dve.tensor_copy(bounds[:, :], bsm[:, 4:6]).then_inc(bounds_ready, 1)
                    x_tile(3)
                elif name == "biasT":
                    wait_filled(dve, job)
                    free(dve.tensor_copy(bias_col[:, :], ps[:, b:b + 60]), job)
                    pump(RAW - RING)
                    dve.wait_ge(bounds_ready, 1)
                    make_chunk(0)
                elif name == "chunk":
                    j, c = args
                    if c == CHUNKS - 1:
                        trips = dve.value_load(bounds[j:j + 1, 1:2], min_val=1, max_val=EP)
                        with dve.Fori(0, trips) as q:
                            for s in range(2):
                                dve.wait_ge(oh_used[j], 2 * q + (s + 1))
                                e = bass.ds(first[j] + q + SPAN, 1)
                                dve.tensor_scalar(oh2_s[:, s, :], iota[:, :], e_col[:, 0, s, e], None, ALU.is_equal)
                                dve.tensor_scalar(oh2_d[:, s, 0:TT], iota[:, TT * j:TT * j + TT], e_col[:, 1, s, e], None,
                                                  ALU.is_equal).then_inc(oh_ready[j], 1)
                    n = CHUNKS * j + c + 1
                    if n < CHUNKS * NT:
                        make_chunk(n)
                elif name == "countT":
                    mask_of(args[0])
                elif name in ("xnT", "xT", "mT"):
                    t, = args
                    if name == "xT" and t + 2 < NT:
                        ln_mr(NT + t + 2)
                    hi, lo = (f1_hi, f1_lo) if name == "mT" else (f0_hi, f0_lo)
                    c = slice(TT * t, TT * t + TT)
                    lo_part(lo[:, :, c], hi[:, :, c], chunks_of(b), job)
                    if name == "xnT" and t == 0:
                        x_tile(4)
                        ln_mr(NT - 1)
                elif name == "ah":
                    fo, half = args
                    c = slice(313 * half, 313 * half + 313)
                    relu_lo_part(f1_lo[:, fo, c], f1_hi[:, fo, c])
                elif name == "gT":
                    layer, pr, c = args
                    k = 3 * pr + c
                    relu_lo_part(f1_lo[:, k, 0:N], f1_hi[:, k, 0:N])
                elif name == "h":
                    layer, g, t = args
                    i = hs
                    hs += 1
                    if g == 0 and t == 0:
                        dve.wait_ge(a_loaded[layer % 2], 32 * (layer // 2 + 1))
                    wait_freed(dve, job)
                    if i:
                        dve.wait_ge(hs_summed, i)
                    for w in range(2):
                        for h in range(2):
                            hd = 2 * g + h
                            ins = dve.tensor_tensor_reduce(out=junk1[:, 2 * w + h, :], in0=h_st[:, i % 3, h, 0:GC],
                                                           in1=a_bc[:, layer % 2, w, GC * hd:GC * hd + GC], scale=1.0, scalar=0.0,
                                                           op0=ALU.mult, op1=ALU.add,
                                                           accum_out=asd[:, t, NHD * w + GH * layer + hd:NHD * w + GH * layer + hd + 1])
                    ins.then_inc(hs_summed, 1)
                elif name == "asT":
                    dve.wait_ge(hs_summed, 2 * NT * L)
                    dve.tensor_scalar(n_as[:, :, :], asd[:, :, 0:NHD], -1.0, None, ALU.mult).then_inc(as_scaled, 1)
                    dve.tensor_scalar(n_as02[:, :, :], asd[:, :, 0:NHD], -0.2, None, ALU.mult).then_inc(as_scaled, 1)
                elif name == "mix":
                    f, part = args
                    if part == 2:
                        dve.wait_ge(mix_rr, f + 1)
                        wait_filled(dve, job)
                        free(dve.scalar_tensor_tensor(out=two(t_fm[:, :]), in0=two(k_fm[:, :]), scalar=mix_r[:, 1:2],
                                                      in1=halves(b), op0=ALU.mult, op1=ALU.mult), job)
                        chain.link(dve.scalar_tensor_tensor(out=k_fm[:, :], in0=q_fm[:, :], scalar=mix_c[:, :], in1=k_fm[:, :],
                                                            op0=ALU.mult, op1=ALU.mult))
                        wait_freed(dve, job)
                        chain.link(dve.tensor_tensor(t_fm[:, :], t_fm[:, :], k_fm[:, :], ALU.mult))
                        if f:
                            dve.wait_ge(y_stored, 32 * f)
                        chain.link(dve.tensor_copy(y_hi[:, :], t_fm[:, :]))
                        dve.tensor_tensor(y_lo[:, :], t_fm[:, :], y_hi[:, :].bitcast(F32), ALU.subtract).then_inc(y_ready, 1)
                elif name == "agg":
                    j = args[0]
                    dve.wait_ge(p_used, NT * (j + 1))
                    chain.link(dve.tensor_scalar(den[:, :], ps[0:TT, AGG:AGG + 256 * NT].rearrange("p (d c) -> p d c", d=NT)[:, :, GC],
                                                 1e-16, None, ALU.add))
                    dve.reciprocal(rden[:, :], den[:, :]).then_inc(rden_ready, 1)
                elif name == "wo":
                    layer, g, t = args
                    c = slice(384 * g, 384 * g + 384)
                    wait_filled(dve, job)
                    if layer == 0:
                        dve.wait_ge(gacc_set, 16 * NT)
                    free(dve.tensor_tensor(gacc[:, t, c], gacc[:, t, c], ps[0:TT, b:b + 384], ALU.add), job)
                elif name == "proj":
                    g, t = args
                    c = slice(384 * g, 384 * g + 384)
                    dve.wait_ge(xr_ready, t + 1)
                    wait_freed(dve, ("wo", L - 1, g, t))
                    chain.link(dve.scalar_tensor_tensor(out=x2[:, t, c], in0=gacc[:, t, c], scalar=0.0, in1=xr[:, t, c],
                                                        op0=ALU.max, op1=ALU.add))
                    wait_filled(dve, job)
                    free(dve.tensor_tensor(x2[:, t, c], x2[:, t, c], ps[0:TT, b:b + 384], ALU.add), job)
                    if g == 1:
                        if t in (1, 2):
                            ln_mr(NT + t - 1)
                        wait_freed(dve, ("proj", 0, t))
                        wait_freed(dve, job)
                        ln_tile(NT + t, x2)
                elif name == "qk":
                    u, g, t = args
                    wait_filled(dve, job)
                    if args == (0, 0, 0):
                        dve.wait_ge(late_loaded, 16)
                        dve.memset(z_fm[:, :, N:TP], 0.0)
                    free(dve.tensor_tensor((q_tm, k_tm)[u][:, t, 384 * g:384 * g + 384], ps[0:TT, b:b + 384],
                                           qk_b[:, D * u + 384 * g:D * u + 384 * g + 384], ALU.add), job)
                elif name == "scores":
                    wait_filled(dve, job)
                    for s in range(2):
                        r = slice(64 * s, 64 * s + 64)
                        v = ps[r, b:b + 128 * KC].rearrange("p (k c) -> p k c", k=KC)[:, :, 64 * s:64 * s + 64]
                        chain.link(dve.tensor_reduce(sm[r, 0:KC], v, AX_X, ALU.max))
                        ins = dve.tensor_tensor(w_t[r, :, r], v, sm[r, 0:KC].to_broadcast([64, KC, 64]), ALU.subtract)
                        ins.then_inc(sc_sub, 1)
                    dve.wait_ge(sc_exp, 2)
                    chain.link(dve.tensor_reduce(sm[:, KC:2 * KC], e_blk[:, :, :], AX_X, ALU.add))
                    chain.link(dve.reciprocal(sm[:, 2 * KC:3 * KC], sm[:, KC:2 * KC]))
                    dve.tensor_tensor(e_blk[:, :, :], e_blk[:, :, :], sm[:, 2 * KC:3 * KC].to_broadcast([128, KC, 128]),
                                      ALU.mult).then_inc(eblk_ready, 1)
                    free(dve.memset(sm[:, 3 * KC:3 * KC + 1], 0.0), job)
                elif name == "wT":
                    wait_filled(dve, job)
                    free(dve.tensor_copy(w_t[:, :, :].rearrange("p k c -> p (k c)"), ps[:, b:b + 128 * KC]), job)
                elif name == "w2":
                    fo, half = args
                    wait_filled(dve, job)
                    if half == 0:
                        dve.wait_ge(z_set, fo + 1)
                    v = z_fm[:, fo, 313 * half:313 * half + 313]
                    free(dve.scalar_tensor_tensor(out=v, in0=ps[:, b + half:b + half + 313], scalar=bias_col[:, 30 + fo:31 + fo],
                                                  in1=v, op0=ALU.add, op1=ALU.add), job)
                    if half:
                        wait_freed(dve, ("w2", fo, 0))
                        wait_freed(dve, job)
                        chain.link(chunk_stats(fo))
                        ins = dve.bn_aggr(z_mv[:, fo, :], stats[:, 2 * fo:2 * fo + 2, :])
                        if fo == KC - 1:
                            chain.link(ins)
                            global_stats(0)
                elif name == "expert_biasT":
                    wait_filled(dve, job)
                    dve.tensor_copy(fcb_all[:, :], ps[:, b:b + 2 * QC * NE])
                    free(dve.tensor_copy(pb_all[:, :], ps[:, b + 2 * QC * NE:b + 2 * QC * NE + KC * NE]), job)
                elif name == "gate":
                    gr = lambda i, n=NE: gate_row[0:1, i:i + n]

                    def split_y(k):
                        if k < KC // 2:
                            dve.wait_ge(y_fm_ready, k + 1)
                            chain.link(dve.tensor_copy(f0_hi[:, k, 0:N], z_fm[:, k, 0:N]))
                        else:
                            dve.wait_ge(y_hi_ready, k - KC // 2 + 1)
                        dve.tensor_tensor(f0_lo[:, k, 0:N], z_fm[:, k, 0:N], f0_hi[:, k, 0:N].bitcast(F32), ALU.subtract
                                          ).then_inc(y_split, 1)

                    dve.wait_ge(gl_ready, 1)
                    chain.link(dve.tensor_tensor(y_mean[:, :], z_mv[:, :, 0], ln_scale[:, :], ALU.mult))
                    dve.tensor_tensor(y_mean[:, :], y_mean[:, :], ln_bias[:, :], ALU.add).then_inc(gate_in, 1)
                    split_y(0)
                    dve.wait_ge(gate_mm, 1)
                    chain.link(dve.tensor_tensor(gr(40), ps[0:1, MISC + 8:MISC + 16], r_b[:, :], ALU.add))
                    chain.link(dve.tensor_reduce(gr(32, 1), gr(40), AX_X, ALU.max))
                    dve.tensor_scalar(gr(0), gr(40), gr(32, 1), None, ALU.subtract).then_inc(gate_e_in, 1)
                    split_y(1)
                    dve.wait_ge(gate_e, 1)
                    chain.link(dve.tensor_reduce(gr(33, 1), gr(8), AX_X, ALU.add))
                    chain.link(dve.reciprocal(gr(34, 1), gr(33, 1)))
                    chain.link(dve.tensor_scalar(gr(16), gr(8), gr(34, 1), None, ALU.mult))
                    chain.link(dve.max(gr(24), gr(16)))
                    dve.max_index(gate_idx[:, :], gr(24), gr(16)).then_inc(gate_ready, 1)
                    for k in range(2, KC):
                        split_y(k)
                    pump(MOE0, MOE0 + RING)
                    dve.wait_ge(gate_bc, 1)
                    for i in range(2):
                        chain.link(dve.tensor_copy(gate_col[:, i:4:2], ps[:, MISC + 16:MISC + 18]))
                    wait_freed(dve, ("expert_biasT",))
                    for i in range(2):
                        e = dve.value_load(gate_idx[0:1, i:i + 1], min_val=0, max_val=NE - 1)
                        dve.tensor_copy(fcb[:, 2 * QC * i:2 * QC * i + 2 * QC], fcb_all[:, bass.ds(e * (2 * QC), 2 * QC)])
                        ins = dve.tensor_copy(pb[:, KC * i:KC * i + KC], pb_all[:, bass.ds(e * KC, KC)])
                    ins.then_inc(eb_ready, 1)
                    dve.wait_ge(eb_ready, 1)
                    chain.link(dve.tensor_scalar(ln_scale[:, :], pb[:, 0:KC], gate_col[:, 0:1], None, ALU.mult))
                    chain.link(dve.scalar_tensor_tensor(out=ln_bias[:, :], in0=pb[:, KC:2 * KC], scalar=gate_col[:, 2:3],
                                                        in1=ln_scale[:, :], op0=ALU.mult, op1=ALU.add))
                    for k in range(KC):
                        ins = dve.tensor_scalar(z_fm[:, k, :], z_fm[:, k, :], ln_bias[:, k:k + 1], None, ALU.add)
                    chain.link(ins)
                    dve.memset(gl[:, 8:9], 0.0).then_inc(g_lo, 3)
                if (name, *args) in MAX_AFTER:
                    for j in MAX_AFTER[(name, *args)]:
                        if j == 0:
                            dve.wait_ge(mask_ready, NT)
                            wait_filled(dve, ("countT", NT - 1))
                        head_max(j)

            def lo_piece(it, k):
                dve.wait_ge(w_hi_ready, MOE0 + 24 * it + (k + 1))
                split_lo(k % RING, k % RAW).then_inc(w_lo_ready, 1)

            def quarter(it, last):
                ins = None
                for c in range(QC + 2):
                    if c < QC:
                        if c:
                            lo_piece(it, c + RING - 1)
                        x, u = gel_x[:, c % 3, :], gel_u[:, c % 3, :]
                        dve.wait_ge(freed[2 * (c % 3)], MOE_USES[c % 3] + 6 * it + (c // 3 + 1))
                        dve.tensor_scalar(u, u, GELU_A, 1.0, ALU.mult, ALU.add).then_inc(g_v, 1)
                        dve.wait_ge(g_v, QC * it + (c + 1))
                        dve.tensor_tensor(u, u, x, ALU.mult).then_inc(g_w, 1)
                    if 1 <= c <= QC:
                        x, u = gel_x[:, (c - 1) % 3, :], gel_u[:, (c - 1) % 3, :]
                        dve.wait_ge(g_th, QC * it + c)
                        dve.scalar_tensor_tensor(out=u, in0=u, scalar=1.0, in1=x, op0=ALU.add, op1=ALU.mult).then_inc(g_q, 1)
                    if c >= 2:
                        u = gel_u[:, (c - 2) % 3, :]
                        dve.wait_ge(g_hi, QC * it + (c - 1))
                        dve.scalar_tensor_tensor(out=hid_lo[:, c - 2, :], in0=u, scalar=0.5, in1=hid_hi[:, c - 2, :].bitcast(F32),
                                                 op0=ALU.mult, op1=ALU.subtract).then_inc(g_lo, 1)
                lo_piece(it, QC + RING - 1)
                for fo in range(KC):
                    p = fo % 3
                    dve.wait_ge(filled[2 * p], MOE_USES[p] + 6 * it + (4 + fo // 3 + 1))
                    v = two(z_fm[:, fo, :])
                    dve.scalar_tensor_tensor(out=v, in0=halves(1024 * p), scalar=gate_col[:, bass.ds(it, 1)], in1=v,
                                             op0=ALU.mult, op1=ALU.add).then_inc(freed[2 * p], 1)
                    if last:
                        dve.wait_ge(freed[2 * p], MOE_USES[p] + 6 * it + (4 + fo // 3 + 1))
                        ins = chunk_stats(fo)
                    for k in (QC + 2 * fo + RING, QC + 2 * fo + RING + 1):
                        if k < (24 if last else 24 + RING):
                            lo_piece(it, k)
                return ins

            with dve.Fori(0, 3) as it:
                quarter(it, False)
            chain.link(quarter(3, True))
            global_stats(1)
            dve.wait_ge(gl_ready, 2)
            for k in range(KC // 2, KC):
                dve.tensor_scalar(z_fm[:, k, 0:N], z_fm[:, k, 0:N], ln_scale[:, k:k + 1], ln_bias[:, k:k + 1], ALU.mult, ALU.add
                                  ).then_inc(fin_ready_v, 1)
            for t in range(NT):
                p = t % 3
                dve.wait_ge(filled[2 * p], MOE_USES[p] + 24 + t // 3 + 1)
                if t >= 2:
                    dve.wait_ge(o_left[t % 2], 32 * (t // 2))
                dve.tensor_tensor(o_tm[:, t % 2, :], ps[0:TT, 1024 * p:1024 * p + D], x2[:, t, :], ALU.add).then_inc(freed[2 * p], 1)


def kernel(**inputs):
    import numpy as _np
    import concourse.bacc as _bacc
    from concourse import mybir as _mybir
    from concourse.bass_utils import run_bass_kernel_spmd as _run

    nc = _bacc.Bacc("TRN2", target_bir_lowering=False, num_devices=1)
    arrays, aps = {}, {}
    for name, value in inputs.items():
        if name == "edge_weight1":
            continue
        v = _np.ascontiguousarray(value)
        arrays[f"in_{name}_dram"] = v
        aps[name] = nc.dram_tensor(f"in_{name}_dram", v.shape, _mybir.dt.from_np(v.dtype), kind="ExternalInput").ap()
    out = nc.dram_tensor("out_0_dram", (N, D), _mybir.dt.float32, kind="ExternalOutput").ap()
    gnn_block(nc, aps, out)
    r = _run(nc, [arrays], core_ids=[0])
    return r.results[0]["out_0_dram"]
```
